# Optimizing a Trainium2 kernel written in Bass

```python
import numpy as np
import jax
import jax.numpy as jnp

def _softmax(x, axis=-1):
    return jax.nn.softmax(x, axis=axis)

def _gelu(x):
    return jax.nn.gelu(x, approximate=True)

def _silu(x):
    return jax.nn.silu(x)

def _sigmoid(x):
    return jax.nn.sigmoid(x)

def _layernorm(x, axis=-1, eps=1e-05):
    m = jnp.mean(x, axis=axis, keepdims=True)
    v = jnp.var(x, axis=axis, keepdims=True)
    return (x - m) / jnp.sqrt(v + eps)

def _scatter_add(tgt, idx, src, axis=0):
    return tgt.at[idx].add(src)

def _segment_sum(src, seg, n):
    return jax.ops.segment_sum(src, seg, n)
kernel_name = 'mk_seq_preln_d2_jaxref_r8_5d5bbf'

def setup_inputs(seed: int=0):
    np.random.seed(seed)
    _w = jnp.asarray

    def _L0_attn_setup():
        import jax, jax.numpy as jnp
        import numpy as np
        NUM_HEADS = 8
        SCALE_BASE = 512.0
        GN_EPS = 1e-05

        def rotate_every_two(x):
            x1 = x[..., ::2]
            x2 = x[..., 1::2]
            return jnp.stack([-x2, x1], axis=-1).reshape(x.shape)

        def xpos_apply(x, downscale):
            L, D = (x.shape[1], x.shape[2])
            half = D // 2
            scale_vec = (jnp.arange(0, D, 2, dtype=jnp.float32) + 0.4 * D) / (1.4 * D)
            pos = jnp.arange(L, dtype=jnp.float32)
            scale = scale_vec[None, :] ** (pos[:, None] / SCALE_BASE)
            inv_freq = 1.0 / 10000.0 ** (jnp.arange(half, dtype=jnp.float32) / half)
            sinusoid = pos[:, None] * inv_freq[None, :]
            sin, cos = (jnp.sin(sinusoid), jnp.cos(sinusoid))
            if downscale:
                scale = 1.0 / scale
            sin_s = jnp.repeat(sin * scale, 2, axis=-1)
            cos_s = jnp.repeat(cos * scale, 2, axis=-1)
            return x * cos_s + rotate_every_two(x) * sin_s

        def decay_mask_fn(T, num_heads):
            s, e = (np.log(1.0 / 32.0), np.log(1.0 / 512.0))
            gamma = 1.0 - jnp.exp(jnp.linspace(s, e, num_heads).astype(jnp.float32))
            log_decay = jnp.log(gamma)
            idx = jnp.arange(T)
            expo = (idx[:, None] - idx[None, :]).astype(jnp.float32)
            tri = idx[:, None] >= idx[None, :]
            expo_safe = jnp.where(tri, expo, 0.0)
            mask = jnp.exp(log_decay[:, None, None] * expo_safe) * tri
            scale = jnp.sqrt(mask.sum(axis=-1, keepdims=True))
            return mask / scale

        def _reference_tuple_inner(hidden_states, w_qkv, b_qkv, w_g, b_g, w_p, b_p):
            B, T, E = hidden_states.shape
            H = NUM_HEADS
            V = 2 * E
            dk, dv = (E // H, V // H)
            qkv = hidden_states @ w_qkv + b_qkv
            q, k, v = (qkv[..., :E], qkv[..., E:2 * E], qkv[..., 2 * E:])
            q = xpos_apply(q, downscale=False)
            k = xpos_apply(k, downscale=True)
            q = q.reshape(B, T, H, dk).transpose(0, 2, 1, 3)
            k = k.reshape(B, T, H, dk).transpose(0, 2, 1, 3)
            v = v.reshape(B, T, H, dv).transpose(0, 2, 1, 3)
            mask = decay_mask_fn(T, H)
            retention = jnp.einsum('bhid,bhjd->bhij', q, k) * dk ** (-0.5)
            retention = retention * mask[None]
            out = jnp.einsum('bhij,bhjv->bhiv', retention, v)
            curr_kv = jnp.einsum('hj,bhjk,bhjv->bhkv', mask[:, -1, :], k, v)
            retention_out = out.transpose(0, 2, 1, 3).reshape(B, T, V)
            g = retention_out.reshape(B * T, H, dv)
            mu = g.mean(axis=-1, keepdims=True)
            var = ((g - mu) ** 2).mean(axis=-1, keepdims=True)
            normed = ((g - mu) / jnp.sqrt(var + GN_EPS)).reshape(B, T, V)
            gated = jax.nn.silu(hidden_states @ w_g + b_g) * normed
            proj = gated @ w_p + b_p
            return (proj, curr_kv)
        key = jax.random.key(seed)
        ks = jax.random.split(key, 4)
        B, T, E = (2, 256, 128)
        V = 2 * E
        return {'hidden_states': jax.random.normal(ks[0], (B, T, E), dtype=jnp.float32), 'w_qkv': jax.random.normal(ks[1], (E, 2 * E + V), dtype=jnp.float32) * 0.02, 'b_qkv': jnp.zeros((2 * E + V,), dtype=jnp.float32), 'w_g': jax.random.normal(ks[2], (E, V), dtype=jnp.float32) * 0.02, 'b_g': jnp.zeros((V,), dtype=jnp.float32), 'w_p': jax.random.normal(ks[3], (V, E), dtype=jnp.float32) * 0.02, 'b_p': jnp.zeros((E,), dtype=jnp.float32)}
    _L0_attn_in = _L0_attn_setup()

    def _L0_ffn_setup():
        import jax, jax.numpy as jnp
        import numpy as np
        D_MODEL, D_FF, N_EXPERTS, TOP_K = (128, 512, 8, 2)
        key = jax.random.key(seed)
        ks = jax.random.split(key, 7)
        B, L = (4, 256)
        s = lambda fan_in: 1.0 / np.sqrt(fan_in)
        x = jax.random.normal(ks[0], (B, L, D_MODEL), dtype=jnp.float32)
        Wr = jax.random.uniform(ks[1], (D_MODEL, N_EXPERTS), minval=-s(D_MODEL), maxval=s(D_MODEL), dtype=jnp.float32)
        br = jnp.zeros((N_EXPERTS,), dtype=jnp.float32)
        W1 = jax.random.uniform(ks[2], (N_EXPERTS, D_MODEL, D_FF), minval=-s(D_MODEL), maxval=s(D_MODEL), dtype=jnp.float32)
        b1 = jax.random.uniform(ks[3], (N_EXPERTS, D_FF), minval=-s(D_MODEL), maxval=s(D_MODEL), dtype=jnp.float32)
        W2 = jax.random.uniform(ks[4], (N_EXPERTS, D_FF, D_MODEL), minval=-s(D_FF), maxval=s(D_FF), dtype=jnp.float32)
        b2 = jax.random.uniform(ks[5], (N_EXPERTS, D_MODEL), minval=-s(D_FF), maxval=s(D_FF), dtype=jnp.float32)
        return {'x': x, 'Wr': Wr, 'br': br, 'W1': W1, 'b1': b1, 'W2': W2, 'b2': b2}
    _L0_ffn_in = _L0_ffn_setup()

    def _L1_attn_setup():
        import jax, jax.numpy as jnp
        import numpy as np
        B, N, D = (4, 512, 128)
        H, F = (16, 32)
        HD = D // H
        EPS_ATTN = 1e-08
        EPS_LN = 1e-05

        def _layernorm(x, gamma, beta):
            mu = jnp.mean(x, axis=-1, keepdims=True)
            var = jnp.var(x, axis=-1, keepdims=True)
            return (x - mu) * jax.lax.rsqrt(var + EPS_LN) * gamma + beta
        key = jax.random.key(seed)
        ks = jax.random.split(key, 10)

        def kaiming(k, shape):
            fan_in = shape[1]
            return jax.random.normal(k, shape, jnp.float32) * jnp.sqrt(2.0 / fan_in)
        pm = jax.random.normal(ks[0], (H, HD, F), jnp.float32)
        return {'x': jax.random.normal(ks[1], (B, N, D), jnp.float32), 'proj': pm, 'w_qkv': kaiming(ks[2], (3 * D, D)), 'w_out': kaiming(ks[3], (D, D)), 'b_out': jnp.zeros((D,), jnp.float32), 'gamma': jnp.ones((D,), jnp.float32), 'beta': jnp.zeros((D,), jnp.float32), 'w1': kaiming(ks[4], (4 * D, D)), 'b1': jnp.zeros((4 * D,), jnp.float32), 'w2': kaiming(ks[5], (D, 4 * D)), 'b2': jnp.zeros((D,), jnp.float32)}
    _L1_attn_in = _L1_attn_setup()

    def _L1_ffn_setup():
        import jax, jax.numpy as jnp
        import numpy as np
        DIM = 128
        DEPTH = 6
        HEADS = 16
        DIM_HEAD = 64
        WINDOW = 32
        INNER = HEADS * DIM_HEAD
        DIM_INNER = int(DIM * 4 * 2 / 3)
        QK_SCALE = 8.0

        def shift_tokens(t):
            a, s = jnp.split(t, 2, -1)
            s = jnp.pad(s, ((0, 0), (1, 0), (0, 0)))[:, :-1]
            return jnp.concatenate([a, s], -1)

        def l2norm(t):
            return t / jnp.maximum(jnp.linalg.norm(t, axis=-1, keepdims=True), 1e-12)

        def rotate_half(x):
            x1, x2 = jnp.split(x, 2, -1)
            return jnp.concatenate([-x2, x1], -1)

        def rotary_tables(n):
            half = jnp.arange(0, DIM_HEAD, 2, dtype=jnp.float32)
            inv_freq = 1.0 / 10000.0 ** (half / DIM_HEAD)
            t = jnp.arange(n, dtype=jnp.float32)
            freqs = t[:, None] * inv_freq[None, :]
            freqs = jnp.concatenate([freqs, freqs], -1)
            base_scale = (half + 0.4 * DIM_HEAD) / (1.4 * DIM_HEAD)
            power = (t - n // 2) / (WINDOW // 2)
            scale = base_scale[None, :] ** power[:, None]
            scale = jnp.concatenate([scale, scale], -1)
            return (freqs, scale)

        def local_attention(q, k, v):
            b, h, n, d = q.shape
            w = WINDOW
            nw = n // w
            bq = q.reshape(b, h, nw, w, d)
            bk = k.reshape(b, h, nw, w, d)
            bv = v.reshape(b, h, nw, w, d)

            def look(t):
                p = jnp.pad(t, ((0, 0), (0, 0), (1, 0), (0, 0), (0, 0)))
                return jnp.concatenate([p[:, :, :nw], p[:, :, 1:]], axis=3)
            bk2, bv2 = (look(bk), look(bv))
            seq = jnp.arange(n).reshape(nw, w)
            seq_p = jnp.pad(seq, ((1, 0), (0, 0)), constant_values=-1)
            jt = jnp.concatenate([seq_p[:nw], seq_p[1:]], axis=1)
            it = seq[:, :, None]
            jb = jt[:, None, :]
            mask = (it < jb) | (it > jb + w) | (jb == -1)
            sim = jnp.einsum('bhwie,bhwje->bhwij', bq, bk2) * QK_SCALE
            sim = jnp.where(mask, -jnp.finfo(sim.dtype).max, sim)
            attn = jax.nn.softmax(sim, -1)
            out = jnp.einsum('bhwij,bhwje->bhwie', attn, bv2)
            return out.reshape(b, h, n, d)

        def attn_layer(x, Wqkv, qs, ksc, Wo):
            b, n, _ = x.shape
            qkv = x @ Wqkv
            q, k, v = jnp.split(qkv, 3, -1)
            sh = lambda t: t.reshape(b, n, HEADS, DIM_HEAD).transpose(0, 2, 1, 3)
            q, k, v = (sh(q), sh(k), sh(v))
            q = l2norm(q) * qs
            k = l2norm(k) * ksc
            freqs, scale = rotary_tables(n)
            cos, sin = (jnp.cos(freqs), jnp.sin(freqs))
            q = q * cos * scale + rotate_half(q) * sin * scale
            inv = 1.0 / scale
            k = k * cos * inv + rotate_half(k) * sin * inv
            out = local_attention(q, k, v)
            out = out.transpose(0, 2, 1, 3).reshape(b, n, INNER)
            return out @ Wo

        def ffn_layer(x, g, bln, W1, b1, W2, b2):
            mu = x.mean(-1, keepdims=True)
            var = ((x - mu) ** 2).mean(-1, keepdims=True)
            xn = (x - mu) / jnp.sqrt(var + 1e-05) * g + bln
            hg = xn @ W1 + b1
            a, gate = jnp.split(hg, 2, -1)
            return a * jax.nn.gelu(gate, approximate=False) @ W2 + b2
        key = jax.random.key(seed)
        ks = jax.random.split(key, 8)
        B, N = (2, 256)
        init = lambda k, shape: jax.random.normal(k, shape, jnp.float32) * 0.02
        return {'x': jax.random.normal(ks[0], (B, N, DIM), jnp.float32), 'Wqkv': init(ks[1], (DEPTH, DIM, 3 * INNER)), 'q_scale': jnp.ones((DEPTH, DIM_HEAD), jnp.float32), 'k_scale': jnp.ones((DEPTH, DIM_HEAD), jnp.float32), 'Wo': init(ks[2], (DEPTH, INNER, DIM)), 'ln_g': jnp.ones((DEPTH, DIM), jnp.float32), 'ln_b': jnp.zeros((DEPTH, DIM), jnp.float32), 'W1': init(ks[3], (DEPTH, DIM, 2 * DIM_INNER)), 'b1': jnp.zeros((DEPTH, 2 * DIM_INNER), jnp.float32), 'W2': init(ks[4], (DEPTH, DIM_INNER, DIM)), 'b2': jnp.zeros((DEPTH, DIM), jnp.float32)}
    _L1_ffn_in = _L1_ffn_setup()
    _d = {'L0_attn_hidden_states': _L0_attn_in['hidden_states'], 'L0_attn_w_qkv': _L0_attn_in['w_qkv'], 'L0_attn_b_qkv': _L0_attn_in['b_qkv'], 'L0_attn_w_g': _L0_attn_in['w_g'], 'L0_attn_b_g': _L0_attn_in['b_g'], 'L0_attn_w_p': _L0_attn_in['w_p'], 'L0_attn_b_p': _L0_attn_in['b_p'], 'L0_ffn_Wr': _L0_ffn_in['Wr'], 'L0_ffn_br': _L0_ffn_in['br'], 'L0_ffn_W1': _L0_ffn_in['W1'], 'L0_ffn_b1': _L0_ffn_in['b1'], 'L0_ffn_W2': _L0_ffn_in['W2'], 'L0_ffn_b2': _L0_ffn_in['b2'], 'L1_attn_proj': _L1_attn_in['proj'], 'L1_attn_w_qkv': _L1_attn_in['w_qkv'], 'L1_attn_w_out': _L1_attn_in['w_out'], 'L1_attn_b_out': _L1_attn_in['b_out'], 'L1_attn_gamma': _L1_attn_in['gamma'], 'L1_attn_beta': _L1_attn_in['beta'], 'L1_attn_w1': _L1_attn_in['w1'], 'L1_attn_b1': _L1_attn_in['b1'], 'L1_attn_w2': _L1_attn_in['w2'], 'L1_attn_b2': _L1_attn_in['b2'], 'L1_ffn_Wqkv': _L1_ffn_in['Wqkv'], 'L1_ffn_q_scale': _L1_ffn_in['q_scale'], 'L1_ffn_k_scale': _L1_ffn_in['k_scale'], 'L1_ffn_Wo': _L1_ffn_in['Wo'], 'L1_ffn_ln_g': _L1_ffn_in['ln_g'], 'L1_ffn_ln_b': _L1_ffn_in['ln_b'], 'L1_ffn_W1': _L1_ffn_in['W1'], 'L1_ffn_b1': _L1_ffn_in['b1'], 'L1_ffn_W2': _L1_ffn_in['W2'], 'L1_ffn_b2': _L1_ffn_in['b2']}
    _x0 = _d['L0_attn_hidden_states']
    _d['L0_attn_hidden_states'] = jax.random.normal(jax.random.fold_in(jax.random.key(seed), 1), (4, 1024, 128), dtype=_x0.dtype)
    del _x0
    return _d

def reference(L0_attn_hidden_states, L0_attn_w_qkv, L0_attn_b_qkv, L0_attn_w_g, L0_attn_b_g, L0_attn_w_p, L0_attn_b_p, L0_ffn_Wr, L0_ffn_br, L0_ffn_W1, L0_ffn_b1, L0_ffn_W2, L0_ffn_b2, L1_attn_proj, L1_attn_w_qkv, L1_attn_w_out, L1_attn_b_out, L1_attn_gamma, L1_attn_beta, L1_attn_w1, L1_attn_b1, L1_attn_w2, L1_attn_b2, L1_ffn_Wqkv, L1_ffn_q_scale, L1_ffn_k_scale, L1_ffn_Wo, L1_ffn_ln_g, L1_ffn_ln_b, L1_ffn_W1, L1_ffn_b1, L1_ffn_W2, L1_ffn_b2):

    def _L0_attn_ref(hidden_states, w_qkv, b_qkv, w_g, b_g, w_p, b_p):
        import jax, jax.numpy as jnp
        import numpy as np
        NUM_HEADS = 8
        SCALE_BASE = 512.0
        GN_EPS = 1e-05

        def rotate_every_two(x):
            x1 = x[..., ::2]
            x2 = x[..., 1::2]
            return jnp.stack([-x2, x1], axis=-1).reshape(x.shape)

        def xpos_apply(x, downscale):
            L, D = (x.shape[1], x.shape[2])
            half = D // 2
            scale_vec = (jnp.arange(0, D, 2, dtype=jnp.float32) + 0.4 * D) / (1.4 * D)
            pos = jnp.arange(L, dtype=jnp.float32)
            scale = scale_vec[None, :] ** (pos[:, None] / SCALE_BASE)
            inv_freq = 1.0 / 10000.0 ** (jnp.arange(half, dtype=jnp.float32) / half)
            sinusoid = pos[:, None] * inv_freq[None, :]
            sin, cos = (jnp.sin(sinusoid), jnp.cos(sinusoid))
            if downscale:
                scale = 1.0 / scale
            sin_s = jnp.repeat(sin * scale, 2, axis=-1)
            cos_s = jnp.repeat(cos * scale, 2, axis=-1)
            return x * cos_s + rotate_every_two(x) * sin_s

        def decay_mask_fn(T, num_heads):
            s, e = (np.log(1.0 / 32.0), np.log(1.0 / 512.0))
            gamma = 1.0 - jnp.exp(jnp.linspace(s, e, num_heads).astype(jnp.float32))
            log_decay = jnp.log(gamma)
            idx = jnp.arange(T)
            expo = (idx[:, None] - idx[None, :]).astype(jnp.float32)
            tri = idx[:, None] >= idx[None, :]
            expo_safe = jnp.where(tri, expo, 0.0)
            mask = jnp.exp(log_decay[:, None, None] * expo_safe) * tri
            scale = jnp.sqrt(mask.sum(axis=-1, keepdims=True))
            return mask / scale

        def _reference_tuple_inner(hidden_states, w_qkv, b_qkv, w_g, b_g, w_p, b_p):
            B, T, E = hidden_states.shape
            H = NUM_HEADS
            V = 2 * E
            dk, dv = (E // H, V // H)
            qkv = hidden_states @ w_qkv + b_qkv
            q, k, v = (qkv[..., :E], qkv[..., E:2 * E], qkv[..., 2 * E:])
            q = xpos_apply(q, downscale=False)
            k = xpos_apply(k, downscale=True)
            q = q.reshape(B, T, H, dk).transpose(0, 2, 1, 3)
            k = k.reshape(B, T, H, dk).transpose(0, 2, 1, 3)
            v = v.reshape(B, T, H, dv).transpose(0, 2, 1, 3)
            mask = decay_mask_fn(T, H)
            retention = jnp.einsum('bhid,bhjd->bhij', q, k) * dk ** (-0.5)
            retention = retention * mask[None]
            out = jnp.einsum('bhij,bhjv->bhiv', retention, v)
            curr_kv = jnp.einsum('hj,bhjk,bhjv->bhkv', mask[:, -1, :], k, v)
            retention_out = out.transpose(0, 2, 1, 3).reshape(B, T, V)
            g = retention_out.reshape(B * T, H, dv)
            mu = g.mean(axis=-1, keepdims=True)
            var = ((g - mu) ** 2).mean(axis=-1, keepdims=True)
            normed = ((g - mu) / jnp.sqrt(var + GN_EPS)).reshape(B, T, V)
            gated = jax.nn.silu(hidden_states @ w_g + b_g) * normed
            proj = gated @ w_p + b_p
            return (proj, curr_kv)
        return _reference_tuple_inner(hidden_states, w_qkv, b_qkv, w_g, b_g, w_p, b_p)[0]

    def _L0_ffn_ref(x, Wr, br, W1, b1, W2, b2):
        import jax, jax.numpy as jnp
        import numpy as np
        D_MODEL, D_FF, N_EXPERTS, TOP_K = (128, 512, 8, 2)
        B, L, D = x.shape
        N = B * L
        x_flat = x.reshape(N, D)
        logits = x_flat @ Wr + br
        probs = jax.nn.softmax(logits, axis=-1)
        topk_probs, topk_idx = jax.lax.top_k(probs, TOP_K)
        topk_probs = topk_probs / (jnp.sum(topk_probs, axis=-1, keepdims=True) + 1e-09)
        rows = jnp.arange(N)[:, None]
        gates = jnp.zeros((N, N_EXPERTS), dtype=x.dtype).at[rows, topk_idx].set(topk_probs)
        out = jnp.zeros((N, D), dtype=x.dtype)
        for e in range(N_EXPERTS):
            h = jax.nn.gelu(x_flat @ W1[e] + b1[e], approximate=False)
            y = h @ W2[e] + b2[e]
            out = out + gates[:, e:e + 1] * y
        return out.reshape(B, L, D)

    def _L1_attn_ref(x, proj, w_qkv, w_out, b_out, gamma, beta, w1, b1, w2, b2):
        import jax, jax.numpy as jnp
        import numpy as np
        B, N, D = (4, 512, 128)
        H, F = (16, 32)
        HD = D // H
        EPS_ATTN = 1e-08
        EPS_LN = 1e-05

        def _layernorm(x, gamma, beta):
            mu = jnp.mean(x, axis=-1, keepdims=True)
            var = jnp.var(x, axis=-1, keepdims=True)
            return (x - mu) * jax.lax.rsqrt(var + EPS_LN) * gamma + beta
        residual = x
        b, n, d = x.shape
        qkv = x @ w_qkv.T
        q, k, v = jnp.split(qkv, 3, axis=-1)

        def to_heads(t):
            return t.reshape(b, n, H, HD).transpose(0, 2, 1, 3)
        q, k, v = (to_heads(q), to_heads(k), to_heads(v))
        q_f = jax.nn.elu(jnp.einsum('bhnd,hdf->bhnf', q, proj)) + 1.0
        k_f = jax.nn.elu(jnp.einsum('bhnd,hdf->bhnf', k, proj)) + 1.0
        kv = jnp.einsum('bhnf,bhnd->bhfd', k_f, v)
        attn = jnp.einsum('bhnf,bhfd->bhnd', q_f, kv)
        k_sum = jnp.sum(k_f, axis=2)
        z = 1.0 / (jnp.einsum('bhnf,bhf->bhn', q_f, k_sum) + EPS_ATTN)
        attn = attn * z[..., None]
        attn = attn.transpose(0, 2, 1, 3).reshape(b, n, d)
        x = residual + attn @ w_out.T + b_out
        x = _layernorm(x, gamma, beta)
        h = jax.nn.gelu(x @ w1.T + b1, approximate=False)
        x = x + h @ w2.T + b2
        x = _layernorm(x, gamma, beta)
        return x

    def _L1_ffn_ref(x, Wqkv, q_scale, k_scale, Wo, ln_g, ln_b, W1, b1, W2, b2):
        import jax, jax.numpy as jnp
        import numpy as np
        DIM = 128
        DEPTH = 6
        HEADS = 16
        DIM_HEAD = 64
        WINDOW = 32
        INNER = HEADS * DIM_HEAD
        DIM_INNER = int(DIM * 4 * 2 / 3)
        QK_SCALE = 8.0

        def shift_tokens(t):
            a, s = jnp.split(t, 2, -1)
            s = jnp.pad(s, ((0, 0), (1, 0), (0, 0)))[:, :-1]
            return jnp.concatenate([a, s], -1)

        def l2norm(t):
            return t / jnp.maximum(jnp.linalg.norm(t, axis=-1, keepdims=True), 1e-12)

        def rotate_half(x):
            x1, x2 = jnp.split(x, 2, -1)
            return jnp.concatenate([-x2, x1], -1)

        def rotary_tables(n):
            half = jnp.arange(0, DIM_HEAD, 2, dtype=jnp.float32)
            inv_freq = 1.0 / 10000.0 ** (half / DIM_HEAD)
            t = jnp.arange(n, dtype=jnp.float32)
            freqs = t[:, None] * inv_freq[None, :]
            freqs = jnp.concatenate([freqs, freqs], -1)
            base_scale = (half + 0.4 * DIM_HEAD) / (1.4 * DIM_HEAD)
            power = (t - n // 2) / (WINDOW // 2)
            scale = base_scale[None, :] ** power[:, None]
            scale = jnp.concatenate([scale, scale], -1)
            return (freqs, scale)

        def local_attention(q, k, v):
            b, h, n, d = q.shape
            w = WINDOW
            nw = n // w
            bq = q.reshape(b, h, nw, w, d)
            bk = k.reshape(b, h, nw, w, d)
            bv = v.reshape(b, h, nw, w, d)

            def look(t):
                p = jnp.pad(t, ((0, 0), (0, 0), (1, 0), (0, 0), (0, 0)))
                return jnp.concatenate([p[:, :, :nw], p[:, :, 1:]], axis=3)
            bk2, bv2 = (look(bk), look(bv))
            seq = jnp.arange(n).reshape(nw, w)
            seq_p = jnp.pad(seq, ((1, 0), (0, 0)), constant_values=-1)
            jt = jnp.concatenate([seq_p[:nw], seq_p[1:]], axis=1)
            it = seq[:, :, None]
            jb = jt[:, None, :]
            mask = (it < jb) | (it > jb + w) | (jb == -1)
            sim = jnp.einsum('bhwie,bhwje->bhwij', bq, bk2) * QK_SCALE
            sim = jnp.where(mask, -jnp.finfo(sim.dtype).max, sim)
            attn = jax.nn.softmax(sim, -1)
            out = jnp.einsum('bhwij,bhwje->bhwie', attn, bv2)
            return out.reshape(b, h, n, d)

        def attn_layer(x, Wqkv, qs, ksc, Wo):
            b, n, _ = x.shape
            qkv = x @ Wqkv
            q, k, v = jnp.split(qkv, 3, -1)
            sh = lambda t: t.reshape(b, n, HEADS, DIM_HEAD).transpose(0, 2, 1, 3)
            q, k, v = (sh(q), sh(k), sh(v))
            q = l2norm(q) * qs
            k = l2norm(k) * ksc
            freqs, scale = rotary_tables(n)
            cos, sin = (jnp.cos(freqs), jnp.sin(freqs))
            q = q * cos * scale + rotate_half(q) * sin * scale
            inv = 1.0 / scale
            k = k * cos * inv + rotate_half(k) * sin * inv
            out = local_attention(q, k, v)
            out = out.transpose(0, 2, 1, 3).reshape(b, n, INNER)
            return out @ Wo

        def ffn_layer(x, g, bln, W1, b1, W2, b2):
            mu = x.mean(-1, keepdims=True)
            var = ((x - mu) ** 2).mean(-1, keepdims=True)
            xn = (x - mu) / jnp.sqrt(var + 1e-05) * g + bln
            hg = xn @ W1 + b1
            a, gate = jnp.split(hg, 2, -1)
            return a * jax.nn.gelu(gate, approximate=False) @ W2 + b2
        for i in range(DEPTH):
            x = attn_layer(shift_tokens(x), Wqkv[i], q_scale[i], k_scale[i], Wo[i]) + x
            x = ffn_layer(shift_tokens(x), ln_g[i], ln_b[i], W1[i], b1[i], W2[i], b2[i]) + x
        return x
    x = L0_attn_hidden_states
    x = x + _L0_attn_ref(_layernorm(x, axis=-1), L0_attn_w_qkv, L0_attn_b_qkv, L0_attn_w_g, L0_attn_b_g, L0_attn_w_p, L0_attn_b_p)
    x = x + _L0_ffn_ref(_layernorm(x, axis=-1), L0_ffn_Wr, L0_ffn_br, L0_ffn_W1, L0_ffn_b1, L0_ffn_W2, L0_ffn_b2)
    x = x + _L1_attn_ref(_layernorm(x, axis=-1), L1_attn_proj, L1_attn_w_qkv, L1_attn_w_out, L1_attn_b_out, L1_attn_gamma, L1_attn_beta, L1_attn_w1, L1_attn_b1, L1_attn_w2, L1_attn_b2)
    x = x + _L1_ffn_ref(_layernorm(x, axis=-1), L1_ffn_Wqkv, L1_ffn_q_scale, L1_ffn_k_scale, L1_ffn_Wo, L1_ffn_ln_g, L1_ffn_ln_b, L1_ffn_W1, L1_ffn_b1, L1_ffn_W2, L1_ffn_b2)
    return x

_drawn_inputs = setup_inputs


def setup_inputs(seed=0):
    import zlib

    import numpy as np

    out = dict(_drawn_inputs(seed))
    spreads = {'L0_attn_b_qkv': (0.0, 0.1),
     'L0_attn_b_g': (0.0, 0.34),
     'L0_attn_b_p': (0.0, 0.1),
     'L0_ffn_br': (0.0, 0.1),
     'L1_attn_b_out': (0.0, 0.1),
     'L1_attn_gamma': (1.0, 0.2),
     'L1_attn_beta': (0.0, 0.1),
     'L1_attn_b1': (0.0, 0.1),
     'L1_attn_b2': (0.0, 0.1),
     'L1_ffn_q_scale': (1.0, 0.6),
     'L1_ffn_k_scale': (1.0, 0.6),
     'L1_ffn_ln_g': (1.0, 0.6),
     'L1_ffn_ln_b': (0.0, 0.8),
     'L1_ffn_b1': (0.0, 0.8),
     'L1_ffn_b2': (0.0, 0.1)}
    factors = {'L0_ffn_b1': 3.94, 'L0_ffn_b2': 2.759, 'L1_ffn_W1': 5.202, 'L1_ffn_W2': 5.058}
    for name, (base, spread) in spreads.items():
        noise = np.random.default_rng([zlib.crc32(name.encode()), seed]).standard_normal(out[name].shape)
        drawn = base * np.exp(spread * noise) if base else spread * noise
        out[name] = jnp.asarray(drawn.astype(out[name].dtype))
    for name, factor in factors.items():
        out[name] = (out[name] * factor).astype(out[name].dtype)
    return out
```

```python
import concourse.bass as bass
from concourse import mybir
from contextlib import ExitStack

F32 = mybir.dt.float32
ALU = mybir.AluOpType
ACT = mybir.ActivationFunctionType
AX = mybir.AxisListType
P = 128
DIM = 128
TILES = 32
SEQ_TILES = 8


def need(eng, sem, value):
    if not (isinstance(value, int) and value <= 0):
        eng.wait_ge(sem, value)


def apart(eng):
    eng.nop(nofuse=True)


class TileNorm:

    def __init__(self, sb, sem, tag, source, S, ident, banks, dest=None):
        self.source, self.S, self.ident, self.banks = source, S, ident, banks
        self.st = sb(tag + "_stats", [P, S, 6])
        self.mv = sb(tag + "_mean_var", [P, S, 2])
        self.ve = sb(tag + "_var_eps", [P, S])
        self.rstd = sb(tag + "_rstd", [P, S])
        self.z = None if dest else sb(tag + "_z", [P, S, DIM])
        self.dest = dest or (lambda n, s: self.z[:, s, :])
        self.zT = sb(tag + "_zT", [P, S * P]) if banks else None
        self.neg_half = sb(tag + "_neg_half", [P, S])
        self.cleared = sem(tag + "_cleared")
        self.stats_made, self.mean_var_made = sem(tag + "_stats_made"), sem(tag + "_mean_var_made")
        self.var_eps_made, self.rstd_made, self.z_made = sem(tag + "_var_eps_made"), sem(tag + "_rstd_made"), sem(tag + "_z_made")
        if banks:
            self.z_turned, self.zT_made = sem(tag + "_z_turned"), sem(tag + "_zT_made")

    def on_pool_start(self, pool):
        pool.memset(self.neg_half[:, :], -0.5).then_inc(self.cleared, 1)
        pool.wait_ge(self.cleared, 1)

    def on_dve(self, dve, n, free_z):
        S = self.S
        for s in range(S):
            dve.bn_stats(self.st[:, s, :], self.source(n, s)).then_inc(self.stats_made, 1)
        dve.wait_ge(self.stats_made, (n + 1) * S)
        apart(dve)
        for s in range(S):
            dve.bn_aggr(self.mv[:, s, :], self.st[:, s, :]).then_inc(self.mean_var_made, 1)
        dve.wait_ge(self.rstd_made, n + 1)
        free_z(dve, n)
        apart(dve)
        for s in range(S):
            dve.tensor_scalar(self.dest(n, s), self.source(n, s), self.mv[:, s, 0:1],
                              self.rstd[:, s:s + 1], ALU.subtract, ALU.mult).then_inc(self.z_made, 1)

    def on_pool(self, pool, n):
        pool.wait_ge(self.mean_var_made, (n + 1) * self.S)
        apart(pool)
        pool.tensor_scalar(self.ve[:, :], self.mv[:, :, 1], 1e-5, None, ALU.add).then_inc(self.var_eps_made, 1)
        pool.wait_ge(self.var_eps_made, n + 1)
        pool.tensor_tensor(self.rstd[:, :], self.ve[:, :], self.neg_half[:, :], ALU.pow).then_inc(self.rstd_made, 1)

    def on_pe(self, pe, n, free_ps):
        pe.wait_ge(self.z_made, (n + 1) * self.S)
        free_ps(pe, n)
        for s in range(self.S):
            e = pe.transpose(self.banks[s // 4][:, s % 4 * P:(s % 4 + 1) * P], self.z[:, s, :], self.ident[:, :])
            if s % 4 == 3:
                e.then_inc(self.z_turned, 1)

    def on_act(self, act, n, free_zT):
        free_zT(act, n)
        for i, b in enumerate(self.banks):
            act.wait_ge(self.z_turned, n * len(self.banks) + i + 1)
            act.activation(self.zT[:, i * 4 * P:(i + 1) * 4 * P], b[:, :], ACT.Copy).then_inc(self.zT_made, 1)


def tiles_of(x, S):
    return lambda n, s: x[:, bass.ds(n * S + s, 1), :].rearrange("p a d -> p (a d)")

def retention_block(nc, sb, sem, bank, ident, ones_row, x, c):
    H = 8
    V = c["w_g"].shape[1]
    QK = 2 * DIM
    DV = V // H
    SEQS = TILES // SEQ_TILES
    NT = SEQ_TILES
    wqkv = sb("ret_wqkv", [P, QK + V])
    wg = sb("ret_wg", [P, V])
    wp = sb("ret_wp", [P, V // P, DIM])
    b_qkv = sb("ret_b_qkv", [1, QK + V])
    b_g = sb("ret_b_g", [1, V])
    b_p = sb("ret_b_p", [1, DIM])
    cos_tab = sb("ret_cos", [P, NT, QK])
    sin_tab = sb("ret_sin", [P, NT, QK])
    tri = sb("ret_tri", [P, P])
    head_of = sb("ret_head_of", [P, H])
    state_mask = sb("ret_state_mask", [P, V])
    decay = sb("ret_decay", [P, 1])
    raw = sb("ret_qkv", [P, 2, QK + V])
    gs = sb("ret_gate", [P, 2, V])
    r1 = sb("ret_cos_part", [P, QK])
    r2 = sb("ret_sin_part", [P, QK])
    qk = sb("ret_qk", [P, 2, QK])
    qkT = sb("ret_qk_T", [P, 2, QK])
    qb = sb("ret_q_by_head", [P, 2, H, P])
    A = sb("ret_scores", [P, 2, H, P])
    state = sb("ret_state", [P, 2, V])
    grown = sb("ret_state_new", [P, V])
    tot = sb("ret_sum", [P, H])
    mu = sb("ret_mean", [P, H])
    xc = sb("ret_centred", [P, V])
    sq = sb("ret_squares", [P, V])
    var = sb("ret_var", [P, H])
    ve = sb("ret_var_eps", [P, H])
    rs = sb("ret_rstd", [P, H])
    neg_half = sb("ret_neg_half", [P, H])
    xn = sb("ret_normed", [P, V])
    gated = sb("ret_gated", [P, V])
    gT = sb("ret_gated_T", [P, V])
    ps_s, ps_q, ps_g, ps_t, ps_o, ps_m = bank[0:2], bank[2:4], bank[4], bank[5], bank[6], bank[7]
    ln = TileNorm(sb, sem, "ret_ln", tiles_of(x, NT), NT, ident, ps_s)
    names = ("loaded cleared qkv_done raw_made g_done gs_made parts_made qk_made qk_turned qkT_made qb_made s_done a_made o_done st_done "
             "grown_made state_made tot_made mu_made xc_made sq_made var_made ve_made rs_made xn_made gated_made gated_turned gT_made "
             "proj_done x_added").split()
    s_ = {k: sem("ret_" + k) for k in names}
    N_LOADS = 12
    wide = [P, H, DV]

    def by_head(a):
        return a.rearrange("p (h d) -> p h d", d=DV)

    with nc.Block() as block:
        @block.sync
        def _(sp):
            n = [0]

            def load(dst, src):
                n[0] += 1
                sp.dma_start(dst, src).then_inc(s_["loaded"], 16)
            load(wqkv[:, :], c["w_qkv"])
            load(wg[:, :], c["w_g"])
            load(wp[:, :, :], c["w_p"].rearrange("(k p) d -> p k d", p=P))
            load(b_qkv[:, :], c["b_qkv"].unsqueeze(0))
            load(b_g[:, :], c["b_g"].unsqueeze(0))
            load(b_p[:, :], c["b_p"].unsqueeze(0))
            load(cos_tab[:, :, :], c["ret_cos"])
            load(sin_tab[:, :, :], c["ret_sin"])
            load(tri[:, :], c["ret_tri"])
            load(head_of[:, :], c["ret_head_of"])
            load(state_mask[:, :], c["ret_state_mask"])
            load(decay[:, :], c["ret_decay"])
            assert n[0] == N_LOADS

        @block.gpsimd
        def _(pool):
            pool.memset(neg_half[:, :], -0.5).then_inc(s_["cleared"], 1)
            ln.on_pool_start(pool)
            pool.wait_ge(s_["cleared"], 1)

            def body(b):
                ln.on_pool(pool, b)
                for t in range(NT):
                    T = NT * b + t
                    pool.wait_ge(s_["var_made"], T + 1)
                    apart(pool)
                    pool.tensor_scalar(ve[:, :], var[:, :], 1.0 / DV, 1e-5, ALU.mult, ALU.add).then_inc(s_["ve_made"], 1)
                    pool.wait_ge(s_["ve_made"], T + 1)
                    need(pool, s_["xn_made"], T)
                    pool.tensor_tensor(rs[:, :], ve[:, :], neg_half[:, :], ALU.pow).then_inc(s_["rs_made"], 1)
            body(0)
            with pool.Fori(1, SEQS) as b:
                body(b)

        @block.scalar
        def _(act):
            def enter(b, t):
                T = NT * b + t
                act.wait_ge(s_["qkv_done"], T + 1)
                need(act, s_["o_done"], T - 1)
                act.activation(raw[:, t % 2, :], ps_q[t % 2][:, :], ACT.Copy).then_inc(s_["raw_made"], 1)
                act.wait_ge(s_["g_done"], T + 1)
                need(act, s_["gated_made"], T - 1)
                act.activation(gs[:, t % 2, :], ps_g[:, 0:V], ACT.Silu).then_inc(s_["gs_made"], 1)

            def body(b):
                ln.on_act(act, b, lambda e, n: need(e, s_["g_done"], NT * n))
                enter(b, 0)
                for t in range(NT):
                    T = NT * b + t
                    act.wait_ge(s_["qk_turned"], T + 1)
                    need(act, s_["o_done"], T - 1)
                    act.activation(qkT[:, t % 2, :], ps_t[:, 0:QK], ACT.Copy).then_inc(s_["qkT_made"], 1)
                    if t + 1 < NT:
                        enter(b, t + 1)
                    act.wait_ge(s_["xc_made"], T + 1)
                    need(act, s_["var_made"], T)
                    act.activation(sq[:, :], xc[:, :], ACT.Square).then_inc(s_["sq_made"], 1)
                    act.wait_ge(s_["gated_turned"], T + 1)
                    need(act, s_["proj_done"], T)
                    act.activation(gT[:, :], ps_t[:, 0:V], ACT.Copy).then_inc(s_["gT_made"], 1)
            body(0)
            with act.Fori(1, SEQS) as b:
                body(b)

        @block.vector
        def _(dve):
            dve.wait_ge(s_["loaded"], 16 * N_LOADS)

            def rope(b, t):
                T = NT * b + t
                dve.wait_ge(s_["raw_made"], T + 1)
                need(dve, s_["qk_made"], T)
                dve.tensor_tensor(r1[:, :], raw[:, t % 2, 0:QK], cos_tab[:, t, :], ALU.mult)
                for i in range(2):
                    m = dve.tensor_tensor(r2[:, i:QK:2], raw[:, t % 2, 1 - i:QK:2], sin_tab[:, t, i:QK:2], ALU.mult)
                m.then_inc(s_["parts_made"], 1)
                dve.wait_ge(s_["parts_made"], T + 1)
                need(dve, s_["st_done"], (NT - 1) * b + t - 1)
                need(dve, s_["qk_turned"], T - 1)
                dve.tensor_tensor(qk[:, t % 2, :], r1[:, :], r2[:, :], ALU.add).then_inc(s_["qk_made"], 1)

            def scores(b, t):
                T = NT * b + t
                dve.wait_ge(s_["qkT_made"], T + 1)
                need(dve, s_["s_done"], 2 * (T - 1))
                dve.tensor_tensor(qb[:, t % 2, :, :], qkT[:, t % 2, 0:P].unsqueeze(1).to_broadcast([P, H, P]),
                                  head_of[:, :].unsqueeze(2).to_broadcast([P, H, P]), ALU.mult).then_inc(s_["qb_made"], 1)
                need(dve, s_["o_done"], T - 1)
                for i in range(2):
                    dve.wait_ge(s_["s_done"], 2 * T + i + 1)
                    dve.tensor_tensor(A[:, t % 2, 4 * i:4 * i + 4, :], ps_s[i].rearrange("p (h q) -> p h q", q=P),
                                      tri[:, :].unsqueeze(1).to_broadcast([P, 4, P]), ALU.mult).then_inc(s_["a_made"], 1)

            def next_state(b, t):
                K = (NT - 1) * b + t
                dve.wait_ge(s_["st_done"], K + 1)
                need(dve, s_["o_done"], NT * b + t)
                out = state[:, (t + 1) % 2, :] if t == 0 else grown[:, :]
                dve.tensor_tensor(out, ps_m[:, 0:V], state_mask[:, :], ALU.mult).then_inc(s_["grown_made"], 1)
                if t:
                    dve.wait_ge(s_["grown_made"], K + 1)
                    dve.wait_ge(s_["state_made"], K)
                    dve.scalar_tensor_tensor(state[:, (t + 1) % 2, :], state[:, t % 2, :], decay[:, 0:1], grown[:, :], ALU.mult, ALU.add
                                             ).then_inc(s_["state_made"], 1)
                else:
                    dve.wait_ge(s_["grown_made"], K + 1)
                    dve.sem_inc(s_["state_made"], 1)

            def group_norm(b, t):
                T = NT * b + t
                o = by_head(ps_o[:, 0:V])
                dve.wait_ge(s_["o_done"], T + 1)
                dve.tensor_reduce(tot[:, :], o, AX.X, ALU.add).then_inc(s_["tot_made"], 1)
                dve.wait_ge(s_["tot_made"], T + 1)
                dve.tensor_scalar(mu[:, :], tot[:, :], 1.0 / DV, None, ALU.mult).then_inc(s_["mu_made"], 1)
                dve.wait_ge(s_["mu_made"], T + 1)
                dve.tensor_tensor(by_head(xc[:, :]), o, mu[:, :].unsqueeze(2).to_broadcast(wide), ALU.subtract).then_inc(s_["xc_made"], 1)
                dve.wait_ge(s_["sq_made"], T + 1)
                dve.tensor_reduce(var[:, :], by_head(sq[:, :]), AX.X, ALU.add).then_inc(s_["var_made"], 1)
                dve.wait_ge(s_["rs_made"], T + 1)
                dve.tensor_tensor(by_head(xn[:, :]), by_head(xc[:, :]), rs[:, :].unsqueeze(2).to_broadcast(wide), ALU.mult).then_inc(s_["xn_made"], 1)
                dve.wait_ge(s_["xn_made"], T + 1)
                dve.wait_ge(s_["gs_made"], T + 1)
                need(dve, s_["gated_turned"], T)
                dve.tensor_tensor(gated[:, :], xn[:, :], gs[:, t % 2, :], ALU.mult).then_inc(s_["gated_made"], 1)

            def residual(b, t):
                T = NT * b + t
                dve.wait_ge(s_["proj_done"], T + 1)
                apart(dve)
                xs = x[:, bass.ds(T, 1), :].rearrange("p a d -> p (a d)")
                dve.tensor_tensor(xs, ps_m[:, V:V + DIM], xs, ALU.add).then_inc(s_["x_added"], 1)

            def body(b):
                ln.on_dve(dve, b, lambda e, n: need(e, ln.z_turned, 2 * n))
                rope(b, 0)
                for t in range(NT):
                    scores(b, t)
                    if t + 1 < NT:
                        next_state(b, t)
                        rope(b, t + 1)
                    group_norm(b, t)
                    residual(b, t)
            body(0)
            with dve.Fori(1, SEQS) as b:
                body(b)

        @block.tensor
        def _(pe):
            pe.wait_ge(s_["loaded"], 16 * N_LOADS)

            def enter(b, t):
                T = NT * b + t
                pe.wait_ge(ln.zT_made, 2 * b + t // 4 + 1)
                zT = ln.zT[:, t * P:(t + 1) * P]
                need(pe, s_["raw_made"], T - 1)
                pe.matmul(ps_q[t % 2][:, :], zT, wqkv[:, :], start=True, stop=False)
                pe.matmul(ps_q[t % 2][:, :], ones_row[0:1, :], b_qkv[0:1, :], start=False, stop=True).then_inc(s_["qkv_done"], 1)
                need(pe, s_["gs_made"], T)
                pe.matmul(ps_g[:, 0:V], zT, wg[:, :], start=True, stop=False)
                pe.matmul(ps_g[:, 0:V], ones_row[0:1, :], b_g[0:1, :], start=False, stop=True).then_inc(s_["g_done"], 1)

            def turn_qk(b, t):
                T = NT * b + t
                pe.wait_ge(s_["qk_made"], T + 1)
                need(pe, s_["gT_made"], T)
                for i in range(2):
                    m = pe.transpose(ps_t[:, i * P:(i + 1) * P], qk[:, t % 2, i * P:(i + 1) * P], ident[:, :])
                m.then_inc(s_["qk_turned"], 1)

            def scores(b, t):
                T = NT * b + t
                pe.wait_ge(s_["qb_made"], T + 1)
                need(pe, s_["a_made"], 2 * T)
                if t == 0:
                    pe.wait_ge(ln.zT_made, 2 * b + 2)
                for i in range(2):
                    pe.matmul(ps_s[i][:, :], qkT[:, t % 2, P:2 * P], qb[:, t % 2, 4 * i:4 * i + 4, :].rearrange("p h q -> p (h q)"),
                              start=True, stop=True).then_inc(s_["s_done"], 1)

            def state_part(b, t):
                T = NT * b + t
                need(pe, s_["x_added"], T)
                need(pe, s_["grown_made"], (NT - 1) * b + t)
                pe.matmul(ps_m[:, 0:V], qk[:, t % 2, P:2 * P], raw[:, t % 2, QK:QK + V], start=True, stop=True).then_inc(s_["st_done"], 1)

            def output(b, t):
                T = NT * b + t
                need(pe, s_["xc_made"], T)
                if t:
                    pe.wait_ge(s_["state_made"], (NT - 1) * b + t)
                    pe.matmul(ps_o[:, 0:V], qkT[:, t % 2, 0:P], state[:, t % 2, :], start=True, stop=True)
                pe.wait_ge(s_["a_made"], 2 * T + 2)
                for h in range(H):
                    m = pe.matmul(ps_o[:, h * DV:(h + 1) * DV], A[:, t % 2, h, :], raw[:, t % 2, QK + h * DV:QK + (h + 1) * DV],
                                  start=(t == 0), stop=True, skip_group_check=True)
                m.then_inc(s_["o_done"], 1)

            def project(b, t):
                T = NT * b + t
                pe.wait_ge(s_["gated_made"], T + 1)
                pe.wait_ge(s_["qkT_made"], T + 1)
                for i in range(V // P):
                    m = pe.transpose(ps_t[:, i * P:(i + 1) * P], gated[:, i * P:(i + 1) * P], ident[:, :])
                m.then_inc(s_["gated_turned"], 1)
                pe.wait_ge(s_["gT_made"], T + 1)
                if t + 1 < NT:
                    pe.wait_ge(s_["grown_made"], (NT - 1) * b + t + 1)
                for i in range(V // P):
                    pe.matmul(ps_m[:, V:V + DIM], gT[:, i * P:(i + 1) * P], wp[:, i, :], start=(i == 0), stop=False)
                pe.matmul(ps_m[:, V:V + DIM], ones_row[0:1, :], b_p[0:1, :], start=False, stop=True).then_inc(s_["proj_done"], 1)

            def body(b):
                ln.on_pe(pe, b, lambda e, n: need(e, s_["a_made"], 2 * NT * n))
                enter(b, 0)
                for t in range(NT):
                    turn_qk(b, t)
                    if t + 1 < NT:
                        enter(b, t + 1)
                    scores(b, t)
                    if t + 1 < NT:
                        state_part(b, t)
                    output(b, t)
                    project(b, t)
            body(0)
            with pe.Fori(1, SEQS) as b:
                body(b)

def mixture(nc, sb, sem, bank, ident, ones_row, x, c):
    EXPERTS, _, FF = c["W1"].shape
    FC = FF // P
    S = 4
    ROUNDS = TILES // S
    w1 = sb("moe_w1", [P, EXPERTS, FF])
    w2 = sb("moe_w2", [P, EXPERTS, FC, DIM])
    wr = sb("moe_wr", [P, EXPERTS])
    br = sb("moe_br", [1, EXPERTS])
    b1c = sb("moe_b1_col", [P, EXPERTS, FC])
    b2 = sb("moe_b2", [EXPERTS, DIM])
    rank = sb("moe_rank", [P, S, EXPERTS])
    hT = sb("moe_hidden_T", [P, 2, FC, S * P])
    acc = sb("moe_acc", [P, S, DIM])
    prob = sb("moe_probs", [P, S, EXPERTS])
    work = sb("moe_work", [P, S, EXPERTS])
    work2 = sb("moe_work2", [P, S, EXPERTS])
    hot1 = sb("moe_first", [P, S, EXPERTS])
    hot2 = sb("moe_second", [P, S, EXPERTS])
    col = sb("moe_col", [P, S])
    colb = sb("moe_colb", [P, S])
    gates = sb("moe_gates", [P, S, EXPERTS])
    gatesT = sb("moe_gates_T", [EXPERTS, S * P])
    psZ, psR = bank[0], bank[1]
    psY, psH = bank[2:4], bank[4:8]
    ln = TileNorm(sb, sem, "moe_ln", tiles_of(x, S), S, ident, [psZ])
    small_loaded, w_loaded = sem("moe_small_loaded"), [sem("moe_weights_loaded_0"), sem("moe_weights_loaded_1")]
    logits_done, exp_made, step_made, gates_made, gates_turned, gatesT_made, bias_done, acc_made = (sem("moe_" + s) for s in (
        "logits_done", "exp_made", "step_made", "gates_made", "gates_turned", "gatesT_made", "bias_done", "acc_made"))
    up_done, gelu_made, down_done, added = sem("moe_up_done"), sem("moe_gelu_made"), sem("moe_down_done"), sem("moe_added")
    N_SMALL = 5
    LOTS = [(0, 2), (2, EXPERTS)]
    STEPS = 21

    with nc.Block() as block:
        @block.sync
        def _(sp):
            sp.dma_start(wr[:, :], c["Wr"]).then_inc(small_loaded, 16)
            sp.dma_start(br[:, :], c["br"].unsqueeze(0)).then_inc(small_loaded, 16)
            sp.dma_start(b2[:, :], c["b2"]).then_inc(small_loaded, 16)
            sp.dma_start(rank[:, :, :], c["rank"]).then_inc(small_loaded, 16)
            with nc.allow_non_contiguous_dma("small columns"):
                sp.dma_start(b1c[:, :, :], c["b1"].rearrange("e (c p) -> p e c", p=P)).then_inc(small_loaded, 16)
            for i, (lo, hi) in enumerate(LOTS):
                for dst, src in ((w1[:, lo:hi, :], c["W1"][lo:hi, :, :].rearrange("e p f -> p e f")),
                                 (w2[:, lo:hi, :, :], c["W2"][lo:hi, :, :].rearrange("e (c p) d -> p e c d", p=P))):
                    sp.dma_start(dst, src).then_inc(w_loaded[i], 16)

        @block.gpsimd
        def _(pool):
            ln.on_pool_start(pool)
            with pool.Fori(0, ROUNDS) as n:
                ln.on_pool(pool, n)

        @block.scalar
        def _(act):
            act.wait_ge(small_loaded, 16 * N_SMALL)

            def body(n):
                ln.on_act(act, n, lambda e, n: need(e, up_done, n * EXPERTS * FC))
                act.wait_ge(step_made, STEPS * n + 2)
                act.activation(prob[:, :, :], work[:, :, :], ACT.Exp).then_inc(exp_made, 1)
                for e in range(EXPERTS):
                    i = n * EXPERTS + e
                    need(act, down_done, i - 1)
                    for ch in range(FC):
                        act.wait_ge(up_done, i * FC + ch + 1)
                        act.activation(hT[:, e % 2, ch, :], psH[ch][:, :], ACT.Gelu, bias=b1c[:, e, ch:ch + 1]).then_inc(gelu_made, 1)
                    if e == 1:
                        act.wait_ge(gates_turned, n + 1)
                        need(act, bias_done, n)
                        act.activation(gatesT[:, :], psZ[0:EXPERTS, :], ACT.Copy).then_inc(gatesT_made, 1)
            body(0)
            with act.Fori(1, ROUNDS) as n:
                body(n)

        @block.vector
        def _(dve):
            dve.wait_ge(small_loaded, 16 * N_SMALL)

            def route(n):
                k = [0]
                wide = [P, S, EXPERTS]

                def step(ins):
                    k[0] += 1
                    ins.then_inc(step_made, 1)
                    dve.wait_ge(step_made, STEPS * n + k[0])

                def spread(a):
                    return a[:, :].unsqueeze(2).to_broadcast(wide)

                def first_of_largest(hot, p):
                    step(dve.tensor_reduce(col[:, :], p[:, :, :], AX.X, ALU.max))
                    step(dve.tensor_tensor(work[:, :, :], p[:, :, :], spread(col), ALU.is_equal))
                    step(dve.tensor_tensor(work[:, :, :], work[:, :, :], rank[:, :, :], ALU.mult))
                    step(dve.tensor_reduce(colb[:, :], work[:, :, :], AX.X, ALU.max))
                    step(dve.tensor_tensor(hot[:, :, :], work[:, :, :], spread(colb), ALU.is_equal))

                logits = psR[:, 0:S * EXPERTS].rearrange("p (s e) -> p s e", e=EXPERTS)
                dve.wait_ge(logits_done, n + 1)
                step(dve.tensor_reduce(col[:, :], logits, AX.X, ALU.max))
                step(dve.tensor_tensor(work[:, :, :], logits, spread(col), ALU.subtract))
                dve.wait_ge(exp_made, n + 1)
                step(dve.tensor_reduce(col[:, :], prob[:, :, :], AX.X, ALU.add))
                step(dve.reciprocal(colb[:, :], col[:, :]))
                step(dve.tensor_tensor(prob[:, :, :], prob[:, :, :], spread(colb), ALU.mult))
                first_of_largest(hot1, prob)
                step(dve.scalar_tensor_tensor(work2[:, :, :], hot1[:, :, :], -2.0, prob[:, :, :], ALU.mult, ALU.add))
                first_of_largest(hot2, work2)
                step(dve.tensor_tensor(work[:, :, :], hot1[:, :, :], hot2[:, :, :], ALU.add))
                step(dve.tensor_tensor(work2[:, :, :], work[:, :, :], prob[:, :, :], ALU.mult))
                step(dve.tensor_reduce(col[:, :], work2[:, :, :], AX.X, ALU.add))
                step(dve.tensor_scalar(colb[:, :], col[:, :], 1e-9, None, ALU.add))
                step(dve.reciprocal(col[:, :], colb[:, :]))
                assert k[0] == STEPS
                need(dve, gates_turned, n)
                dve.tensor_tensor(gates[:, :, :], work2[:, :, :], spread(col), ALU.mult).then_inc(gates_made, 1)

            def body(n):
                ln.on_dve(dve, n, lambda e, n: need(e, ln.z_turned, n))
                route(n)
                dve.wait_ge(bias_done, n + 1)
                apart(dve)
                dve.tensor_tensor(acc[:, :, :].rearrange("p s d -> p (s d)"), psR[:, :],
                                  x[:, bass.ds(n * S, S), :].rearrange("p s d -> p (s d)"), ALU.add).then_inc(acc_made, 1)
                dve.wait_ge(acc_made, n + 1)
                for e in range(EXPERTS):
                    i = n * EXPERTS + e
                    dve.wait_ge(down_done, i + 1)
                    if e:
                        dve.wait_ge(added, S * i)
                    else:
                        dve.wait_ge(gates_made, n + 1)
                    apart(dve)
                    for s in range(S):
                        out = x[:, bass.ds(n * S + s, 1), :].rearrange("p a d -> p (a d)") if e == EXPERTS - 1 else acc[:, s, :]
                        dve.scalar_tensor_tensor(out, psY[e % 2][:, s * P:(s + 1) * P], gates[:, s, e:e + 1], acc[:, s, :],
                                                 ALU.mult, ALU.add).then_inc(added, 1)
            body(0)
            with dve.Fori(1, ROUNDS) as n:
                body(n)

        @block.tensor
        def _(pe):
            pe.wait_ge(small_loaded, 16 * N_SMALL)

            def up(n, e):
                i = n * EXPERTS + e
                if isinstance(n, int):
                    pe.wait_ge(w_loaded[0 if e < 2 else 1], 32)
                for ch in range(FC):
                    need(pe, gelu_made, (i - 1) * FC + ch + 1)
                    pe.matmul(psH[ch][:, :], w1[:, e, ch * P:(ch + 1) * P], ln.zT[:, :], start=True, stop=True).then_inc(up_done, 1)

            def down(n, e):
                i = n * EXPERTS + e
                need(pe, added, S * (i - 1))
                pe.wait_ge(gelu_made, (i + 1) * FC)
                for s in range(S):
                    for ch in range(FC):
                        m = pe.matmul(psY[e % 2][:, s * P:(s + 1) * P], hT[:, e % 2, ch, s * P:(s + 1) * P], w2[:, e, ch, :],
                                      start=(ch == 0), stop=(ch == FC - 1))
                m.then_inc(down_done, 1)

            def body(n):
                ln.on_pe(pe, n, lambda e, n: need(e, gatesT_made, n))
                pe.wait_ge(ln.zT_made, n + 1)
                need(pe, acc_made, n)
                for s in range(S):
                    o = psR[:, s * EXPERTS:(s + 1) * EXPERTS]
                    pe.matmul(o, ln.zT[:, s * P:(s + 1) * P], wr[:, :], start=True, stop=False)
                    m = pe.matmul(o, ones_row[0:1, :], br[0:1, :], start=False, stop=True)
                m.then_inc(logits_done, 1)
                up(n, 0)
                up(n, 1)
                down(n, 0)
                pe.wait_ge(gates_made, n + 1)
                for s in range(S):
                    m = pe.transpose(psZ[0:EXPERTS, s * P:(s + 1) * P], gates[:, s, :], ident[:, :])
                m.then_inc(gates_turned, 1)
                pe.wait_ge(gatesT_made, n + 1)
                apart(pe)
                for s in range(S):
                    m = pe.matmul(psR[:, s * P:(s + 1) * P], gatesT[:, s * P:(s + 1) * P], b2[:, :], start=True, stop=True)
                m.then_inc(bias_done, 1)
                for e in range(2, EXPERTS):
                    up(n, e)
                    down(n, e - 1)
                down(n, EXPERTS - 1)
            body(0)
            with pe.Fori(1, ROUNDS) as n:
                body(n)

def linear_block(nc, sb, sem, bank, ident, ones_row, x, c):
    H, HD, NF = c["proj"].shape
    FF = c["w1T"].shape[1]
    FC = FF // P
    KC = H * NF // P
    HC = P // NF
    SEQS = TILES // SEQ_TILES
    S = 4
    W = S * P
    wqk = sb("lin_wqk", [P, 2, DIM])
    wvT = sb("lin_wvT", [P, DIM])
    blocks = sb("lin_proj_blocks", [P, H * NF])
    G = sb("lin_feature_weights", [P, 2, H * NF])
    w_outT = sb("lin_w_outT", [P, DIM])
    w1T = sb("lin_w1T", [P, FF])
    w2T = sb("lin_w2T", [P, FC, DIM])
    b_out = sb("lin_b_out", [1, DIM])
    b2 = sb("lin_b2", [1, DIM])
    b1c = sb("lin_b1_col", [P, FC])
    gamma = sb("lin_gamma", [P, DIM])
    beta = sb("lin_beta", [P, DIM])
    kv_mask = sb("lin_kv_mask", [P, KC, DIM])
    ks_mask = sb("lin_ks_mask", [P, KC, H])
    low = sb("lin_low", [P, 2, W])
    kf = sb("lin_kf", [P, 2, H * NF])
    v1 = sb("lin_v_and_one", [P, SEQ_TILES, DIM + 1])
    kv = sb("lin_kv", [P, KC, DIM])
    ks = sb("lin_ksum", [P, KC, H])
    qf = sb("lin_qf_T", [P, KC, SEQ_TILES * P])
    den = sb("lin_den", [P, S * H])
    rden = sb("lin_inv_den", [P, S * H])
    at = sb("lin_attn", [P, W])
    atT = sb("lin_attn_T", [P, W])
    x1 = sb("lin_x1", [P, S, DIM])
    gm = sb("lin_gained", [P, S, DIM])
    x1n = sb("lin_x1_normed", [P, S, DIM])
    x1T = sb("lin_x1_T", [P, W])
    hT = sb("lin_hidden_T", [P, FC, W])
    x2 = sb("lin_x2", [P, S, DIM])
    gm2 = sb("lin_gained2", [P, S, DIM])
    y = sb("lin_y", [P, S, DIM])
    ps_z, ps_u, ps_kv, ps_v, ps_m = bank[0:2], bank[2:4], bank[4:6], bank[6], bank[7]
    ln = TileNorm(sb, sem, "lin_ln", tiles_of(x, SEQ_TILES), SEQ_TILES, ident, ps_z)
    ln1 = TileNorm(sb, sem, "lin_ln1", lambda n, s: x1[:, s, :], S, ident, None)
    ln2 = TileNorm(sb, sem, "lin_ln2", lambda n, s: x2[:, s, :], S, ident, None)
    names = ("loaded weights_cleared blocks_loaded g_done g_made u_done low_made exp_made kf_made v_done v_made kv_done kv_made "
             "attn_done den_made rden_made at_made at_turned atT_made o_done x1_made gained1 x1n_made x1n_turned x1T_made "
             "up_done gelu_made down_done x2_made gained2 y_made x_added").split()
    s_ = {k: sem("lin_" + k) for k in names}
    N_LOADS = 12
    UT = 2 * SEQ_TILES

    with nc.Block() as block:
        @block.sync
        def _(sp):
            n = [0]

            def load(dst, src):
                n[0] += 1
                sp.dma_start(dst, src).then_inc(s_["loaded"], 16)
            load(wqk[:, :, :], c["w_qkv"][0:2 * DIM, :].rearrange("(a o) i -> o a i", a=2))
            load(wvT[:, :], c["wvT"])
            load(w_outT[:, :], c["w_outT"])
            load(w1T[:, :], c["w1T"])
            load(w2T[:, :, :], c["w2T"].rearrange("(c p) d -> p c d", p=P))
            load(b_out[:, :], c["b_out"].unsqueeze(0))
            load(b2[:, :], c["b2"].unsqueeze(0))
            with nc.allow_non_contiguous_dma("small columns"):
                load(b1c[:, :], c["b1"].rearrange("(c p) -> p c", p=P))
            load(gamma[:, :], c["gamma"].partition_broadcast(P))
            load(beta[:, :], c["beta"].partition_broadcast(P))
            load(kv_mask[:, :, :], c["kv_mask"])
            load(ks_mask[:, :, :], c["ks_mask"])
            assert n[0] == N_LOADS
            sp.wait_ge(s_["weights_cleared"], 2)
            for h in range(H):
                sp.dma_start(blocks[h * HD:(h + 1) * HD, h * NF:(h + 1) * NF], c["proj"][h, :, :]).then_inc(s_["blocks_loaded"], 16)

        @block.gpsimd
        def _(pool):
            pool.memset(blocks[:, :], 0.0).then_inc(s_["weights_cleared"], 1)
            pool.memset(v1[:, :, DIM:DIM + 1], 1.0).then_inc(s_["weights_cleared"], 1)
            for l in (ln, ln1, ln2):
                l.on_pool_start(pool)
            pool.wait_ge(s_["loaded"], 16 * N_LOADS)

            def gain(l, r, g_buf, out, gained, made, free):
                pool.wait_ge(l.z_made, S * (r + 1))
                need(pool, made, r)
                apart(pool)
                pool.tensor_tensor(g_buf[:, :, :], l.z[:, :, :], gamma[:, :].unsqueeze(1).to_broadcast([P, S, DIM]), ALU.mult).then_inc(gained, 1)
                pool.wait_ge(gained, r + 1)
                free(r)
                apart(pool)
                pool.tensor_tensor(out[:, :, :], g_buf[:, :, :], beta[:, :].unsqueeze(1).to_broadcast([P, S, DIM]), ALU.add).then_inc(made, 1)

            def body(b):
                ln.on_pool(pool, b)
                for g in range(2):
                    r = 2 * b + g
                    ln1.on_pool(pool, r)
                    gain(ln1, r, gm, x1n, s_["gained1"], s_["x1n_made"], lambda r: need(pool, s_["x2_made"], r))
                    ln2.on_pool(pool, r)
                    gain(ln2, r, gm2, y, s_["gained2"], s_["y_made"], lambda r: need(pool, s_["x_added"], r))
            body(0)
            with pool.Fori(1, SEQS) as b:
                body(b)

        @block.scalar
        def _(act):
            act.wait_ge(s_["loaded"], 16 * N_LOADS)
            act.wait_ge(s_["g_done"], 2)
            for a in range(2):
                act.activation(G[:, a, :], ps_u[a][:, :], ACT.Copy).then_inc(s_["g_made"], 1)

            def exp_low(b, i):
                U = UT * b + i
                act.wait_ge(s_["low_made"], U + 1)
                act.activation(low[:, i % 2, :], low[:, i % 2, :], ACT.Exp).then_inc(s_["exp_made"], 1)

            def evac(src, dst, done, made, free, r):
                act.wait_ge(done, r + 1)
                need(act, free, r)
                act.activation(dst[:, :], src[:, :], ACT.Copy).then_inc(made, 1)

            def body(b):
                ln.on_act(act, b, lambda e, n: need(e, s_["u_done"], UT * n))
                for half in range(2):
                    act.wait_ge(s_["v_done"], 2 * b + half + 1)
                    need(act, s_["kv_done"], b)
                    act.activation(v1[:, 4 * half:4 * half + 4, 0:DIM], ps_v.rearrange("p (s d) -> p s d", d=DIM), ACT.Copy).then_inc(s_["v_made"], 1)
                    for i in range(4 * half, 4 * half + 4):
                        exp_low(b, i)
                for i in range(SEQ_TILES, UT):
                    exp_low(b, i)
                for g in range(2):
                    r = 2 * b + g
                    evac(ps_m, atT, s_["at_turned"], s_["atT_made"], s_["o_done"], r)
                    evac(ps_m, x1T, s_["x1n_turned"], s_["x1T_made"], s_["down_done"], r)
                    for ch in range(FC):
                        act.wait_ge(s_["up_done"], FC * r + ch + 1)
                        need(act, s_["down_done"], r)
                        act.activation(hT[:, ch, :], ps_u[ch % 2][:, :], ACT.Gelu, bias=b1c[:, ch:ch + 1]).then_inc(s_["gelu_made"], 1)
            body(0)
            with act.Fori(1, SEQS) as b:
                body(b)

        @block.vector
        def _(dve):
            dve.wait_ge(s_["loaded"], 16 * N_LOADS)

            def feature(b, i):
                U = UT * b + i
                dve.wait_ge(s_["u_done"], U + 1)
                need(dve, s_["kf_made"], U - 1)
                dve.tensor_scalar(low[:, i % 2, :], ps_u[i % 2][:, :], 0.0, None, ALU.min).then_inc(s_["low_made"], 1)

            def feature_end(b, i):
                U = UT * b + i
                out = kf[:, i % 2, :] if i < SEQ_TILES else qf[:, i % KC, (i - SEQ_TILES) // KC * W:((i - SEQ_TILES) // KC + 1) * W]
                dve.wait_ge(s_["exp_made"], U + 1)
                if i < SEQ_TILES:
                    need(dve, s_["kv_done"], SEQ_TILES * b + i - 1)
                else:
                    need(dve, s_["attn_done"], 2 * b)
                dve.scalar_tensor_tensor(out, ps_u[i % 2][:, :], 0.0, low[:, i % 2, :], ALU.max, ALU.add).then_inc(s_["kf_made"], 1)

            def body(b):
                ln.on_dve(dve, b, lambda e, n: need(e, s_["x1_made"], 2 * n))
                feature(b, 0)
                for i in range(1, SEQ_TILES):
                    feature(b, i)
                    feature_end(b, i - 1)
                feature_end(b, SEQ_TILES - 1)
                dve.wait_ge(s_["kv_done"], SEQ_TILES * (b + 1))
                need(dve, s_["attn_done"], 2 * b)
                apart(dve)
                for ch in range(KC):
                    o = (ch % 2) * (DIM + 1)
                    dve.tensor_tensor(kv[:, ch, :], ps_kv[ch // 2][:, o:o + DIM], kv_mask[:, ch, :], ALU.mult)
                    dve.tensor_tensor(ks[:, ch, :], ps_kv[ch // 2][:, o + DIM:o + DIM + 1].to_broadcast([P, H]), ks_mask[:, ch, :],
                                      ALU.mult).then_inc(s_["kv_made"], 1)
                feature(b, SEQ_TILES)
                for i in range(SEQ_TILES + 1, UT):
                    feature(b, i)
                    feature_end(b, i - 1)
                feature_end(b, UT - 1)
                for g in range(2):
                    r = 2 * b + g
                    dve.wait_ge(s_["attn_done"], r + 1)
                    dve.tensor_scalar(den[:, :], ps_v[:, 0:S * H], 1e-8, None, ALU.add).then_inc(s_["den_made"], 1)
                    dve.wait_ge(s_["den_made"], r + 1)
                    dve.reciprocal(rden[:, :], den[:, :]).then_inc(s_["rden_made"], 1)
                    dve.wait_ge(s_["rden_made"], r + 1)
                    need(dve, s_["at_turned"], r)
                    dve.tensor_tensor(at[:, :].rearrange("p (h d) -> p h d", d=HD), ps_m.rearrange("p (h d) -> p h d", d=HD),
                                      rden[:, :].unsqueeze(2).to_broadcast([P, S * H, HD]), ALU.mult).then_inc(s_["at_made"], 1)
                    dve.wait_ge(s_["o_done"], r + 1)
                    apart(dve)
                    dve.tensor_tensor(x1[:, :, :].rearrange("p s d -> p (s d)"), ps_m[:, :], ln.z[:, 4 * g:4 * g + 4, :].rearrange("p s d -> p (s d)"),
                                      ALU.add).then_inc(s_["x1_made"], 1)
                    dve.wait_ge(s_["x1_made"], r + 1)
                    apart(dve)
                    ln1.on_dve(dve, r, lambda e, n: need(e, s_["gained1"], n))
                    dve.wait_ge(s_["down_done"], r + 1)
                    dve.wait_ge(s_["x1n_made"], r + 1)
                    dve.tensor_tensor(x2[:, :, :].rearrange("p s d -> p (s d)"), ps_m[:, :], x1n[:, :, :].rearrange("p s d -> p (s d)"),
                                      ALU.add).then_inc(s_["x2_made"], 1)
                    dve.wait_ge(s_["x2_made"], r + 1)
                    apart(dve)
                    ln2.on_dve(dve, r, lambda e, n: need(e, s_["gained2"], n))
                    dve.wait_ge(s_["y_made"], r + 1)
                    apart(dve)
                    xs = x[:, bass.ds(r * S, S), :].rearrange("p s d -> p (s d)")
                    dve.tensor_tensor(xs, xs, y[:, :, :].rearrange("p s d -> p (s d)"), ALU.add).then_inc(s_["x_added"], 1)
            body(0)
            with dve.Fori(1, SEQS) as b:
                body(b)

        @block.tensor
        def _(pe):
            pe.wait_ge(s_["loaded"], 16 * N_LOADS)
            pe.wait_ge(s_["blocks_loaded"], 16 * H)
            for a in range(2):
                pe.matmul(ps_u[a][:, :], wqk[:, a, :], blocks[:, :], start=True, stop=True).then_inc(s_["g_done"], 1)
            pe.wait_ge(s_["g_made"], 2)

            def free_u(b, i):
                if i < 2:
                    need(pe, s_["gelu_made"], 2 * FC * b)
                need(pe, s_["kf_made"], UT * b + i - 1)

            def body(b):
                ln.on_pe(pe, b, lambda e, n: need(e, ln.zT_made, 2 * n))
                pe.wait_ge(ln.zT_made, 2 * b + 2)

                def values(half):
                    need(pe, s_["v_made"] if half else s_["rden_made"], 2 * b + half)
                    for t in range(4 * half, 4 * half + 4):
                        m = pe.matmul(ps_v[:, t % 4 * DIM:(t % 4 + 1) * DIM], ln.zT[:, t * P:(t + 1) * P], wvT[:, :], start=True, stop=True)
                    m.then_inc(s_["v_done"], 1)

                def keys(t):
                    free_u(b, t)
                    pe.matmul(ps_u[t % 2][:, :], ln.zT[:, t * P:(t + 1) * P], G[:, 1, :], start=True, stop=True).then_inc(s_["u_done"], 1)

                def add_kv(t):
                    pe.wait_ge(s_["v_made"], 2 * b + t // 4 + 1)
                    pe.wait_ge(s_["kf_made"], UT * b + t + 1)
                    if t == 0:
                        need(pe, s_["kv_made"], KC * b)
                    for ch in range(KC):
                        o = (ch % 2) * (DIM + 1)
                        m = pe.matmul(ps_kv[ch // 2][:, o:o + DIM + 1], kf[:, t % 2, ch * P:(ch + 1) * P], v1[:, t, :],
                                      start=(t == 0 and ch % 2 == 0), stop=(t == SEQ_TILES - 1 and ch % 2 == 1), skip_group_check=True)
                    m.then_inc(s_["kv_done"], 1)
                values(0)
                keys(0)
                keys(1)
                for t in range(2, SEQ_TILES):
                    add_kv(t - 2)
                    if t == 4:
                        values(1)
                    keys(t)
                add_kv(SEQ_TILES - 2)
                add_kv(SEQ_TILES - 1)
                for i in range(SEQ_TILES, UT):
                    free_u(b, i)
                    ch, half = i % KC, (i - SEQ_TILES) // KC
                    pe.matmul(ps_u[i % 2][:, :], G[:, 0, ch * P:(ch + 1) * P], ln.zT[:, half * W:(half + 1) * W], start=True, stop=True).then_inc(s_["u_done"], 1)
                for g in range(2):
                    r = 2 * b + g
                    pe.wait_ge(s_["kf_made"], UT * b + SEQ_TILES + KC * (g + 1))
                    pe.wait_ge(s_["kv_made"], KC * (b + 1))
                    need(pe, s_["x2_made"], r)
                    need(pe, s_["v_made"], 2 * b + 2)
                    for t in range(S):
                        for ch in range(KC):
                            lhs = qf[:, ch, (4 * g + t) * P:(4 * g + t + 1) * P]
                            pe.matmul(ps_m[:, t * DIM:(t + 1) * DIM], lhs, kv[:, ch, :], start=(ch == 0), stop=(ch == KC - 1))
                        for ch in range(KC):
                            lhs = qf[:, ch, (4 * g + t) * P:(4 * g + t + 1) * P]
                            m = pe.matmul(ps_v[:, t * H:(t + 1) * H], lhs, ks[:, ch, :], start=(ch == 0), stop=(ch == KC - 1))
                    m.then_inc(s_["attn_done"], 1)
                    pe.wait_ge(s_["at_made"], r + 1)
                    for t in range(S):
                        m = pe.transpose(ps_m[:, t * P:(t + 1) * P], at[:, t * P:(t + 1) * P], ident[:, :])
                    m.then_inc(s_["at_turned"], 1)
                    pe.wait_ge(s_["atT_made"], r + 1)
                    for t in range(S):
                        o = ps_m[:, t * DIM:(t + 1) * DIM]
                        pe.matmul(o, atT[:, t * P:(t + 1) * P], w_outT[:, :], start=True, stop=False)
                        m = pe.matmul(o, ones_row[0:1, :], b_out[0:1, :], start=False, stop=True)
                    m.then_inc(s_["o_done"], 1)
                    pe.wait_ge(s_["x1_made"], r + 1)
                    pe.wait_ge(s_["x1n_made"], r + 1)
                    for t in range(S):
                        m = pe.transpose(ps_m[:, t * P:(t + 1) * P], x1n[:, t, :], ident[:, :])
                    m.then_inc(s_["x1n_turned"], 1)
                    pe.wait_ge(s_["x1T_made"], r + 1)
                    for ch in range(FC):
                        if ch < 2:
                            pe.wait_ge(s_["kf_made"], UT * (b + 1))
                        need(pe, s_["gelu_made"], FC * r + ch - 1)
                        pe.matmul(ps_u[ch % 2][:, :], w1T[:, ch * P:(ch + 1) * P], x1T[:, :], start=True, stop=True).then_inc(s_["up_done"], 1)
                    pe.wait_ge(s_["gelu_made"], FC * (r + 1))
                    for t in range(S):
                        o = ps_m[:, t * DIM:(t + 1) * DIM]
                        for ch in range(FC):
                            pe.matmul(o, hT[:, ch, t * P:(t + 1) * P], w2T[:, ch, :], start=(ch == 0), stop=False)
                        m = pe.matmul(o, ones_row[0:1, :], b2[0:1, :], start=False, stop=True)
                    m.then_inc(s_["down_done"], 1)
            body(0)
            with pe.Fori(1, SEQS) as b:
                body(b)


def local_transformer(nc, sb, sem, bank, ident, x, out, c):
    LAYERS, DIM, FF2 = c["W1"].shape
    FF = FF2 // 2
    INNER = c["Wo"].shape[1]
    HD = c["q_scale"].shape[1]
    H = INNER // HD
    PAIRS = TILES // 2
    SEQS = TILES // SEQ_TILES
    BP = 4
    WIN = 32
    KW = P + WIN
    HALF = DIM // 2
    CH = [(0, 128), (128, 128), (256, FF - 256)]
    NB = LAYERS * PAIRS

    XA = sb("layer_x", [P, TILES, DIM])
    wqkv = sb("wqkv", [P, 3 * INNER])
    wo = sb("wo", [P, INNER // P, DIM])
    w1 = sb("w1", [P, FF2])
    w2 = sb("w2", [P, 3, DIM])
    rope_c = sb("rope_const", [P, 8, 4, HD])
    qk_scales = sb("qk_scales", [P, LAYERS, 4, HD])
    ln_g = sb("ln_g_col", [P, LAYERS])
    ln_b = sb("ln_b_col", [P, LAYERS])
    b1_col = sb("b1_col", [P, LAYERS, 2, 3])
    b2_row = sb("b2_row", [P, LAYERS, DIM])
    mask = sb("mask", [P, 5, KW + 1])
    mask_now = sb("mask_now", [P, KW + 1])
    flag = sb("flag", [P, 4])
    neg_half = sb("neg_half", [P, 32])

    xc = sb("x_now", [P, 2, DIM])
    tab = sb("rope_tab", [P, 2, 4, HD])
    xsT = sb("x_shift_T", [P, 2, P])
    carry_a = sb("carry_attn", [P, 2])
    sq = sb("squares", [P, 4 * 512])
    t1 = sb("qk_roped", [P, 2, 2 * INNER])
    t2 = sb("rope_sin_part", [P, 2 * INNER])
    V = sb("v", [P, 2, INNER])
    v_last = sb("v_last_window", [P, INNER])
    ss = sb("sumsq", [P, 2, 2 * H])
    ssc = sb("sumsq_clamped", [P, 2, 2 * H])
    rn = sb("inv_norm", [P, 2, 2 * H])
    rq8 = sb("q_logit_scale", [P, 2, H])
    qT = sb("qT", [P, 2, H // 2, P])
    kT = sb("kT", [P, 2, H // 2, KW])
    Sm = sb("masked_scores", [P, H, KW])
    mx = sb("row_max", [P, 2, H])
    nb = sb("neg_max", [P, 2, H])
    PR = sb("probs", [P, 2, H, KW])
    den = sb("denoms", [P, 2, H])
    rden = sb("inv_denoms", [P, 2, H])
    PT = sb("probs_T", [P, H, P])
    PTp = sb("probs_T_prev", [P, H, WIN])
    On = sb("attn_out", [P, INNER])
    OT = sb("attn_out_T", [P, INNER // P, P])
    xm = sb("x_mid", [P, 2, DIM])
    xmb = sb("x_mid_plus_b2", [P, 2, DIM])
    xmT = sb("x_mid_shift_T", [P, 2, P])
    carry_m = sb("carry_ffn", [P, 2])
    st = sb("ln_stats", [P, 2, 6])
    mv = sb("ln_mean_var", [P, 2, 2])
    ve = sb("ln_var_eps", [P, 2])
    rstd = sb("ln_rstd", [P, 2])
    z = sb("ln_out", [P, 2, DIM])
    zT = sb("ln_out_T", [P, 2, P])
    gel = sb("gelu_gate", [P, 2, 3, P])
    hT = sb("hidden_T", [P, 2, 3, P])

    psQ, psT, psS, psD = bank[0:2], bank[2:4], bank[4:6], bank[6:8]

    consts_loaded = sem("consts_loaded")
    wqkv_loaded, wo_loaded, w1_loaded, w2_loaded = sem("wqkv_loaded"), sem("wo_loaded"), sem("w1_loaded"), sem("w2_loaded")
    cleared = sem("cleared")
    mask_picked = sem("mask_picked")
    xa_written = sem("xa_written")
    x_copied, tab_made, x_turned, xs_ready, carry_saved = sem("x_copied"), sem("tab_made"), sem("x_turned"), sem("xs_ready"), sem("carry_saved")
    qkv_done, sq_made, v_copied, v_last_saved = sem("qkv_done"), sem("sq_made"), sem("v_copied"), sem("v_last_saved")
    rope_terms, u_made, ss_made, ss_clamped, rn_made, kn_made = (sem(n) for n in ("rope_terms", "u_made", "ss_made", "ss_clamped", "rn_made", "kn_made"))
    qk_turned, qT_copied, kT_copied, kprev_copied = sem("qk_turned"), sem("qT_copied"), sem("kT_copied"), sem("kprev_copied")
    scores_done, sm_made, rq8_made, nb_made, p_made, rden_made = (sem(n) for n in ("scores_done", "sm_made", "rq8_made", "nb_made", "p_made", "rden_made"))
    p_turned, pt_act, pt_dve, av_done, o_normed, o_turned, o_copied, y_done, xm_made = (sem(n) for n in (
        "p_turned", "pt_act", "pt_dve", "av_done", "o_normed", "o_turned", "o_copied", "y_done", "xm_made"))
    xm_turned, xmT_ready, carry_m_saved, xmb_made, xs2_turned = (sem(n) for n in ("xm_turned", "xmT_ready", "carry_m_saved", "xmb_made", "xs2_turned"))
    stats_made, mv_made, ve_made, rstd_made, z_made, z_turned, zT_made = (sem(n) for n in ("stats_made", "mv_made", "ve_made", "rstd_made", "z_made", "z_turned", "zT_made"))
    ff_done, gelu_made, h_made, y2_done = sem("ff_done"), sem("gelu_made"), sem("h_made"), sem("y2_done")
    stored = sem("stored")

    summed = sem("summed")
    ln = TileNorm(sb, sem, "loc_ln", tiles_of(x, 4), 4, ident, None, dest=tiles_of(XA, 4))
    const_dma = [0]

    T_USES = ([[(xs_ready, 3, p, 3), (carry_saved, 1, p, 1)] for p in (0, 1)]
              + [[((qT_copied, 2, p, j + 1) if j < 2 else (kT_copied, 2, p, j - 1))] for p in (0, 1) for j in range(4)]
              + [[u] for p in (0, 1) for u in ((pt_act, 2, p, 1), (pt_dve, 3, p, 1), (pt_act, 2, p, 2), (pt_dve, 3, p, 2),
                                               (pt_dve, 3, p, 3), (o_copied, 2, p, 1), (o_copied, 2, p, 2))])
    Q_USES = ([[(sq_made, 4, p, j + 1), (rope_terms, 4, p, j + 1)] if j < 4 else [(v_copied, 2, p, j - 3)] for p in (0, 1) for j in range(6)]
              + [[u] for p in (0, 1) for u in ((o_normed, 2, p, 1), (o_normed, 2, p, 2), (xm_made, 1, p, 1))])
    S_USES = [[(sm_made, 6, p, g + 1)] for p in (0, 1) for g in range(6)]
    S_GROUPS = [(0, 2, 4), (1, 3, 5), (6, 8, 10), (7, 9, 11), (12, 14), (13, 15)]

    def free_bank(pe, uses, i, n):
        j = i - 2
        m = n if j >= 0 else n - 1
        for s, k, par, cnt in uses[j % len(uses)]:
            need(pe, s, k * (2 * m + par) + cnt)

    with nc.Block() as block:
        @block.sync
        def _(sp):
            def load(dst, src):
                const_dma[0] += 1
                sp.dma_start(dst, src).then_inc(consts_loaded, 16)
            load(rope_c[:, :, :, :], c["rope_const"])
            for k, (name, lo) in enumerate((("q_scale", 0), ("q_scale", 1), ("k_scale", 0), ("k_scale", 1))):
                src = c[name].partition_broadcast(P)
                if lo == 0:
                    load(qk_scales[:, :, k, :], src)
                else:
                    load(qk_scales[:, :, k, 0:HD // 2], src[:, :, HD // 2:HD])
                    load(qk_scales[:, :, k, HD // 2:HD], src[:, :, 0:HD // 2])
            with nc.allow_non_contiguous_dma("small columns"):
                load(ln_g[:, :], c["ln_g"].rearrange("l d -> d l"))
                load(ln_b[:, :], c["ln_b"].rearrange("l d -> d l"))
                for half in range(2):
                    for ch, (lo, w) in enumerate(CH):
                        load(b1_col[0:w, :, half, ch], c["b1"][:, half * FF + lo:half * FF + lo + w].rearrange("l d -> d l"))
            load(b2_row[:, :, :], c["b2"].partition_broadcast(P))
            load(mask[:, :, :], c["mask"])
            load(flag[:, :], c["flag"])

            def load_wqkv(l):
                sp.dma_start(wqkv[:, :], c["Wqkv"][bass.ds(l, 1), :, :].rearrange("a k n -> k (a n)")).then_inc(wqkv_loaded, 16)

            def load_wo(l):
                sp.dma_start(wo[:, :, :], c["Wo"][bass.ds(l, 1), :, :].rearrange("a (k p) n -> p (a k) n", p=P)).then_inc(wo_loaded, 16)

            def load_w12(l):
                sp.dma_start(w1[:, :], c["W1"][bass.ds(l, 1), :, :].rearrange("a k n -> k (a n)")).then_inc(w1_loaded, 16)
                sp.dma_start(w2[:, 0:2, :], c["W2"][bass.ds(l, 1), 0:256, :].rearrange("a (k p) n -> p (a k) n", p=P)).then_inc(w2_loaded, 16)
                sp.dma_start(w2[0:FF - 256, 2, :], c["W2"][bass.ds(l, 1), 256:FF, :].rearrange("a k n -> k (a n)")).then_inc(w2_loaded, 16)

            def save_v_last(n):
                need(sp, v_copied, 4 * n)
                need(sp, av_done, 2 * (2 * n - 1))
                sp.dma_start(v_last[P - WIN:P, :], V[P - WIN:P, 1, :]).then_inc(v_last_saved, 16)

            load_wqkv(0)
            load_wo(0)
            sp.wait_ge(cleared, 1)
            save_v_last(0)
            load_w12(0)
            with sp.Fori(1, PAIRS) as j:
                save_v_last(j)
            with sp.Fori(1, LAYERS) as l:
                sp.wait_ge(qkv_done, 6 * TILES * l)
                load_wqkv(l)
                sp.wait_ge(y_done, TILES * l)
                load_wo(l)
                save_v_last(l * PAIRS)
                sp.wait_ge(ff_done, 2 * TILES * l)
                sp.wait_ge(y2_done, TILES * l)
                load_w12(l)
                with sp.Fori(1, PAIRS) as j:
                    save_v_last(l * PAIRS + j)
            outs = out.rearrange("b (t p) d -> p b t d", p=P)
            for b in range(SEQS):
                sp.wait_ge(summed, b + 1)
                sp.dma_start(outs[:, b, :, :], XA[:, b * SEQ_TILES:(b + 1) * SEQ_TILES, :]).then_inc(stored, 16)
            sp.wait_ge(stored, 16 * SEQS)

        @block.gpsimd
        def _(pool):
            ln.on_pool_start(pool)
            with pool.Fori(0, TILES // 4) as n:
                ln.on_pool(pool, n)
            pool.memset(V[:, 1, :], 0.0)
            pool.memset(kT[:, 1, :, P - WIN:P], 0.0)
            pool.memset(carry_a[:, :], 0.0)
            pool.memset(carry_m[:, :], 0.0)
            pool.memset(neg_half[:, :], -0.5).then_inc(cleared, 1)
            pool.wait_ge(cleared, 1)
            pool.wait_ge(consts_loaded, 16 * const_dma[0])

            def fetch(n, par):
                T = 2 * n + par
                t = (n % PAIRS) * 2 + par
                need(pool, xa_written, T + 1)
                need(pool, x_turned, T - 1)
                apart(pool)
                pool.tensor_copy(xc[:, par, :], XA[:, bass.ds(t, 1), :]).then_inc(x_copied, 1)
                need(pool, rope_terms, 4 * (T - 1))
                apart(pool)
                pool.tensor_tensor(tab[:, par, :, :], rope_c[:, bass.ds((n % BP) * 2 + par, 1), :, :].rearrange("p a k d -> p (a k) d"),
                                   qk_scales[:, bass.ds(n // PAIRS, 1), :, :].rearrange("p a k d -> p (a k) d"), ALU.mult).then_inc(tab_made, 1)

            def pick_mask(n):
                need(pool, sm_made, 6 * (2 * n - 1))
                apart(pool)
                pool.tensor_copy(mask_now[:, :], mask[:, bass.ds(n % BP, 1), :].rearrange("p a k -> p (a k)")).then_inc(mask_picked, 1)

            def rope_sum(n, par):
                T = 2 * n + par
                for j in range(2):
                    pool.wait_ge(rope_terms, 4 * T + 2 * j + 2)
                    part = slice(j * INNER, (j + 1) * INNER)
                    pool.tensor_tensor(t1[:, par, part], t1[:, par, part], t2[:, part], ALU.add).then_inc(u_made, 1)

            def norms(n, par):
                T = 2 * n + par
                pool.wait_ge(ss_made, T + 1)
                apart(pool)
                pool.tensor_scalar(ssc[:, par, :], ss[:, par, :], 1e-24, None, ALU.max).then_inc(ss_clamped, 1)
                pool.wait_ge(ss_clamped, T + 1)
                need(pool, kn_made, T - 1)
                pool.tensor_tensor(rn[:, par, :], ssc[:, par, :], neg_half[:, :], ALU.pow).then_inc(rn_made, 1)

            def k_prev(n, par):
                T = 2 * n + par
                need(pool, kT_copied, 2 * T)
                need(pool, scores_done, 6 * (T - 1))
                apart(pool)
                if par == 0:
                    pool.wait_ge(mask_picked, n + 1)
                    apart(pool)
                    pool.tensor_scalar(kT[:, par, :, P:KW], kT[:, 1, :, P - WIN:P], mask_now[:, KW:KW + 1], None, ALU.mult).then_inc(kprev_copied, 1)
                else:
                    pool.tensor_copy(kT[:, par, :, P:KW], kT[:, 0, :, P - WIN:P]).then_inc(kprev_copied, 1)

            def add_b2(n, par):
                U = 2 * n + par
                pool.wait_ge(xm_made, U + 1)
                need(pool, xa_written, TILES + U - 1)
                apart(pool)
                pool.tensor_tensor(xmb[:, par, :], xm[:, par, :], b2_row[:, bass.ds(n // PAIRS, 1), :].rearrange("p a d -> p (a d)"),
                                   ALU.add).then_inc(xmb_made, 1)

            def ln_rstd(n, par):
                U = 2 * n + par
                pool.wait_ge(mv_made, U + 1)
                apart(pool)
                pool.tensor_scalar(ve[:, par:par + 1], mv[:, par, 1:2], 1e-5, None, ALU.add).then_inc(ve_made, 1)
                pool.wait_ge(ve_made, U + 1)
                need(pool, z_made, U - 1)
                pool.tensor_tensor(rstd[:, par:par + 1], ve[:, par:par + 1], neg_half[:, 0:1], ALU.pow).then_inc(rstd_made, 1)

            def body(n, ffn=True):
                fetch(n, 0)
                if ffn:
                    add_b2(n - 1, 0)
                    add_b2(n - 1, 1)
                rope_sum(n, 0)
                norms(n, 0)
                fetch(n, 1)
                if ffn:
                    ln_rstd(n - 1, 0)
                rope_sum(n, 1)
                if ffn:
                    ln_rstd(n - 1, 1)
                norms(n, 1)
                pick_mask(n)
                k_prev(n, 0)
                k_prev(n, 1)

            body(0, ffn=False)
            body(1)
            with pool.Fori(2, NB) as n:
                body(n)
            add_b2(NB - 1, 0)
            add_b2(NB - 1, 1)
            ln_rstd(NB - 1, 0)
            ln_rstd(NB - 1, 1)

        @block.scalar
        def _(act):
            act.wait_ge(cleared, 1)
            act.wait_ge(consts_loaded, 16 * const_dma[0])

            def shift(n, par, T, ps, dst, carry, ready, saved):
                act.activation(dst[0:HALF, par, :], ps[0:HALF, 0:P], ACT.Copy).then_inc(ready, 1)
                act.activation(dst[HALF:P, par, 1:P], ps[HALF:P, 0:P - 1], ACT.Copy).then_inc(ready, 1)
                need(act, saved, T)
                if par == 0:
                    apart(act)
                    act.activation(dst[HALF:P, par, 0:1], carry[HALF:P, 1:2], ACT.Copy, scale=flag[HALF:P, bass.ds(n % BP, 1)]).then_inc(ready, 1)
                else:
                    act.activation(dst[HALF:P, par, 0:1], carry[HALF:P, 0:1], ACT.Copy).then_inc(ready, 1)
                need(act, ready, 3 * T)
                act.activation(carry[HALF:P, par:par + 1], ps[HALF:P, P - 1:P], ACT.Copy).then_inc(saved, 1)

            def attn_in(n, par):
                T = 2 * n + par
                act.wait_ge(x_turned, T + 1)
                need(act, qkv_done, 6 * (T - 1))
                shift(n, par, T, psT[par], xsT, carry_a, xs_ready, carry_saved)

            def squares(n, par):
                T = 2 * n + par
                need(act, ss_made, T)
                for j in range(4):
                    act.wait_ge(qkv_done, 6 * T + j + 1)
                    act.activation(sq[:, j * 512:(j + 1) * 512], psQ[j % 2][:, :], ACT.Square).then_inc(sq_made, 1)
                need(act, av_done, 2 * (T - 1))
                if par == 1:
                    act.wait_ge(v_last_saved, 16 * (n + 1))
                for j in range(2):
                    act.wait_ge(qkv_done, 6 * T + j + 5)
                    act.activation(V[:, par, j * 512:(j + 1) * 512], psQ[j % 2][:, :], ACT.Copy).then_inc(v_copied, 1)

            def evac_q(n, par):
                T = 2 * n + par
                need(act, scores_done, 6 * (T - 1))
                for j in range(2):
                    act.wait_ge(qk_turned, 4 * T + j + 1)
                    act.activation(qT[:, par, 4 * j:4 * j + 4, :], psT[j % 2].rearrange("p (a b) -> p a b", b=P), ACT.Copy).then_inc(qT_copied, 1)

            def exps(n, par):
                T = 2 * n + par
                act.wait_ge(nb_made, T + 1)
                need(act, p_turned, 5 * (T - 1))
                need(act, rden_made, T - 1)
                for h in range(H):
                    e = act.activation(PR[:, par, h, :], Sm[:, h, :], ACT.Exp, bias=nb[:, par, h:h + 1],
                                       scale=rq8[:, par, h:h + 1], accum_out=den[:, par, h:h + 1])
                    if h % 4 == 3:
                        e.then_inc(p_made, 1)

            def evac_p(n, par):
                T = 2 * n + par
                need(act, av_done, 2 * T)
                for q in (0, 2):
                    act.wait_ge(p_turned, 5 * T + q + 1)
                    act.activation(PT[:, 4 * q:4 * q + 4, :], psT[(q + par) % 2].rearrange("p (a b) -> p a b", b=P), ACT.Copy).then_inc(pt_act, 1)

            def evac_o(n, par):
                T = 2 * n + par
                need(act, y_done, T)
                for j in range(2):
                    act.wait_ge(o_turned, 2 * T + j + 1)
                    act.activation(OT[:, 4 * j:4 * j + 4, :], psT[(1 + j + par) % 2].rearrange("p (a b) -> p a b", b=P), ACT.Copy).then_inc(o_copied, 1)

            def ffn_in(n, par):
                U = 2 * n + par
                act.wait_ge(xm_turned, U + 1)
                need(act, xs2_turned, U - 1)
                shift(n, par, U, psD[par], xmT, carry_m, xmT_ready, carry_m_saved)

            def evac_z(n, par):
                U = 2 * n + par
                act.wait_ge(z_turned, U + 1)
                need(act, ff_done, 2 * (U - 1))
                apart(act)
                act.activation(zT[:, par, :], psD[par][:, 2 * P:3 * P], ACT.Identity, scale=ln_g[:, bass.ds(n // PAIRS, 1)],
                               bias=ln_b[:, bass.ds(n // PAIRS, 1)]).then_inc(zT_made, 1)

            def gelu(n, par):
                U = 2 * n + par
                need(act, h_made, 3 * (U - 1))
                for ch, (lo, w) in enumerate(CH):
                    act.wait_ge(ff_done, 2 * U + (1 if ch < 2 else 2))
                    apart(act)
                    o = (ch % 2) * 2 * P + P
                    act.activation(gel[0:w, par, ch, :], psD[par][0:w, o:o + P], ACT.Gelu,
                                   bias=b1_col[0:w, bass.ds(n // PAIRS, 1), 1, ch]).then_inc(gelu_made, 1)

            def body(n, ffn=True):
                attn_in(n, 0)
                if ffn:
                    ffn_in(n - 1, 0)
                    ffn_in(n - 1, 1)
                squares(n, 0)
                attn_in(n, 1)
                squares(n, 1)
                evac_q(n, 0)
                if ffn:
                    evac_z(n - 1, 0)
                    evac_z(n - 1, 1)
                evac_q(n, 1)
                exps(n, 0)
                exps(n, 1)
                evac_p(n, 0)
                if ffn:
                    gelu(n - 1, 0)
                    gelu(n - 1, 1)
                evac_o(n, 0)
                evac_p(n, 1)
                evac_o(n, 1)

            body(0, ffn=False)
            body(1)
            with act.Fori(2, NB) as n:
                body(n)
            for stage in (ffn_in, evac_z, gelu):
                stage(NB - 1, 0)
                stage(NB - 1, 1)

        @block.vector
        def _(dve):
            with dve.Fori(0, TILES // 4) as n:
                ln.on_dve(dve, n, lambda e, n: None)
            dve.wait_ge(ln.z_made, TILES)
            dve.sem_inc(xa_written, TILES)
            dve.wait_ge(cleared, 1)
            dve.wait_ge(consts_loaded, 16 * const_dma[0])

            def rope(n, par):
                T = 2 * n + par
                dve.wait_ge(tab_made, T + 1)
                need(dve, u_made, 2 * T)
                need(dve, qk_turned, 4 * (T - 1))
                for j in range(4):
                    k = 2 * (j // 2)
                    dve.wait_ge(sq_made, 4 * T + j + 1)
                    src = psQ[j % 2].rearrange("p (h d) -> p h d", d=HD)
                    o1 = t1[:, par, j * 512:(j + 1) * 512].rearrange("p (h d) -> p h d", d=HD)
                    o2 = t2[:, j * 512:(j + 1) * 512].rearrange("p (h d) -> p h d", d=HD)
                    HH = HD // 2
                    dve.tensor_tensor(o1, src, tab[:, par, k, :].unsqueeze(1).to_broadcast([P, 8, HD]), ALU.mult)
                    dve.tensor_tensor(o2[:, :, 0:HH], src[:, :, HH:HD], tab[:, par, k + 1, 0:HH].unsqueeze(1).to_broadcast([P, 8, HH]), ALU.mult)
                    dve.tensor_tensor(o2[:, :, HH:HD], src[:, :, 0:HH], tab[:, par, k + 1, HH:HD].unsqueeze(1).to_broadcast([P, 8, HH]),
                                      ALU.mult).then_inc(rope_terms, 1)

            def sumsq(n, par):
                T = 2 * n + par
                dve.wait_ge(sq_made, 4 * T + 4)
                need(dve, ss_clamped, T - 1)
                dve.tensor_reduce(ss[:, par, :], sq[:, :].rearrange("p (h d) -> p h d", d=HD), AX.X, ALU.add).then_inc(ss_made, 1)

            def k_norm(n, par):
                T = 2 * n + par
                dve.wait_ge(rn_made, T + 1)
                need(dve, nb_made, T - 1)
                need(dve, p_made, 4 * (T - 1))
                dve.tensor_scalar(rq8[:, par, :], rn[:, par, 0:H], 8.0, None, ALU.mult).then_inc(rq8_made, 1)
                dve.wait_ge(u_made, 2 * T + 2)
                dve.tensor_tensor(t1[:, par, INNER:2 * INNER].rearrange("p (h d) -> p h d", d=HD), t1[:, par, INNER:2 * INNER].rearrange("p (h d) -> p h d", d=HD),
                                  rn[:, par, H:2 * H].unsqueeze(2).to_broadcast([P, H, HD]), ALU.mult).then_inc(kn_made, 1)

            def evac_k(n, par):
                T = 2 * n + par
                need(dve, kprev_copied, T)
                for j in range(2):
                    dve.wait_ge(qk_turned, 4 * T + j + 3)
                    dve.tensor_copy(kT[:, par, 4 * j:4 * j + 4, 0:P], psT[j % 2].rearrange("p (a b) -> p a b", b=P)).then_inc(kT_copied, 1)

            def masked(n, par):
                T = 2 * n + par
                need(dve, p_made, 4 * T)
                dve.wait_ge(mask_picked, n + 1)
                m = mask_now[:, 0:KW] if par == 0 else mask[:, 4, 0:KW]
                for g, heads in enumerate(S_GROUPS):
                    dve.wait_ge(scores_done, 6 * T + g + 1)
                    apart(dve)
                    for i, h in enumerate(heads):
                        e = dve.tensor_tensor_reduce(out=Sm[:, h, :], in0=psS[g % 2][:, i * KW:(i + 1) * KW], in1=m, scale=1.0, scalar=-3e38,
                                                     op0=ALU.add, op1=ALU.max, accum_out=mx[:, par, h:h + 1])
                    e.then_inc(sm_made, 1)
                dve.wait_ge(sm_made, 6 * T + 6)
                dve.wait_ge(rq8_made, T + 1)
                dve.scalar_tensor_tensor(nb[:, par, :], mx[:, par, :], -1.0, rq8[:, par, :], ALU.mult, ALU.mult).then_inc(nb_made, 1)

            def evac_p(n, par):
                T = 2 * n + par
                need(dve, av_done, 2 * T)
                for q in (1, 3):
                    dve.wait_ge(p_turned, 5 * T + q + 1)
                    dve.tensor_copy(PT[:, 4 * q:4 * q + 4, :], psT[(q + par) % 2].rearrange("p (a b) -> p a b", b=P)).then_inc(pt_dve, 1)
                dve.wait_ge(p_turned, 5 * T + 5)
                dve.tensor_copy(PTp[P - WIN:P, :, :], psT[par][P - WIN:P, :].rearrange("p (a b) -> p a b", b=WIN)).then_inc(pt_dve, 1)
                dve.wait_ge(p_made, 4 * T + 4)
                dve.reciprocal(rden[:, par, :], den[:, par, :]).then_inc(rden_made, 1)

            def normalise(n, par):
                T = 2 * n + par
                dve.wait_ge(rden_made, T + 1)
                for j in range(2):
                    dve.wait_ge(av_done, 2 * T + j + 1)
                    need(dve, o_turned, 2 * (T - 1) + j + 1)
                    dve.tensor_tensor(On[:, j * 512:(j + 1) * 512].rearrange("p (h d) -> p h d", d=HD),
                                      psQ[(par * 3 + j) % 2].rearrange("p (h d) -> p h d", d=HD),
                                      rden[:, par, 8 * j:8 * j + 8].unsqueeze(2).to_broadcast([P, 8, HD]), ALU.mult).then_inc(o_normed, 1)

            def residual(n, par):
                T = 2 * n + par
                dve.wait_ge(y_done, T + 1)
                need(dve, xm_turned, T - 1)
                need(dve, xmb_made, T - 1)
                dve.tensor_tensor(xm[:, par, :], psQ[(par * 3 + 2) % 2][:, 0:DIM], XA[:, bass.ds((n % PAIRS) * 2 + par, 1), :].rearrange("p a d -> p (a d)"),
                                  ALU.add).then_inc(xm_made, 1)

            def ln_stats(n, par):
                U = 2 * n + par
                dve.wait_ge(xs2_turned, U + 1)
                dve.bn_stats(st[:, par, :], psD[par][:, P:2 * P]).then_inc(stats_made, 1)
                dve.wait_ge(stats_made, U + 1)
                need(dve, ve_made, U - 1)
                apart(dve)
                dve.bn_aggr(mv[:, par, :], st[:, par, :]).then_inc(mv_made, 1)

            def ln_apply(n, par):
                U = 2 * n + par
                dve.wait_ge(rstd_made, U + 1)
                need(dve, z_turned, U - 1)
                dve.tensor_scalar(z[:, par, :], psD[par][:, P:2 * P], mv[:, par, 0:1], rstd[:, par:par + 1], ALU.subtract, ALU.mult).then_inc(z_made, 1)

            def gate(n, par):
                U = 2 * n + par
                need(dve, y2_done, U - 1)
                for ch, (lo, w) in enumerate(CH):
                    o = (ch % 2) * 2 * P
                    dve.wait_ge(gelu_made, 3 * U + (2 if ch < 2 else 3))
                    dve.scalar_tensor_tensor(hT[0:w, par, ch, :], psD[par][0:w, o:o + P], b1_col[0:w, bass.ds(n // PAIRS, 1), 0, ch],
                                             gel[0:w, par, ch, :], ALU.add, ALU.mult).then_inc(h_made, 1)

            def ffn_out(n, par):
                U = 2 * n + par
                dve.wait_ge(y2_done, U + 1)
                dve.wait_ge(xmb_made, U + 1)
                dve.tensor_tensor(XA[:, bass.ds((n % PAIRS) * 2 + par, 1), :].rearrange("p a d -> p (a d)"), psD[par][:, 2 * P:3 * P], xmb[:, par, :],
                                  ALU.add).then_inc(xa_written, 1)

            def body(n, ffn=True):
                rope(n, 0)
                sumsq(n, 0)
                if ffn:
                    ln_stats(n - 1, 0)
                rope(n, 1)
                if ffn:
                    ln_stats(n - 1, 1)
                    ln_apply(n - 1, 0)
                sumsq(n, 1)
                k_norm(n, 0)
                if ffn:
                    ln_apply(n - 1, 1)
                evac_k(n, 0)
                k_norm(n, 1)
                evac_k(n, 1)
                masked(n, 0)
                masked(n, 1)
                evac_p(n, 0)
                if ffn:
                    gate(n - 1, 0)
                normalise(n, 0)
                if ffn:
                    gate(n - 1, 1)
                residual(n, 0)
                evac_p(n, 1)
                normalise(n, 1)
                if ffn:
                    ffn_out(n - 1, 0)
                    ffn_out(n - 1, 1)
                residual(n, 1)

            body(0, ffn=False)
            body(1)
            with dve.Fori(2, NB) as n:
                body(n)
            for stage in (ln_stats, ln_apply, gate, ffn_out):
                stage(NB - 1, 0)
                stage(NB - 1, 1)
            dve.wait_ge(xa_written, TILES + 2 * NB)
            for b in range(SEQS):
                part = slice(b * SEQ_TILES, (b + 1) * SEQ_TILES)
                dve.tensor_tensor(XA[:, part, :], XA[:, part, :], x[:, part, :], ALU.add).then_inc(summed, 1)

        @block.tensor
        def _(pe):
            pe.wait_ge(cleared, 1)
            pe.wait_ge(consts_loaded, 16 * const_dma[0])

            def turn_x(n, par):
                T = 2 * n + par
                pe.wait_ge(x_copied, T + 1)
                free_bank(pe, T_USES, par, n)
                pe.transpose(psT[par][:, 0:P], xc[:, par, :], ident[:, :]).then_inc(x_turned, 1)

            def qkv(n, par):
                T = 2 * n + par
                pe.wait_ge(xs_ready, 3 * T + 3)
                pe.wait_ge(wqkv_loaded, 16 * (n // PAIRS + 1))
                for j in range(6):
                    free_bank(pe, Q_USES, 6 * par + j, n)
                    pe.matmul(psQ[j % 2][:, :], xsT[:, par, :], wqkv[:, j * 512:(j + 1) * 512], start=True, stop=True).then_inc(qkv_done, 1)

            def turn_qk(n, par):
                T = 2 * n + par
                for j in range(4):
                    if j == 0:
                        pe.wait_ge(u_made, 2 * T + 1)
                    if j == 2:
                        pe.wait_ge(kn_made, T + 1)
                    free_bank(pe, T_USES, 2 + 4 * par + j, n)
                    for i in range(4):
                        col = (4 * (j % 2) + i) * P
                        src = t1[:, par, (j // 2) * INNER + col:(j // 2) * INNER + col + P]
                        e = pe.transpose(psT[j % 2][:, i * P:(i + 1) * P], src, ident[:, :])
                    e.then_inc(qk_turned, 1)

            def scores(n, par):
                T = 2 * n + par
                pe.wait_ge(qT_copied, 2 * T + 2)
                pe.wait_ge(kT_copied, 2 * T + 2)
                pe.wait_ge(kprev_copied, T + 1)
                for g, heads in enumerate(S_GROUPS):
                    free_bank(pe, S_USES, 6 * par + g, n)
                    for i, h in enumerate(heads):
                        r = slice(HD * (h % 2), HD * (h % 2) + HD)
                        e = pe.matmul(psS[g % 2][:, i * KW:(i + 1) * KW], qT[r, par, h // 2, :], kT[r, par, h // 2, :], start=True, stop=True)
                    e.then_inc(scores_done, 1)

            def turn_p(n, par):
                T = 2 * n + par
                u = 10 + 7 * par
                for q in range(4):
                    pe.wait_ge(p_made, 4 * T + q + 1)
                    free_bank(pe, T_USES, u + q, n)
                    for i in range(4):
                        e = pe.transpose(psT[(u + q) % 2][:, i * P:(i + 1) * P], PR[:, par, 4 * q + i, 0:P], ident[:, :])
                    e.then_inc(p_turned, 1)
                free_bank(pe, T_USES, u + 4, n)
                apart(pe)
                for h in range(H):
                    e = pe.transpose(psT[(u + 4) % 2][:, h * WIN:(h + 1) * WIN], PR[0:WIN, par, h, WIN:KW], ident[0:WIN, 0:WIN])
                e.then_inc(p_turned, 1)

            def attend(n, par):
                T = 2 * n + par
                pe.wait_ge(v_copied, 2 * T + 2)
                pe.wait_ge(v_last_saved, 16 * (n + 1))
                pe.wait_ge(pt_dve, 3 * T + 3)
                pe.wait_ge(pt_act, 2 * T + 2)
                for j in range(2):
                    free_bank(pe, Q_USES, 12 + 3 * par + j, n)
                    ps = psQ[(3 * par + j) % 2]
                    for i in range(8):
                        h = 8 * j + i
                        hd = slice(h * HD, (h + 1) * HD)
                        pe.matmul(ps[:, i * HD:(i + 1) * HD], PT[:, h, :], V[:, par, hd], start=True, stop=True)
                        vp = v_last[P - WIN:P, hd] if par == 0 else V[P - WIN:P, 0, hd]
                        e = pe.matmul(ps[0:WIN, i * HD:(i + 1) * HD], PTp[P - WIN:P, h, :], vp, start=False, stop=True, skip_group_check=True)
                    e.then_inc(av_done, 1)

            def project(n, par):
                T = 2 * n + par
                u = 15 + 7 * par
                for j in range(2):
                    pe.wait_ge(o_normed, 2 * T + j + 1)
                    free_bank(pe, T_USES, u + j, n)
                    for i in range(4):
                        col = (4 * j + i) * P
                        e = pe.transpose(psT[(u + j) % 2][:, i * P:(i + 1) * P], On[:, col:col + P], ident[:, :])
                    e.then_inc(o_turned, 1)
                pe.wait_ge(wo_loaded, 16 * (n // PAIRS + 1))
                free_bank(pe, Q_USES, 14 + 3 * par, n)
                for k in range(INNER // P):
                    pe.wait_ge(o_copied, 2 * T + k // 4 + 1)
                    e = pe.matmul(psQ[(3 * par + 2) % 2][:, 0:DIM], OT[:, k, :], wo[:, k, :], start=(k == 0), stop=(k == INNER // P - 1))
                e.then_inc(y_done, 1)

            def turn_xm(n, par):
                U = 2 * n + par
                pe.wait_ge(xm_made, U + 1)
                need(pe, xa_written, TILES + U - 1)
                pe.transpose(psD[par][:, 0:P], xm[:, par, :], ident[:, :]).then_inc(xm_turned, 1)

            def turn_back(n, par):
                U = 2 * n + par
                pe.wait_ge(xmT_ready, 3 * U + 3)
                pe.wait_ge(carry_m_saved, U + 1)
                pe.transpose(psD[par][:, P:2 * P], xmT[:, par, :], ident[:, :]).then_inc(xs2_turned, 1)

            def turn_z(n, par):
                U = 2 * n + par
                pe.wait_ge(z_made, U + 1)
                pe.transpose(psD[par][:, 2 * P:3 * P], z[:, par, :], ident[:, :]).then_inc(z_turned, 1)

            def ffn_up(n, par):
                U = 2 * n + par
                pe.wait_ge(zT_made, U + 1)
                pe.wait_ge(w1_loaded, 16 * (n // PAIRS + 1))
                for ch, (lo, w) in enumerate(CH):
                    if ch == 2:
                        pe.wait_ge(h_made, 3 * U + 2)
                    for half in (0, 1):
                        o = (ch % 2) * 2 * P + half * P
                        e = pe.matmul(psD[par][0:w, o:o + P], w1[:, half * FF + lo:half * FF + lo + w], zT[:, par, :], start=True, stop=True)
                    if ch >= 1:
                        e.then_inc(ff_done, 1)

            def ffn_down(n, par):
                U = 2 * n + par
                pe.wait_ge(w2_loaded, 32 * (n // PAIRS + 1))
                pe.wait_ge(h_made, 3 * U + 3)
                for ch, (lo, w) in enumerate(CH):
                    e = pe.matmul(psD[par][:, 2 * P:3 * P], hT[0:w, par, ch, :], w2[0:w, ch, :], start=(ch == 0), stop=(ch == 2))
                e.then_inc(y2_done, 1)

            def body(n, ffn=True):
                turn_x(n, 0)
                if ffn:
                    turn_xm(n - 1, 0)
                    turn_xm(n - 1, 1)
                qkv(n, 0)
                turn_x(n, 1)
                if ffn:
                    turn_back(n - 1, 0)
                    turn_back(n - 1, 1)
                qkv(n, 1)
                turn_qk(n, 0)
                if ffn:
                    turn_z(n - 1, 0)
                    turn_z(n - 1, 1)
                turn_qk(n, 1)
                scores(n, 0)
                scores(n, 1)
                turn_p(n, 0)
                if ffn:
                    ffn_up(n - 1, 0)
                attend(n, 0)
                if ffn:
                    ffn_up(n - 1, 1)
                project(n, 0)
                turn_p(n, 1)
                attend(n, 1)
                if ffn:
                    ffn_down(n - 1, 0)
                    ffn_down(n - 1, 1)
                project(n, 1)

            body(0, ffn=False)
            body(1)
            with pe.Fori(2, NB) as n:
                body(n)
            for stage in (turn_xm, turn_back, turn_z, ffn_up, ffn_down):
                stage(NB - 1, 0)
                stage(NB - 1, 1)


def retention_constants(T=1024, E=128, H=8, V=256, C=128):
    import numpy as np
    f = np.float32
    vec = ((np.arange(0, E, 2, dtype=f) + f(0.4 * E)) / f(1.4 * E)).astype(f)
    pos = np.arange(T, dtype=f)
    scale = (vec[None, :] ** (pos[:, None] / f(512.0))).astype(f)
    inv_freq = (f(1.0) / f(10000.0) ** (np.arange(E // 2, dtype=f) / f(E // 2))).astype(f)
    angle = (pos[:, None] * inv_freq[None, :]).astype(f)
    sin, cos = np.sin(angle).astype(f), np.cos(angle).astype(f)
    gamma = (f(1.0) - np.exp(np.linspace(np.log(1.0 / 32.0), np.log(1.0 / 512.0), H).astype(f))).astype(f)
    log_decay = np.log(gamma).astype(f).astype(np.float64)
    local = np.arange(T) % C
    row = np.sqrt(np.cumsum(np.exp(log_decay[None, :] * np.arange(T)[:, None]), 0))
    head = np.arange(E) // (E // H)
    fq = (np.exp(log_decay[None, :] * local[:, None]) / row * (E // H) ** -0.5)[:, head]
    fk = np.exp(-log_decay[None, :] * local[:, None])[:, head]
    two = lambda a: np.repeat(a.astype(np.float64), 2, axis=-1)
    sign = np.tile([-1.0, 1.0], E // 2)
    cq, sq_ = two(cos * scale) * fq, two(sin * scale) * sign * fq
    ck, sk = two(cos * (f(1.0) / scale)) * fk, two(sin * (f(1.0) / scale)) * sign * fk
    tile = lambda a: np.ascontiguousarray(a.reshape(T // C, C, 2 * E).transpose(1, 0, 2)).astype(f)
    p = np.arange(E)
    over = np.exp(log_decay * C)[head]
    return {"ret_cos": tile(np.concatenate([cq, ck], 1)), "ret_sin": tile(np.concatenate([sq_, sk], 1)),
            "ret_tri": (p[:, None] <= p[None, :]).astype(f), "ret_head_of": (head[:, None] == np.arange(H)[None, :]).astype(f),
            "ret_state_mask": ((head[:, None] == np.arange(V)[None, :] // (V // H)) * over[:, None]).astype(f),
            "ret_decay": over[:, None].astype(f)}


def linear_constants():
    import numpy as np
    f = np.float32
    p, ch = np.arange(128)[:, None, None], np.arange(4)[None, :, None]
    head = 4 * ch + p // 32
    return {"kv_mask": (head == np.arange(128)[None, None, :] // 8).astype(f), "ks_mask": (head == np.arange(16)[None, None, :]).astype(f)}


def local_constants(HD=64, n=1024, W=32, C=128):
    import numpy as np
    f = np.float32
    half = np.arange(0, HD, 2, dtype=f)
    inv_freq = (f(1.0) / f(10000.0) ** (half / f(HD))).astype(f)
    t = np.arange(n, dtype=f)
    freqs = (t[:, None] * inv_freq[None, :]).astype(f)
    freqs = np.concatenate([freqs, freqs], -1)
    base = ((half + f(0.4 * HD)) / f(1.4 * HD)).astype(f)
    power = ((t - n // 2) / f(W // 2)).astype(f)
    scale = (base[None, :] ** power[:, None]).astype(f)
    scale = np.concatenate([scale, scale], -1)
    sign = np.concatenate([-np.ones(HD // 2, f), np.ones(HD // 2, f)])
    inv = (f(1.0) / scale).astype(f)
    cos, sin = np.cos(freqs).astype(f), np.sin(freqs).astype(f)
    rope = np.stack([cos * scale, sin * scale * sign, cos * inv, sin * inv * sign], 1).astype(f)
    i, j = np.arange(C)[:, None], np.arange(C)[None, :]
    own = ((i // W == j // W) & (i >= j)) | ((i // W == j // W + 1) & (i <= j + W))
    prev = (i < W) & (i <= np.arange(W)[None, :])
    mask = np.full((C, 5, C + W + 1), -1e30, f)
    for k in range(5):
        mask[:, k, 0:C][own] = 0.0
        mask[:, k, C + W] = float(k > 0)
        if k:
            mask[:, k, C:C + W][prev] = 0.0
    flag = np.ones((C, 4), f)
    flag[:, 0] = 0.0
    return {"rope_const": rope.reshape(n // C, C, 4, HD).transpose(1, 0, 2, 3), "mask": mask, "flag": flag}


def program(nc, d, out):
    outer = ExitStack()
    with outer:
        def sem(name):
            return outer.enter_context(nc.semaphore(name))

        def keep(name, shape, dt=F32):
            return outer.enter_context(nc.sbuf_tensor(name, shape, dt))

        def part(prefix):
            return {k[len(prefix):]: v for k, v in d.items() if k.startswith(prefix)}

        bank = [outer.enter_context(nc.psum_tensor(f"bank{i}", [P, 512], F32))[:, :] for i in range(8)]
        ident = keep("identity", [P, P])
        ones_row = keep("ones_row", [1, P])
        x = keep("x", [P, TILES, DIM])
        loaded = sem("x_loaded")
        with nc.Block() as block:
            @block.sync
            def _(sp):
                sp.dma_start(ident[:, :], d["identity"]).then_inc(loaded, 16)
                sp.dma_start(x[:, :, :], d["hidden_states"].rearrange("b (t p) d -> p (b t) d", p=P)).then_inc(loaded, 16)
                sp.wait_ge(loaded, 32)

            @block.vector
            def _(dve):
                dve.memset(ones_row[:, :], 1.0)

        def phase(run):
            sems = []

            def signal(name):
                sems.append(nc.alloc_semaphore(name))
                return sems[-1]

            with ExitStack() as stack:
                run(lambda name, shape, dt=F32: stack.enter_context(nc.sbuf_tensor(name, shape, dt)), signal)
            nc.clear_and_free_semaphores(sems)
            nc.all_engine_barrier()

        phase(lambda sb, sem: retention_block(nc, sb, sem, bank, ident, ones_row, x, part("L0_attn_")))
        phase(lambda sb, sem: mixture(nc, sb, sem, bank, ident, ones_row, x, part("L0_ffn_")))
        phase(lambda sb, sem: linear_block(nc, sb, sem, bank, ident, ones_row, x, part("L1_attn_")))
        phase(lambda sb, sem: local_transformer(nc, sb, sem, bank, ident, x, out, part("L1_ffn_")))


_INS = ["L0_attn_w_qkv", "L0_attn_b_qkv", "L0_attn_w_g", "L0_attn_b_g", "L0_attn_w_p", "L0_attn_b_p",
        "L0_ffn_Wr", "L0_ffn_br", "L0_ffn_W1", "L0_ffn_b1", "L0_ffn_W2", "L0_ffn_b2",
        "L1_attn_proj", "L1_attn_w_qkv", "L1_attn_b_out", "L1_attn_gamma", "L1_attn_beta", "L1_attn_b1", "L1_attn_b2",
        "L1_ffn_Wqkv", "L1_ffn_q_scale", "L1_ffn_k_scale", "L1_ffn_Wo", "L1_ffn_ln_g", "L1_ffn_ln_b",
        "L1_ffn_W1", "L1_ffn_b1", "L1_ffn_W2", "L1_ffn_b2"]


def kernel(**inputs):
    import numpy as np
    import concourse.bacc as bacc
    from concourse.bass_utils import run_bass_kernel_spmd as run
    nc = bacc.Bacc("TRN2", target_bir_lowering=False, num_devices=1)
    arrays = {"hidden_states": inputs["L0_attn_hidden_states"], "identity": np.eye(P, dtype=np.float32)}
    for name in _INS:
        arrays[name] = inputs[name]
    w_qkv = inputs["L1_attn_w_qkv"]
    arrays.update(L1_attn_wvT=w_qkv[2 * DIM:].T, L1_attn_w_outT=inputs["L1_attn_w_out"].T,
                  L1_attn_w1T=inputs["L1_attn_w1"].T, L1_attn_w2T=inputs["L1_attn_w2"].T)
    arrays["L0_ffn_rank"] = np.broadcast_to(8.0 - np.arange(8, dtype=np.float32), (P, 4, 8))
    for prefix, consts in (("L0_attn_", retention_constants()), ("L1_attn_", linear_constants()), ("L1_ffn_", local_constants())):
        arrays.update({prefix + k: v for k, v in consts.items()})
    arrays = {"in_" + k: np.ascontiguousarray(v) for k, v in arrays.items()}
    d = {k[3:]: nc.dram_tensor(k, v.shape, F32, kind="ExternalInput").ap() for k, v in arrays.items()}
    out = nc.dram_tensor("out", (4, 1024, 128), F32, kind="ExternalOutput").ap()
    program(nc, d, out)
    return run(nc, [arrays], core_ids=[0]).results[0]["out"]
```

```python
import concourse.bass as bass
from concourse import mybir
from contextlib import ExitStack

F32 = mybir.dt.float32
ALU = mybir.AluOpType
ACT = mybir.ActivationFunctionType
AX = mybir.AxisListType
P = 128
DIM = 128
TILES = 32
SEQ_TILES = 8


def need(eng, sem, value):
    if not (isinstance(value, int) and value <= 0):
        eng.wait_ge(sem, value)


def apart(eng):
    eng.nop(nofuse=True)


class TileNorm:

    def __init__(self, sb, sem, tag, source, S, ident, banks, dest=None):
        self.source, self.S, self.ident, self.banks = source, S, ident, banks
        self.st = sb(tag + "_stats", [P, S, 6])
        self.mv = sb(tag + "_mean_var", [P, S, 2])
        self.ve = sb(tag + "_var_eps", [P, S])
        self.rstd = sb(tag + "_rstd", [P, S])
        self.z = None if dest else sb(tag + "_z", [P, S, DIM])
        self.dest = dest or (lambda n, s: self.z[:, s, :])
        self.zT = sb(tag + "_zT", [P, S * P]) if banks else None
        self.neg_half = sb(tag + "_neg_half", [P, S])
        self.cleared = sem(tag + "_cleared")
        self.stats_made, self.mean_var_made = sem(tag + "_stats_made"), sem(tag + "_mean_var_made")
        self.var_eps_made, self.rstd_made, self.z_made = sem(tag + "_var_eps_made"), sem(tag + "_rstd_made"), sem(tag + "_z_made")
        if banks:
            self.z_turned, self.zT_made = sem(tag + "_z_turned"), sem(tag + "_zT_made")

    def on_pool_start(self, pool):
        pool.memset(self.neg_half[:, :], -0.5).then_inc(self.cleared, 1)
        pool.wait_ge(self.cleared, 1)

    def on_dve(self, dve, n, free_z):
        S = self.S
        for s in range(S):
            dve.bn_stats(self.st[:, s, :], self.source(n, s)).then_inc(self.stats_made, 1)
        dve.wait_ge(self.stats_made, (n + 1) * S)
        apart(dve)
        for s in range(S):
            dve.bn_aggr(self.mv[:, s, :], self.st[:, s, :]).then_inc(self.mean_var_made, 1)
        dve.wait_ge(self.rstd_made, n + 1)
        free_z(dve, n)
        apart(dve)
        for s in range(S):
            dve.tensor_scalar(self.dest(n, s), self.source(n, s), self.mv[:, s, 0:1],
                              self.rstd[:, s:s + 1], ALU.subtract, ALU.mult).then_inc(self.z_made, 1)

    def on_pool(self, pool, n):
        pool.wait_ge(self.mean_var_made, (n + 1) * self.S)
        apart(pool)
        pool.tensor_scalar(self.ve[:, :], self.mv[:, :, 1], 1e-5, None, ALU.add).then_inc(self.var_eps_made, 1)
        pool.wait_ge(self.var_eps_made, n + 1)
        pool.tensor_tensor(self.rstd[:, :], self.ve[:, :], self.neg_half[:, :], ALU.pow).then_inc(self.rstd_made, 1)

    def on_pe(self, pe, n, free_ps):
        pe.wait_ge(self.z_made, (n + 1) * self.S)
        free_ps(pe, n)
        for s in range(self.S):
            e = pe.transpose(self.banks[s // 4][:, s % 4 * P:(s % 4 + 1) * P], self.z[:, s, :], self.ident[:, :])
            if s % 4 == 3:
                e.then_inc(self.z_turned, 1)

    def on_act(self, act, n, free_zT):
        free_zT(act, n)
        for i, b in enumerate(self.banks):
            act.wait_ge(self.z_turned, n * len(self.banks) + i + 1)
            act.activation(self.zT[:, i * 4 * P:(i + 1) * 4 * P], b[:, :], ACT.Copy).then_inc(self.zT_made, 1)


def tiles_of(x, S):
    return lambda n, s: x[:, bass.ds(n * S + s, 1), :].rearrange("p a d -> p (a d)")

def retention_block(nc, sb, sem, bank, ident, ones_row, x, c):
    H = 8
    V = c["w_g"].shape[1]
    QK = 2 * DIM
    DV = V // H
    SEQS = TILES // SEQ_TILES
    NT = SEQ_TILES
    wqkv = sb("ret_wqkv", [P, QK + V])
    wg = sb("ret_wg", [P, V])
    wp = sb("ret_wp", [P, V // P, DIM])
    b_qkv = sb("ret_b_qkv", [1, QK + V])
    b_g = sb("ret_b_g", [1, V])
    b_p = sb("ret_b_p", [1, DIM])
    cos_tab = sb("ret_cos", [P, NT, QK])
    sin_tab = sb("ret_sin", [P, NT, QK])
    tri = sb("ret_tri", [P, P])
    head_of = sb("ret_head_of", [P, H])
    state_mask = sb("ret_state_mask", [P, V])
    decay = sb("ret_decay", [P, 1])
    raw = sb("ret_qkv", [P, 2, QK + V])
    gs = sb("ret_gate", [P, 2, V])
    r1 = sb("ret_cos_part", [P, QK])
    r2 = sb("ret_sin_part", [P, QK])
    qk = sb("ret_qk", [P, 2, QK])
    qkT = sb("ret_qk_T", [P, 2, QK])
    qb = sb("ret_q_by_head", [P, 2, H, P])
    A = sb("ret_scores", [P, 2, H, P])
    state = sb("ret_state", [P, 2, V])
    grown = sb("ret_state_new", [P, V])
    tot = sb("ret_sum", [P, H])
    mu = sb("ret_mean", [P, H])
    xc = sb("ret_centred", [P, V])
    sq = sb("ret_squares", [P, V])
    var = sb("ret_var", [P, H])
    ve = sb("ret_var_eps", [P, H])
    rs = sb("ret_rstd", [P, H])
    neg_half = sb("ret_neg_half", [P, H])
    xn = sb("ret_normed", [P, V])
    gated = sb("ret_gated", [P, V])
    gT = sb("ret_gated_T", [P, V])
    ps_s, ps_q, ps_g, ps_t, ps_o, ps_m = bank[0:2], bank[2:4], bank[4], bank[5], bank[6], bank[7]
    ln = TileNorm(sb, sem, "ret_ln", tiles_of(x, NT), NT, ident, ps_s)
    names = ("loaded cleared qkv_done raw_made g_done gs_made parts_made qk_made qk_turned qkT_made qb_made s_done a_made o_done st_done "
             "grown_made state_made tot_made mu_made xc_made sq_made var_made ve_made rs_made xn_made gated_made gated_turned gT_made "
             "proj_done x_added").split()
    s_ = {k: sem("ret_" + k) for k in names}
    N_LOADS = 12
    wide = [P, H, DV]

    def by_head(a):
        return a.rearrange("p (h d) -> p h d", d=DV)

    with nc.Block() as block:
        @block.sync
        def _(sp):
            n = [0]

            def load(dst, src):
                n[0] += 1
                sp.dma_start(dst, src).then_inc(s_["loaded"], 16)
            load(wqkv[:, :], c["w_qkv"])
            load(wg[:, :], c["w_g"])
            load(wp[:, :, :], c["w_p"].rearrange("(k p) d -> p k d", p=P))
            load(b_qkv[:, :], c["b_qkv"].unsqueeze(0))
            load(b_g[:, :], c["b_g"].unsqueeze(0))
            load(b_p[:, :], c["b_p"].unsqueeze(0))
            load(cos_tab[:, :, :], c["ret_cos"])
            load(sin_tab[:, :, :], c["ret_sin"])
            load(tri[:, :], c["ret_tri"])
            load(head_of[:, :], c["ret_head_of"])
            load(state_mask[:, :], c["ret_state_mask"])
            load(decay[:, :], c["ret_decay"])
            assert n[0] == N_LOADS

        @block.gpsimd
        def _(pool):
            pool.memset(neg_half[:, :], -0.5).then_inc(s_["cleared"], 1)
            ln.on_pool_start(pool)
            pool.wait_ge(s_["cleared"], 1)

            def body(b):
                ln.on_pool(pool, b)
                for t in range(NT):
                    T = NT * b + t
                    pool.wait_ge(s_["var_made"], T + 1)
                    apart(pool)
                    pool.tensor_scalar(ve[:, :], var[:, :], 1.0 / DV, 1e-5, ALU.mult, ALU.add).then_inc(s_["ve_made"], 1)
                    pool.wait_ge(s_["ve_made"], T + 1)
                    need(pool, s_["xn_made"], T)
                    pool.tensor_tensor(rs[:, :], ve[:, :], neg_half[:, :], ALU.pow).then_inc(s_["rs_made"], 1)
            body(0)
            with pool.Fori(1, SEQS) as b:
                body(b)

        @block.scalar
        def _(act):
            def enter(b, t):
                T = NT * b + t
                act.wait_ge(s_["qkv_done"], T + 1)
                need(act, s_["o_done"], T - 1)
                act.activation(raw[:, t % 2, :], ps_q[t % 2][:, :], ACT.Copy).then_inc(s_["raw_made"], 1)
                act.wait_ge(s_["g_done"], T + 1)
                need(act, s_["gated_made"], T - 1)
                act.activation(gs[:, t % 2, :], ps_g[:, 0:V], ACT.Silu).then_inc(s_["gs_made"], 1)

            def body(b):
                ln.on_act(act, b, lambda e, n: need(e, s_["g_done"], NT * n))
                enter(b, 0)
                for t in range(NT):
                    T = NT * b + t
                    act.wait_ge(s_["qk_turned"], T + 1)
                    need(act, s_["o_done"], T - 1)
                    act.activation(qkT[:, t % 2, :], ps_t[:, 0:QK], ACT.Copy).then_inc(s_["qkT_made"], 1)
                    if t + 1 < NT:
                        enter(b, t + 1)
                    act.wait_ge(s_["xc_made"], T + 1)
                    need(act, s_["var_made"], T)
                    act.activation(sq[:, :], xc[:, :], ACT.Square).then_inc(s_["sq_made"], 1)
                    act.wait_ge(s_["gated_turned"], T + 1)
                    need(act, s_["proj_done"], T)
                    act.activation(gT[:, :], ps_t[:, 0:V], ACT.Copy).then_inc(s_["gT_made"], 1)
            body(0)
            with act.Fori(1, SEQS) as b:
                body(b)

        @block.vector
        def _(dve):
            dve.wait_ge(s_["loaded"], 16 * N_LOADS)

            def rope(b, t):
                T = NT * b + t
                dve.wait_ge(s_["raw_made"], T + 1)
                need(dve, s_["qk_made"], T)
                dve.tensor_tensor(r1[:, :], raw[:, t % 2, 0:QK], cos_tab[:, t, :], ALU.mult)
                for i in range(2):
                    m = dve.tensor_tensor(r2[:, i:QK:2], raw[:, t % 2, 1 - i:QK:2], sin_tab[:, t, i:QK:2], ALU.mult)
                m.then_inc(s_["parts_made"], 1)
                dve.wait_ge(s_["parts_made"], T + 1)
                need(dve, s_["st_done"], (NT - 1) * b + t - 1)
                need(dve, s_["qk_turned"], T - 1)
                dve.tensor_tensor(qk[:, t % 2, :], r1[:, :], r2[:, :], ALU.add).then_inc(s_["qk_made"], 1)

            def scores(b, t):
                T = NT * b + t
                dve.wait_ge(s_["qkT_made"], T + 1)
                need(dve, s_["s_done"], 2 * (T - 1))
                dve.tensor_tensor(qb[:, t % 2, :, :], qkT[:, t % 2, 0:P].unsqueeze(1).to_broadcast([P, H, P]),
                                  head_of[:, :].unsqueeze(2).to_broadcast([P, H, P]), ALU.mult).then_inc(s_["qb_made"], 1)
                need(dve, s_["o_done"], T - 1)
                for i in range(2):
                    dve.wait_ge(s_["s_done"], 2 * T + i + 1)
                    dve.tensor_tensor(A[:, t % 2, 4 * i:4 * i + 4, :], ps_s[i].rearrange("p (h q) -> p h q", q=P),
                                      tri[:, :].unsqueeze(1).to_broadcast([P, 4, P]), ALU.mult).then_inc(s_["a_made"], 1)

            def next_state(b, t):
                K = (NT - 1) * b + t
                dve.wait_ge(s_["st_done"], K + 1)
                need(dve, s_["o_done"], NT * b + t)
                out = state[:, (t + 1) % 2, :] if t == 0 else grown[:, :]
                dve.tensor_tensor(out, ps_m[:, 0:V], state_mask[:, :], ALU.mult).then_inc(s_["grown_made"], 1)
                if t:
                    dve.wait_ge(s_["grown_made"], K + 1)
                    dve.wait_ge(s_["state_made"], K)
                    dve.scalar_tensor_tensor(state[:, (t + 1) % 2, :], state[:, t % 2, :], decay[:, 0:1], grown[:, :], ALU.mult, ALU.add
                                             ).then_inc(s_["state_made"], 1)
                else:
                    dve.wait_ge(s_["grown_made"], K + 1)
                    dve.sem_inc(s_["state_made"], 1)

            def group_norm(b, t):
                T = NT * b + t
                o = by_head(ps_o[:, 0:V])
                dve.wait_ge(s_["o_done"], T + 1)
                dve.tensor_reduce(tot[:, :], o, AX.X, ALU.add).then_inc(s_["tot_made"], 1)
                dve.wait_ge(s_["tot_made"], T + 1)
                dve.tensor_scalar(mu[:, :], tot[:, :], 1.0 / DV, None, ALU.mult).then_inc(s_["mu_made"], 1)
                dve.wait_ge(s_["mu_made"], T + 1)
                dve.tensor_tensor(by_head(xc[:, :]), o, mu[:, :].unsqueeze(2).to_broadcast(wide), ALU.subtract).then_inc(s_["xc_made"], 1)
                dve.wait_ge(s_["sq_made"], T + 1)
                dve.tensor_reduce(var[:, :], by_head(sq[:, :]), AX.X, ALU.add).then_inc(s_["var_made"], 1)
                dve.wait_ge(s_["rs_made"], T + 1)
                dve.tensor_tensor(by_head(xn[:, :]), by_head(xc[:, :]), rs[:, :].unsqueeze(2).to_broadcast(wide), ALU.mult).then_inc(s_["xn_made"], 1)
                dve.wait_ge(s_["xn_made"], T + 1)
                dve.wait_ge(s_["gs_made"], T + 1)
                need(dve, s_["gated_turned"], T)
                dve.tensor_tensor(gated[:, :], xn[:, :], gs[:, t % 2, :], ALU.mult).then_inc(s_["gated_made"], 1)

            def residual(b, t):
                T = NT * b + t
                dve.wait_ge(s_["proj_done"], T + 1)
                apart(dve)
                xs = x[:, bass.ds(T, 1), :].rearrange("p a d -> p (a d)")
                dve.tensor_tensor(xs, ps_m[:, V:V + DIM], xs, ALU.add).then_inc(s_["x_added"], 1)

            def body(b):
                ln.on_dve(dve, b, lambda e, n: need(e, ln.z_turned, 2 * n))
                rope(b, 0)
                for t in range(NT):
                    scores(b, t)
                    if t + 1 < NT:
                        next_state(b, t)
                        rope(b, t + 1)
                    group_norm(b, t)
                    residual(b, t)
            body(0)
            with dve.Fori(1, SEQS) as b:
                body(b)

        @block.tensor
        def _(pe):
            pe.wait_ge(s_["loaded"], 16 * N_LOADS)

            def enter(b, t):
                T = NT * b + t
                pe.wait_ge(ln.zT_made, 2 * b + t // 4 + 1)
                zT = ln.zT[:, t * P:(t + 1) * P]
                need(pe, s_["raw_made"], T - 1)
                pe.matmul(ps_q[t % 2][:, :], zT, wqkv[:, :], start=True, stop=False)
                pe.matmul(ps_q[t % 2][:, :], ones_row[0:1, :], b_qkv[0:1, :], start=False, stop=True).then_inc(s_["qkv_done"], 1)
                need(pe, s_["gs_made"], T)
                pe.matmul(ps_g[:, 0:V], zT, wg[:, :], start=True, stop=False)
                pe.matmul(ps_g[:, 0:V], ones_row[0:1, :], b_g[0:1, :], start=False, stop=True).then_inc(s_["g_done"], 1)

            def turn_qk(b, t):
                T = NT * b + t
                pe.wait_ge(s_["qk_made"], T + 1)
                need(pe, s_["gT_made"], T)
                for i in range(2):
                    m = pe.transpose(ps_t[:, i * P:(i + 1) * P], qk[:, t % 2, i * P:(i + 1) * P], ident[:, :])
                m.then_inc(s_["qk_turned"], 1)

            def scores(b, t):
                T = NT * b + t
                pe.wait_ge(s_["qb_made"], T + 1)
                need(pe, s_["a_made"], 2 * T)
                if t == 0:
                    pe.wait_ge(ln.zT_made, 2 * b + 2)
                for i in range(2):
                    pe.matmul(ps_s[i][:, :], qkT[:, t % 2, P:2 * P], qb[:, t % 2, 4 * i:4 * i + 4, :].rearrange("p h q -> p (h q)"),
                              start=True, stop=True).then_inc(s_["s_done"], 1)

            def state_part(b, t):
                T = NT * b + t
                need(pe, s_["x_added"], T)
                need(pe, s_["grown_made"], (NT - 1) * b + t)
                pe.matmul(ps_m[:, 0:V], qk[:, t % 2, P:2 * P], raw[:, t % 2, QK:QK + V], start=True, stop=True).then_inc(s_["st_done"], 1)

            def output(b, t):
                T = NT * b + t
                need(pe, s_["xc_made"], T)
                if t:
                    pe.wait_ge(s_["state_made"], (NT - 1) * b + t)
                    pe.matmul(ps_o[:, 0:V], qkT[:, t % 2, 0:P], state[:, t % 2, :], start=True, stop=True)
                pe.wait_ge(s_["a_made"], 2 * T + 2)
                for h in range(H):
                    m = pe.matmul(ps_o[:, h * DV:(h + 1) * DV], A[:, t % 2, h, :], raw[:, t % 2, QK + h * DV:QK + (h + 1) * DV],
                                  start=(t == 0), stop=True, skip_group_check=True)
                m.then_inc(s_["o_done"], 1)

            def project(b, t):
                T = NT * b + t
                pe.wait_ge(s_["gated_made"], T + 1)
                pe.wait_ge(s_["qkT_made"], T + 1)
                for i in range(V // P):
                    m = pe.transpose(ps_t[:, i * P:(i + 1) * P], gated[:, i * P:(i + 1) * P], ident[:, :])
                m.then_inc(s_["gated_turned"], 1)
                pe.wait_ge(s_["gT_made"], T + 1)
                if t + 1 < NT:
                    pe.wait_ge(s_["grown_made"], (NT - 1) * b + t + 1)
                for i in range(V // P):
                    pe.matmul(ps_m[:, V:V + DIM], gT[:, i * P:(i + 1) * P], wp[:, i, :], start=(i == 0), stop=False)
                pe.matmul(ps_m[:, V:V + DIM], ones_row[0:1, :], b_p[0:1, :], start=False, stop=True).then_inc(s_["proj_done"], 1)

            def body(b):
                ln.on_pe(pe, b, lambda e, n: need(e, s_["a_made"], 2 * NT * n))
                enter(b, 0)
                for t in range(NT):
                    turn_qk(b, t)
                    if t + 1 < NT:
                        enter(b, t + 1)
                    scores(b, t)
                    if t + 1 < NT:
                        state_part(b, t)
                    output(b, t)
                    project(b, t)
            body(0)
            with pe.Fori(1, SEQS) as b:
                body(b)

def mixture(nc, sb, sem, bank, ident, ones_row, x, c):
    EXPERTS, _, FF = c["W1"].shape
    FC = FF // P
    S = 4
    ROUNDS = TILES // S
    w1 = sb("moe_w1", [P, EXPERTS, FF])
    w2 = sb("moe_w2", [P, EXPERTS, FC, DIM])
    wr = sb("moe_wr", [P, EXPERTS])
    br = sb("moe_br", [1, EXPERTS])
    b1c = sb("moe_b1_col", [P, EXPERTS, FC])
    b2 = sb("moe_b2", [EXPERTS, DIM])
    rank = sb("moe_rank", [P, S, EXPERTS])
    hT = sb("moe_hidden_T", [P, 2, FC, S * P])
    acc = sb("moe_acc", [P, S, DIM])
    prob = sb("moe_probs", [P, S, EXPERTS])
    work = sb("moe_work", [P, S, EXPERTS])
    work2 = sb("moe_work2", [P, S, EXPERTS])
    hot1 = sb("moe_first", [P, S, EXPERTS])
    hot2 = sb("moe_second", [P, S, EXPERTS])
    col = sb("moe_col", [P, S])
    colb = sb("moe_colb", [P, S])
    gates = sb("moe_gates", [P, S, EXPERTS])
    gatesT = sb("moe_gates_T", [EXPERTS, S * P])
    psZ, psR = bank[0], bank[1]
    psY, psH = bank[2:4], bank[4:8]
    ln = TileNorm(sb, sem, "moe_ln", tiles_of(x, S), S, ident, [psZ])
    small_loaded, w_loaded = sem("moe_small_loaded"), [sem("moe_weights_loaded_0"), sem("moe_weights_loaded_1")]
    logits_done, exp_made, step_made, gates_made, gates_turned, gatesT_made, bias_done, acc_made = (sem("moe_" + s) for s in (
        "logits_done", "exp_made", "step_made", "gates_made", "gates_turned", "gatesT_made", "bias_done", "acc_made"))
    up_done, gelu_made, down_done, added = sem("moe_up_done"), sem("moe_gelu_made"), sem("moe_down_done"), sem("moe_added")
    N_SMALL = 5
    LOTS = [(0, 2), (2, EXPERTS)]
    STEPS = 21

    with nc.Block() as block:
        @block.sync
        def _(sp):
            sp.dma_start(wr[:, :], c["Wr"]).then_inc(small_loaded, 16)
            sp.dma_start(br[:, :], c["br"].unsqueeze(0)).then_inc(small_loaded, 16)
            sp.dma_start(b2[:, :], c["b2"]).then_inc(small_loaded, 16)
            sp.dma_start(rank[:, :, :], c["rank"]).then_inc(small_loaded, 16)
            with nc.allow_non_contiguous_dma("small columns"):
                sp.dma_start(b1c[:, :, :], c["b1"].rearrange("e (c p) -> p e c", p=P)).then_inc(small_loaded, 16)
            for i, (lo, hi) in enumerate(LOTS):
                for dst, src in ((w1[:, lo:hi, :], c["W1"][lo:hi, :, :].rearrange("e p f -> p e f")),
                                 (w2[:, lo:hi, :, :], c["W2"][lo:hi, :, :].rearrange("e (c p) d -> p e c d", p=P))):
                    sp.dma_start(dst, src).then_inc(w_loaded[i], 16)

        @block.gpsimd
        def _(pool):
            ln.on_pool_start(pool)
            with pool.Fori(0, ROUNDS) as n:
                ln.on_pool(pool, n)

        @block.scalar
        def _(act):
            act.wait_ge(small_loaded, 16 * N_SMALL)

            def body(n):
                ln.on_act(act, n, lambda e, n: need(e, up_done, n * EXPERTS * FC))
                act.wait_ge(step_made, STEPS * n + 2)
                act.activation(prob[:, :, :], work[:, :, :], ACT.Exp).then_inc(exp_made, 1)
                for e in range(EXPERTS):
                    i = n * EXPERTS + e
                    need(act, down_done, i - 1)
                    for ch in range(FC):
                        act.wait_ge(up_done, i * FC + ch + 1)
                        act.activation(hT[:, e % 2, ch, :], psH[ch][:, :], ACT.Gelu, bias=b1c[:, e, ch:ch + 1]).then_inc(gelu_made, 1)
                    if e == 1:
                        act.wait_ge(gates_turned, n + 1)
                        need(act, bias_done, n)
                        act.activation(gatesT[:, :], psZ[0:EXPERTS, :], ACT.Copy).then_inc(gatesT_made, 1)
            body(0)
            with act.Fori(1, ROUNDS) as n:
                body(n)

        @block.vector
        def _(dve):
            dve.wait_ge(small_loaded, 16 * N_SMALL)

            def route(n):
                k = [0]
                wide = [P, S, EXPERTS]

                def step(ins):
                    k[0] += 1
                    ins.then_inc(step_made, 1)
                    dve.wait_ge(step_made, STEPS * n + k[0])

                def spread(a):
                    return a[:, :].unsqueeze(2).to_broadcast(wide)

                def first_of_largest(hot, p):
                    step(dve.tensor_reduce(col[:, :], p[:, :, :], AX.X, ALU.max))
                    step(dve.tensor_tensor(work[:, :, :], p[:, :, :], spread(col), ALU.is_equal))
                    step(dve.tensor_tensor(work[:, :, :], work[:, :, :], rank[:, :, :], ALU.mult))
                    step(dve.tensor_reduce(colb[:, :], work[:, :, :], AX.X, ALU.max))
                    step(dve.tensor_tensor(hot[:, :, :], work[:, :, :], spread(colb), ALU.is_equal))

                logits = psR[:, 0:S * EXPERTS].rearrange("p (s e) -> p s e", e=EXPERTS)
                dve.wait_ge(logits_done, n + 1)
                step(dve.tensor_reduce(col[:, :], logits, AX.X, ALU.max))
                step(dve.tensor_tensor(work[:, :, :], logits, spread(col), ALU.subtract))
                dve.wait_ge(exp_made, n + 1)
                step(dve.tensor_reduce(col[:, :], prob[:, :, :], AX.X, ALU.add))
                step(dve.reciprocal(colb[:, :], col[:, :]))
                step(dve.tensor_tensor(prob[:, :, :], prob[:, :, :], spread(colb), ALU.mult))
                first_of_largest(hot1, prob)
                step(dve.scalar_tensor_tensor(work2[:, :, :], hot1[:, :, :], -2.0, prob[:, :, :], ALU.mult, ALU.add))
                first_of_largest(hot2, work2)
                step(dve.tensor_tensor(work[:, :, :], hot1[:, :, :], hot2[:, :, :], ALU.add))
                step(dve.tensor_tensor(work2[:, :, :], work[:, :, :], prob[:, :, :], ALU.mult))
                step(dve.tensor_reduce(col[:, :], work2[:, :, :], AX.X, ALU.add))
                step(dve.tensor_scalar(colb[:, :], col[:, :], 1e-9, None, ALU.add))
                step(dve.reciprocal(col[:, :], colb[:, :]))
                assert k[0] == STEPS
                need(dve, gates_turned, n)
                dve.tensor_tensor(gates[:, :, :], work2[:, :, :], spread(col), ALU.mult).then_inc(gates_made, 1)

            def body(n):
                ln.on_dve(dve, n, lambda e, n: need(e, ln.z_turned, n))
                route(n)
                dve.wait_ge(bias_done, n + 1)
                apart(dve)
                dve.tensor_tensor(acc[:, :, :].rearrange("p s d -> p (s d)"), psR[:, :],
                                  x[:, bass.ds(n * S, S), :].rearrange("p s d -> p (s d)"), ALU.add).then_inc(acc_made, 1)
                dve.wait_ge(acc_made, n + 1)
                for e in range(EXPERTS):
                    i = n * EXPERTS + e
                    dve.wait_ge(down_done, i + 1)
                    if e:
                        dve.wait_ge(added, S * i)
                    else:
                        dve.wait_ge(gates_made, n + 1)
                    apart(dve)
                    for s in range(S):
                        out = x[:, bass.ds(n * S + s, 1), :].rearrange("p a d -> p (a d)") if e == EXPERTS - 1 else acc[:, s, :]
                        dve.scalar_tensor_tensor(out, psY[e % 2][:, s * P:(s + 1) * P], gates[:, s, e:e + 1], acc[:, s, :],
                                                 ALU.mult, ALU.add).then_inc(added, 1)
            body(0)
            with dve.Fori(1, ROUNDS) as n:
                body(n)

        @block.tensor
        def _(pe):
            pe.wait_ge(small_loaded, 16 * N_SMALL)

            def up(n, e):
                i = n * EXPERTS + e
                if isinstance(n, int):
                    pe.wait_ge(w_loaded[0 if e < 2 else 1], 32)
                for ch in range(FC):
                    need(pe, gelu_made, (i - 1) * FC + ch + 1)
                    pe.matmul(psH[ch][:, :], w1[:, e, ch * P:(ch + 1) * P], ln.zT[:, :], start=True, stop=True).then_inc(up_done, 1)

            def down(n, e):
                i = n * EXPERTS + e
                need(pe, added, S * (i - 1))
                pe.wait_ge(gelu_made, (i + 1) * FC)
                for s in range(S):
                    for ch in range(FC):
                        m = pe.matmul(psY[e % 2][:, s * P:(s + 1) * P], hT[:, e % 2, ch, s * P:(s + 1) * P], w2[:, e, ch, :],
                                      start=(ch == 0), stop=(ch == FC - 1))
                m.then_inc(down_done, 1)

            def body(n):
                ln.on_pe(pe, n, lambda e, n: need(e, gatesT_made, n))
                pe.wait_ge(ln.zT_made, n + 1)
                need(pe, acc_made, n)
                for s in range(S):
                    o = psR[:, s * EXPERTS:(s + 1) * EXPERTS]
                    pe.matmul(o, ln.zT[:, s * P:(s + 1) * P], wr[:, :], start=True, stop=False)
                    m = pe.matmul(o, ones_row[0:1, :], br[0:1, :], start=False, stop=True)
                m.then_inc(logits_done, 1)
                up(n, 0)
                up(n, 1)
                down(n, 0)
                pe.wait_ge(gates_made, n + 1)
                for s in range(S):
                    m = pe.transpose(psZ[0:EXPERTS, s * P:(s + 1) * P], gates[:, s, :], ident[:, :])
                m.then_inc(gates_turned, 1)
                pe.wait_ge(gatesT_made, n + 1)
                apart(pe)
                for s in range(S):
                    m = pe.matmul(psR[:, s * P:(s + 1) * P], gatesT[:, s * P:(s + 1) * P], b2[:, :], start=True, stop=True)
                m.then_inc(bias_done, 1)
                for e in range(2, EXPERTS):
                    up(n, e)
                    down(n, e - 1)
                down(n, EXPERTS - 1)
            body(0)
            with pe.Fori(1, ROUNDS) as n:
                body(n)

def linear_block(nc, sb, sem, bank, ident, ones_row, x, c):
    H, HD, NF = c["proj"].shape
    FF = c["w1T"].shape[1]
    FC = FF // P
    KC = H * NF // P
    HC = P // NF
    SEQS = TILES // SEQ_TILES
    S = 4
    W = S * P
    wqk = sb("lin_wqk", [P, 2, DIM])
    wvT = sb("lin_wvT", [P, DIM])
    blocks = sb("lin_proj_blocks", [P, H * NF])
    G = sb("lin_feature_weights", [P, 2, H * NF])
    w_outT = sb("lin_w_outT", [P, DIM])
    w1T = sb("lin_w1T", [P, FF])
    w2T = sb("lin_w2T", [P, FC, DIM])
    b_out = sb("lin_b_out", [1, DIM])
    b2 = sb("lin_b2", [1, DIM])
    b1c = sb("lin_b1_col", [P, FC])
    gamma = sb("lin_gamma", [P, DIM])
    beta = sb("lin_beta", [P, DIM])
    kv_mask = sb("lin_kv_mask", [P, KC, DIM])
    ks_mask = sb("lin_ks_mask", [P, KC, H])
    low = sb("lin_low", [P, 2, W])
    kf = sb("lin_kf", [P, 2, H * NF])
    v1 = sb("lin_v_and_one", [P, SEQ_TILES, DIM + 1])
    kv = sb("lin_kv", [P, KC, DIM])
    ks = sb("lin_ksum", [P, KC, H])
    qf = sb("lin_qf_T", [P, KC, SEQ_TILES * P])
    den = sb("lin_den", [P, S * H])
    rden = sb("lin_inv_den", [P, S * H])
    at = sb("lin_attn", [P, W])
    atT = sb("lin_attn_T", [P, W])
    x1 = sb("lin_x1", [P, S, DIM])
    gm = sb("lin_gained", [P, S, DIM])
    x1n = sb("lin_x1_normed", [P, S, DIM])
    x1T = sb("lin_x1_T", [P, W])
    hT = sb("lin_hidden_T", [P, FC, W])
    x2 = sb("lin_x2", [P, S, DIM])
    gm2 = sb("lin_gained2", [P, S, DIM])
    y = sb("lin_y", [P, S, DIM])
    ps_z, ps_u, ps_kv, ps_v, ps_m = bank[0:2], bank[2:4], bank[4:6], bank[6], bank[7]
    ln = TileNorm(sb, sem, "lin_ln", tiles_of(x, SEQ_TILES), SEQ_TILES, ident, ps_z)
    ln1 = TileNorm(sb, sem, "lin_ln1", lambda n, s: x1[:, s, :], S, ident, None)
    ln2 = TileNorm(sb, sem, "lin_ln2", lambda n, s: x2[:, s, :], S, ident, None)
    names = ("loaded weights_cleared blocks_loaded g_done g_made u_done low_made exp_made kf_made v_done v_made kv_done kv_made "
             "attn_done den_made rden_made at_made at_turned atT_made o_done x1_made gained1 x1n_made x1n_turned x1T_made "
             "up_done gelu_made down_done x2_made gained2 y_made x_added").split()
    s_ = {k: sem("lin_" + k) for k in names}
    N_LOADS = 12
    UT = 2 * SEQ_TILES

    with nc.Block() as block:
        @block.sync
        def _(sp):
            n = [0]

            def load(dst, src):
                n[0] += 1
                sp.dma_start(dst, src).then_inc(s_["loaded"], 16)
            load(wqk[:, :, :], c["w_qkv"][0:2 * DIM, :].rearrange("(a o) i -> o a i", a=2))
            load(wvT[:, :], c["wvT"])
            load(w_outT[:, :], c["w_outT"])
            load(w1T[:, :], c["w1T"])
            load(w2T[:, :, :], c["w2T"].rearrange("(c p) d -> p c d", p=P))
            load(b_out[:, :], c["b_out"].unsqueeze(0))
            load(b2[:, :], c["b2"].unsqueeze(0))
            with nc.allow_non_contiguous_dma("small columns"):
                load(b1c[:, :], c["b1"].rearrange("(c p) -> p c", p=P))
            load(gamma[:, :], c["gamma"].partition_broadcast(P))
            load(beta[:, :], c["beta"].partition_broadcast(P))
            load(kv_mask[:, :, :], c["kv_mask"])
            load(ks_mask[:, :, :], c["ks_mask"])
            assert n[0] == N_LOADS
            sp.wait_ge(s_["weights_cleared"], 2)
            for h in range(H):
                sp.dma_start(blocks[h * HD:(h + 1) * HD, h * NF:(h + 1) * NF], c["proj"][h, :, :]).then_inc(s_["blocks_loaded"], 16)

        @block.gpsimd
        def _(pool):
            pool.memset(blocks[:, :], 0.0).then_inc(s_["weights_cleared"], 1)
            pool.memset(v1[:, :, DIM:DIM + 1], 1.0).then_inc(s_["weights_cleared"], 1)
            for l in (ln, ln1, ln2):
                l.on_pool_start(pool)
            pool.wait_ge(s_["loaded"], 16 * N_LOADS)

            def gain(l, r, g_buf, out, gained, made, free):
                pool.wait_ge(l.z_made, S * (r + 1))
                need(pool, made, r)
                apart(pool)
                pool.tensor_tensor(g_buf[:, :, :], l.z[:, :, :], gamma[:, :].unsqueeze(1).to_broadcast([P, S, DIM]), ALU.mult).then_inc(gained, 1)
                pool.wait_ge(gained, r + 1)
                free(r)
                apart(pool)
                pool.tensor_tensor(out[:, :, :], g_buf[:, :, :], beta[:, :].unsqueeze(1).to_broadcast([P, S, DIM]), ALU.add).then_inc(made, 1)

            def body(b):
                ln.on_pool(pool, b)
                for g in range(2):
                    r = 2 * b + g
                    ln1.on_pool(pool, r)
                    gain(ln1, r, gm, x1n, s_["gained1"], s_["x1n_made"], lambda r: need(pool, s_["x2_made"], r))
                    ln2.on_pool(pool, r)
                    gain(ln2, r, gm2, y, s_["gained2"], s_["y_made"], lambda r: need(pool, s_["x_added"], r))
            body(0)
            with pool.Fori(1, SEQS) as b:
                body(b)

        @block.scalar
        def _(act):
            act.wait_ge(s_["loaded"], 16 * N_LOADS)
            act.wait_ge(s_["g_done"], 2)
            for a in range(2):
                act.activation(G[:, a, :], ps_u[a][:, :], ACT.Copy).then_inc(s_["g_made"], 1)

            def exp_low(b, i):
                U = UT * b + i
                act.wait_ge(s_["low_made"], U + 1)
                act.activation(low[:, i % 2, :], low[:, i % 2, :], ACT.Exp).then_inc(s_["exp_made"], 1)

            def evac(src, dst, done, made, free, r):
                act.wait_ge(done, r + 1)
                need(act, free, r)
                act.activation(dst[:, :], src[:, :], ACT.Copy).then_inc(made, 1)

            def body(b):
                ln.on_act(act, b, lambda e, n: need(e, s_["u_done"], UT * n))
                for half in range(2):
                    act.wait_ge(s_["v_done"], 2 * b + half + 1)
                    need(act, s_["kv_done"], b)
                    act.activation(v1[:, 4 * half:4 * half + 4, 0:DIM], ps_v.rearrange("p (s d) -> p s d", d=DIM), ACT.Copy).then_inc(s_["v_made"], 1)
                    for i in range(4 * half, 4 * half + 4):
                        exp_low(b, i)
                for i in range(SEQ_TILES, UT):
                    exp_low(b, i)
                for g in range(2):
                    r = 2 * b + g
                    evac(ps_m, atT, s_["at_turned"], s_["atT_made"], s_["o_done"], r)
                    evac(ps_m, x1T, s_["x1n_turned"], s_["x1T_made"], s_["down_done"], r)
                    for ch in range(FC):
                        act.wait_ge(s_["up_done"], FC * r + ch + 1)
                        need(act, s_["down_done"], r)
                        act.activation(hT[:, ch, :], ps_u[ch % 2][:, :], ACT.Gelu, bias=b1c[:, ch:ch + 1]).then_inc(s_["gelu_made"], 1)
            body(0)
            with act.Fori(1, SEQS) as b:
                body(b)

        @block.vector
        def _(dve):
            dve.wait_ge(s_["loaded"], 16 * N_LOADS)

            def feature(b, i):
                U = UT * b + i
                dve.wait_ge(s_["u_done"], U + 1)
                need(dve, s_["kf_made"], U - 1)
                dve.tensor_scalar(low[:, i % 2, :], ps_u[i % 2][:, :], 0.0, None, ALU.min).then_inc(s_["low_made"], 1)

            def feature_end(b, i):
                U = UT * b + i
                out = kf[:, i % 2, :] if i < SEQ_TILES else qf[:, i % KC, (i - SEQ_TILES) // KC * W:((i - SEQ_TILES) // KC + 1) * W]
                dve.wait_ge(s_["exp_made"], U + 1)
                if i < SEQ_TILES:
                    need(dve, s_["kv_done"], SEQ_TILES * b + i - 1)
                else:
                    need(dve, s_["attn_done"], 2 * b)
                dve.scalar_tensor_tensor(out, ps_u[i % 2][:, :], 0.0, low[:, i % 2, :], ALU.max, ALU.add).then_inc(s_["kf_made"], 1)

            def body(b):
                ln.on_dve(dve, b, lambda e, n: need(e, s_["x1_made"], 2 * n))
                feature(b, 0)
                for i in range(1, SEQ_TILES):
                    feature(b, i)
                    feature_end(b, i - 1)
                feature_end(b, SEQ_TILES - 1)
                dve.wait_ge(s_["kv_done"], SEQ_TILES * (b + 1))
                need(dve, s_["attn_done"], 2 * b)
                apart(dve)
                for ch in range(KC):
                    o = (ch % 2) * (DIM + 1)
                    dve.tensor_tensor(kv[:, ch, :], ps_kv[ch // 2][:, o:o + DIM], kv_mask[:, ch, :], ALU.mult)
                    dve.tensor_tensor(ks[:, ch, :], ps_kv[ch // 2][:, o + DIM:o + DIM + 1].to_broadcast([P, H]), ks_mask[:, ch, :],
                                      ALU.mult).then_inc(s_["kv_made"], 1)
                feature(b, SEQ_TILES)
                for i in range(SEQ_TILES + 1, UT):
                    feature(b, i)
                    feature_end(b, i - 1)
                feature_end(b, UT - 1)
                for g in range(2):
                    r = 2 * b + g
                    dve.wait_ge(s_["attn_done"], r + 1)
                    dve.tensor_scalar(den[:, :], ps_v[:, 0:S * H], 1e-8, None, ALU.add).then_inc(s_["den_made"], 1)
                    dve.wait_ge(s_["den_made"], r + 1)
                    dve.reciprocal(rden[:, :], den[:, :]).then_inc(s_["rden_made"], 1)
                    dve.wait_ge(s_["rden_made"], r + 1)
                    need(dve, s_["at_turned"], r)
                    dve.tensor_tensor(at[:, :].rearrange("p (h d) -> p h d", d=HD), ps_m.rearrange("p (h d) -> p h d", d=HD),
                                      rden[:, :].unsqueeze(2).to_broadcast([P, S * H, HD]), ALU.mult).then_inc(s_["at_made"], 1)
                    dve.wait_ge(s_["o_done"], r + 1)
                    apart(dve)
                    dve.tensor_tensor(x1[:, :, :].rearrange("p s d -> p (s d)"), ps_m[:, :], ln.z[:, 4 * g:4 * g + 4, :].rearrange("p s d -> p (s d)"),
                                      ALU.add).then_inc(s_["x1_made"], 1)
                    dve.wait_ge(s_["x1_made"], r + 1)
                    apart(dve)
                    ln1.on_dve(dve, r, lambda e, n: need(e, s_["gained1"], n))
                    dve.wait_ge(s_["down_done"], r + 1)
                    dve.wait_ge(s_["x1n_made"], r + 1)
                    dve.tensor_tensor(x2[:, :, :].rearrange("p s d -> p (s d)"), ps_m[:, :], x1n[:, :, :].rearrange("p s d -> p (s d)"),
                                      ALU.add).then_inc(s_["x2_made"], 1)
                    dve.wait_ge(s_["x2_made"], r + 1)
                    apart(dve)
                    ln2.on_dve(dve, r, lambda e, n: need(e, s_["gained2"], n))
                    dve.wait_ge(s_["y_made"], r + 1)
                    apart(dve)
                    xs = x[:, bass.ds(r * S, S), :].rearrange("p s d -> p (s d)")
                    dve.tensor_tensor(xs, xs, y[:, :, :].rearrange("p s d -> p (s d)"), ALU.add).then_inc(s_["x_added"], 1)
            body(0)
            with dve.Fori(1, SEQS) as b:
                body(b)

        @block.tensor
        def _(pe):
            pe.wait_ge(s_["loaded"], 16 * N_LOADS)
            pe.wait_ge(s_["blocks_loaded"], 16 * H)
            for a in range(2):
                pe.matmul(ps_u[a][:, :], wqk[:, a, :], blocks[:, :], start=True, stop=True).then_inc(s_["g_done"], 1)
            pe.wait_ge(s_["g_made"], 2)

            def free_u(b, i):
                if i < 2:
                    need(pe, s_["gelu_made"], 2 * FC * b)
                need(pe, s_["kf_made"], UT * b + i - 1)

            def body(b):
                ln.on_pe(pe, b, lambda e, n: need(e, ln.zT_made, 2 * n))
                pe.wait_ge(ln.zT_made, 2 * b + 2)

                def values(half):
                    need(pe, s_["v_made"] if half else s_["rden_made"], 2 * b + half)
                    for t in range(4 * half, 4 * half + 4):
                        m = pe.matmul(ps_v[:, t % 4 * DIM:(t % 4 + 1) * DIM], ln.zT[:, t * P:(t + 1) * P], wvT[:, :], start=True, stop=True)
                    m.then_inc(s_["v_done"], 1)

                def keys(t):
                    free_u(b, t)
                    pe.matmul(ps_u[t % 2][:, :], ln.zT[:, t * P:(t + 1) * P], G[:, 1, :], start=True, stop=True).then_inc(s_["u_done"], 1)

                def add_kv(t):
                    pe.wait_ge(s_["v_made"], 2 * b + t // 4 + 1)
                    pe.wait_ge(s_["kf_made"], UT * b + t + 1)
                    if t == 0:
                        need(pe, s_["kv_made"], KC * b)
                    for ch in range(KC):
                        o = (ch % 2) * (DIM + 1)
                        m = pe.matmul(ps_kv[ch // 2][:, o:o + DIM + 1], kf[:, t % 2, ch * P:(ch + 1) * P], v1[:, t, :],
                                      start=(t == 0 and ch % 2 == 0), stop=(t == SEQ_TILES - 1 and ch % 2 == 1), skip_group_check=True)
                    m.then_inc(s_["kv_done"], 1)
                values(0)
                keys(0)
                keys(1)
                for t in range(2, SEQ_TILES):
                    add_kv(t - 2)
                    if t == 4:
                        values(1)
                    keys(t)
                add_kv(SEQ_TILES - 2)
                add_kv(SEQ_TILES - 1)
                for i in range(SEQ_TILES, UT):
                    free_u(b, i)
                    ch, half = i % KC, (i - SEQ_TILES) // KC
                    pe.matmul(ps_u[i % 2][:, :], G[:, 0, ch * P:(ch + 1) * P], ln.zT[:, half * W:(half + 1) * W], start=True, stop=True).then_inc(s_["u_done"], 1)
                for g in range(2):
                    r = 2 * b + g
                    pe.wait_ge(s_["kf_made"], UT * b + SEQ_TILES + KC * (g + 1))
                    pe.wait_ge(s_["kv_made"], KC * (b + 1))
                    need(pe, s_["x2_made"], r)
                    need(pe, s_["v_made"], 2 * b + 2)
                    for t in range(S):
                        for ch in range(KC):
                            lhs = qf[:, ch, (4 * g + t) * P:(4 * g + t + 1) * P]
                            pe.matmul(ps_m[:, t * DIM:(t + 1) * DIM], lhs, kv[:, ch, :], start=(ch == 0), stop=(ch == KC - 1))
                        for ch in range(KC):
                            lhs = qf[:, ch, (4 * g + t) * P:(4 * g + t + 1) * P]
                            m = pe.matmul(ps_v[:, t * H:(t + 1) * H], lhs, ks[:, ch, :], start=(ch == 0), stop=(ch == KC - 1))
                    m.then_inc(s_["attn_done"], 1)
                    pe.wait_ge(s_["at_made"], r + 1)
                    for t in range(S):
                        m = pe.transpose(ps_m[:, t * P:(t + 1) * P], at[:, t * P:(t + 1) * P], ident[:, :])
                    m.then_inc(s_["at_turned"], 1)
                    pe.wait_ge(s_["atT_made"], r + 1)
                    for t in range(S):
                        o = ps_m[:, t * DIM:(t + 1) * DIM]
                        pe.matmul(o, atT[:, t * P:(t + 1) * P], w_outT[:, :], start=True, stop=False)
                        m = pe.matmul(o, ones_row[0:1, :], b_out[0:1, :], start=False, stop=True)
                    m.then_inc(s_["o_done"], 1)
                    pe.wait_ge(s_["x1_made"], r + 1)
                    pe.wait_ge(s_["x1n_made"], r + 1)
                    for t in range(S):
                        m = pe.transpose(ps_m[:, t * P:(t + 1) * P], x1n[:, t, :], ident[:, :])
                    m.then_inc(s_["x1n_turned"], 1)
                    pe.wait_ge(s_["x1T_made"], r + 1)
                    for ch in range(FC):
                        if ch < 2:
                            pe.wait_ge(s_["kf_made"], UT * (b + 1))
                        need(pe, s_["gelu_made"], FC * r + ch - 1)
                        pe.matmul(ps_u[ch % 2][:, :], w1T[:, ch * P:(ch + 1) * P], x1T[:, :], start=True, stop=True).then_inc(s_["up_done"], 1)
                    pe.wait_ge(s_["gelu_made"], FC * (r + 1))
                    for t in range(S):
                        o = ps_m[:, t * DIM:(t + 1) * DIM]
                        for ch in range(FC):
                            pe.matmul(o, hT[:, ch, t * P:(t + 1) * P], w2T[:, ch, :], start=(ch == 0), stop=False)
                        m = pe.matmul(o, ones_row[0:1, :], b2[0:1, :], start=False, stop=True)
                    m.then_inc(s_["down_done"], 1)
            body(0)
            with pe.Fori(1, SEQS) as b:
                body(b)


def local_transformer(nc, sb, sem, bank, ident, x, out, c):
    LAYERS, DIM, FF2 = c["W1"].shape
    FF = FF2 // 2
    INNER = c["Wo"].shape[1]
    HD = c["q_scale"].shape[1]
    H = INNER // HD
    PAIRS = TILES // 2
    SEQS = TILES // SEQ_TILES
    BP = 4
    WIN = 32
    KW = P + WIN
    HALF = DIM // 2
    CH = [(0, 128), (128, 128), (256, FF - 256)]
    NB = LAYERS * PAIRS

    XA = sb("layer_x", [P, TILES, DIM])
    wqk = sb("wqk", [P, 2 * INNER])
    wv = sb("wv", [P, INNER])
    wo = sb("wo", [P, INNER // P, DIM])
    w1 = sb("w1", [P, FF2])
    w2 = sb("w2", [P, 3, DIM])
    rope_c = sb("rope_const", [P, 8, 4, HD])
    qk_scales = sb("qk_scales", [P, LAYERS, 4, HD])
    ln_g = sb("ln_g_col", [P, LAYERS])
    ln_b = sb("ln_b_col", [P, LAYERS])
    b1_col = sb("b1_col", [P, LAYERS, 2, 3])
    b2_row = sb("b2_row", [P, LAYERS, DIM])
    mask = sb("mask", [P, 5, KW + 1])
    mask_now = sb("mask_now", [P, KW + 1])
    flag = sb("flag", [P, 4])
    neg_half = sb("neg_half", [P, 32])

    xc = sb("x_now", [P, 2, DIM])
    tab = sb("rope_tab", [P, 2, 4, HD])
    xsT = sb("x_shift_T", [P, 2, P])
    carry_a = sb("carry_attn", [P, 2])
    sq = sb("squares", [P, 4 * 512])
    t1 = sb("qk_roped", [P, 2, 2 * INNER])
    t2 = sb("rope_sin_part", [P, 2 * INNER])
    V = sb("v", [P, 2, INNER])
    ss = sb("sumsq", [P, 2, 2 * H])
    ssc = sb("sumsq_clamped", [P, 2, 2 * H])
    rn = sb("inv_norm", [P, 2, 2 * H])
    rq8 = sb("q_logit_scale", [P, 2, H])
    qT = sb("qT", [P, 2, H // 2, P])
    kT = sb("kT", [P, 2, H // 2, KW])
    Sm = sb("masked_scores", [P, H, KW])
    mx = sb("row_max", [P, 2, H])
    nb = sb("neg_max", [P, 2, H])
    PR = sb("probs", [P, 2, H, KW])
    den = sb("denoms", [P, 2, H])
    rden = sb("inv_denoms", [P, 2, H])
    PT = sb("probs_T", [P, H, P])
    PTp = sb("probs_T_prev", [P, H, WIN])
    On = sb("attn_out", [P, INNER])
    OT = sb("attn_out_T", [P, INNER // P, P])
    xm = sb("x_mid", [P, 2, DIM])
    xmb = sb("x_mid_plus_b2", [P, 2, DIM])
    xmT = sb("x_mid_shift_T", [P, 2, P])
    carry_m = sb("carry_ffn", [P, 2])
    st = sb("ln_stats", [P, 2, 6])
    mv = sb("ln_mean_var", [P, 2, 2])
    ve = sb("ln_var_eps", [P, 2])
    rstd = sb("ln_rstd", [P, 2])
    z = sb("ln_out", [P, 2, DIM])
    zT = sb("ln_out_T", [P, 2, P])
    gel = sb("gelu_gate", [P, 2, 3, P])
    hT = sb("hidden_T", [P, 2, 3, P])

    psQ, psT, psS, psD = bank[0:2], bank[2:4], bank[4:6], bank[6:8]

    consts_loaded = sem("consts_loaded")
    wqk_loaded, wv_loaded, wo_loaded, w1_loaded, w2_loaded = sem("wqk_loaded"), sem("wv_loaded"), sem("wo_loaded"), sem("w1_loaded"), sem("w2_loaded")
    cleared = sem("cleared")
    mask_picked = sem("mask_picked")
    xa_written = sem("xa_written")
    x_copied, tab_made, x_turned, xs_ready, carry_saved = sem("x_copied"), sem("tab_made"), sem("x_turned"), sem("xs_ready"), sem("carry_saved")
    qk_done, v_done, sq_made, v_copied = sem("qk_done"), sem("v_done"), sem("sq_made"), sem("v_copied")
    rope_terms, u_made, ss_made, ss_clamped, rn_made, kn_made = (sem(n) for n in ("rope_terms", "u_made", "ss_made", "ss_clamped", "rn_made", "kn_made"))
    qk_turned, qT_copied, kT_copied, kprev_copied = sem("qk_turned"), sem("qT_copied"), sem("kT_copied"), sem("kprev_copied")
    scores_done, sm_made, rq8_made, nb_made, p_made, rden_made = (sem(n) for n in ("scores_done", "sm_made", "rq8_made", "nb_made", "p_made", "rden_made"))
    p_turned, pt_act, pt_dve, av_done, o_normed, o_turned, o_copied, y_done, xm_made = (sem(n) for n in (
        "p_turned", "pt_act", "pt_dve", "av_done", "o_normed", "o_turned", "o_copied", "y_done", "xm_made"))
    xm_turned, xmT_ready, carry_m_saved, xmb_made, xs2_turned = (sem(n) for n in ("xm_turned", "xmT_ready", "carry_m_saved", "xmb_made", "xs2_turned"))
    stats_made, mv_made, ve_made, rstd_made, z_made, z_turned, zT_made = (sem(n) for n in ("stats_made", "mv_made", "ve_made", "rstd_made", "z_made", "z_turned", "zT_made"))
    ff_done, gelu_made, h_made, y2_done = sem("ff_done"), sem("gelu_made"), sem("h_made"), sem("y2_done")
    stored = sem("stored")

    summed = sem("summed")
    ln = TileNorm(sb, sem, "loc_ln", tiles_of(x, 4), 4, ident, None, dest=tiles_of(XA, 4))
    const_dma = [0]

    T_RING = [
        ("turn_qk0", 1, [(qT_copied, 2, 1)]),
        ("turn_o0", 3, [(o_copied, 2, 1)]),
        ("turn_x", 0, [(xs_ready, 3, 3), (carry_saved, 1, 1)]),
        ("turn_o1", 3, [(o_copied, 2, 2)]),
        ("turn_p0", 2, [(pt_act, 2, 1)]),
        ("turn_qk1", 1, [(qT_copied, 2, 2)]),
        ("turn_qk2", 1, [(kT_copied, 2, 1)]),
        ("turn_qk3", 1, [(kT_copied, 2, 2)]),
        ("turn_p1", 2, [(pt_dve, 3, 1)]),
        ("turn_p2", 2, [(pt_act, 2, 2)]),
        ("turn_p3", 2, [(pt_dve, 3, 2)]),
        ("turn_p4", 2, [(pt_dve, 3, 3)])]
    Q_RING = [
        ("values0", 2, [(v_copied, 2, 1)]),
        ("values1", 2, [(v_copied, 2, 2)]),
        ("qk0", 0, [(sq_made, 4, 1), (rope_terms, 4, 1)]),
        ("project", 3, [(xm_made, 1, 1)]),
        ("qk1", 0, [(sq_made, 4, 2), (rope_terms, 4, 2)]),
        ("ffn_down", 4, [(xa_written, 1, TILES + 1)]),
        ("qk2", 0, [(sq_made, 4, 3), (rope_terms, 4, 3)]),
        ("qk3", 0, [(sq_made, 4, 4), (rope_terms, 4, 4)]),
        ("attend0", 2, [(o_normed, 2, 1)]),
        ("attend1", 2, [(o_normed, 2, 2)])]
    S_RING = [
        ("scores0", 1, [(sm_made, 6, 1)]),
        ("scores1", 1, [(sm_made, 6, 2)]),
        ("scores2", 1, [(sm_made, 6, 3)]),
        ("scores3", 1, [(sm_made, 6, 4)]),
        ("scores4", 1, [(sm_made, 6, 5)]),
        ("scores5", 1, [(sm_made, 6, 6)])]
    RINGS = ((T_RING, psT), (Q_RING, psQ), (S_RING, psS))
    BANK = {use: banks[i % 2] for ring, banks in RINGS for i, (use, _, _) in enumerate(ring)}
    S_GROUPS = [(0, 2, 4), (1, 3, 5), (6, 8, 10), (7, 9, 11), (12, 14), (13, 15)]
    NT = LAYERS * TILES

    def behind(n, p, lag):
        return n + (p - lag) // 2, (p - lag) % 2

    def is_tile(m, par):
        return not isinstance(m, int) or 0 <= 2 * m + par < NT

    def free_bank(pe, ring, use, n, p):
        i = [name for name, _, _ in ring].index(use)
        for j in range(i - 2, i - 2 - 4 * len(ring), -2):
            _, lag, emptied = ring[j % len(ring)]
            m, par = behind(n, p, lag - j // len(ring))
            if is_tile(m, par):
                for s, k, signal in emptied:
                    pe.wait_ge(s, k * (2 * m + par) + signal)
                return

    def in_steps(eng, step):
        for n in range(3):
            step(n, 0)
            step(n, 1)
        with eng.Fori(3, NB - 1) as n:
            step(n, 0)
            step(n, 1)
        for n in range(NB - 1, NB + 2):
            step(n, 0)
            step(n, 1)

    def on(stage, n, p, lag, *more):
        m, par = behind(n, p, lag)
        if is_tile(m, par):
            stage(m, par, *more)

    with nc.Block() as block:
        @block.sync
        def _(sp):
            def load(dst, src):
                const_dma[0] += 1
                sp.dma_start(dst, src).then_inc(consts_loaded, 16)
            load(rope_c[:, :, :, :], c["rope_const"])
            for k, (name, lo) in enumerate((("q_scale", 0), ("q_scale", 1), ("k_scale", 0), ("k_scale", 1))):
                src = c[name].partition_broadcast(P)
                if lo == 0:
                    load(qk_scales[:, :, k, :], src)
                else:
                    load(qk_scales[:, :, k, 0:HD // 2], src[:, :, HD // 2:HD])
                    load(qk_scales[:, :, k, HD // 2:HD], src[:, :, 0:HD // 2])
            with nc.allow_non_contiguous_dma("small columns"):
                load(ln_g[:, :], c["ln_g"].rearrange("l d -> d l"))
                load(ln_b[:, :], c["ln_b"].rearrange("l d -> d l"))
                for half in range(2):
                    for ch, (lo, w) in enumerate(CH):
                        load(b1_col[0:w, :, half, ch], c["b1"][:, half * FF + lo:half * FF + lo + w].rearrange("l d -> d l"))
            load(b2_row[:, :, :], c["b2"].partition_broadcast(P))
            load(mask[:, :, :], c["mask"])
            load(flag[:, :], c["flag"])

            def load_wqk(l):
                sp.dma_start(wqk[:, :], c["Wqkv"][bass.ds(l, 1), :, 0:2 * INNER].rearrange("a k n -> k (a n)")).then_inc(wqk_loaded, 16)

            def load_wv(l):
                sp.dma_start(wv[:, :], c["Wqkv"][bass.ds(l, 1), :, 2 * INNER:3 * INNER].rearrange("a k n -> k (a n)")).then_inc(wv_loaded, 16)

            def load_wo(l):
                sp.dma_start(wo[:, :, :], c["Wo"][bass.ds(l, 1), :, :].rearrange("a (k p) n -> p (a k) n", p=P)).then_inc(wo_loaded, 16)

            def load_w1(l):
                sp.dma_start(w1[:, :], c["W1"][bass.ds(l, 1), :, :].rearrange("a k n -> k (a n)")).then_inc(w1_loaded, 16)

            def load_w2(l):
                sp.dma_start(w2[:, 0:2, :], c["W2"][bass.ds(l, 1), 0:256, :].rearrange("a (k p) n -> p (a k) n", p=P)).then_inc(w2_loaded, 16)
                sp.dma_start(w2[0:FF - 256, 2, :], c["W2"][bass.ds(l, 1), 256:FF, :].rearrange("a k n -> k (a n)")).then_inc(w2_loaded, 16)

            for load_it in (load_wqk, load_wv, load_wo, load_w1, load_w2):
                load_it(0)
            with sp.Fori(1, LAYERS) as l:
                for used, k, load_it in ((qk_done, 4, load_wqk), (v_done, 2, load_wv), (y_done, 1, load_wo), (ff_done, 1, load_w1), (y2_done, 1, load_w2)):
                    sp.wait_ge(used, k * TILES * l)
                    load_it(l)
            outs = out.rearrange("b (t p) d -> p b t d", p=P)
            for b in range(SEQS):
                sp.wait_ge(summed, b + 1)
                sp.dma_start(outs[:, b, :, :], XA[:, b * SEQ_TILES:(b + 1) * SEQ_TILES, :]).then_inc(stored, 16)
            sp.wait_ge(stored, 16 * SEQS)

        @block.gpsimd
        def _(pool):
            ln.on_pool_start(pool)
            with pool.Fori(0, TILES // 4) as n:
                ln.on_pool(pool, n)
            pool.memset(V[:, 1, :], 0.0)
            pool.memset(kT[:, 1, :, P - WIN:P], 0.0)
            pool.memset(carry_a[:, :], 0.0)
            pool.memset(carry_m[:, :], 0.0)
            pool.memset(neg_half[:, :], -0.5).then_inc(cleared, 1)
            pool.wait_ge(cleared, 1)
            pool.wait_ge(consts_loaded, 16 * const_dma[0])

            def fetch(n, par):
                T = 2 * n + par
                t = (n % PAIRS) * 2 + par
                need(pool, xa_written, T + 1)
                need(pool, x_turned, T - 1)
                apart(pool)
                pool.tensor_copy(xc[:, par, :], XA[:, bass.ds(t, 1), :]).then_inc(x_copied, 1)
                need(pool, rope_terms, 4 * (T - 1))
                apart(pool)
                pool.tensor_tensor(tab[:, par, :, :], rope_c[:, bass.ds((n % BP) * 2 + par, 1), :, :].rearrange("p a k d -> p (a k) d"),
                                   qk_scales[:, bass.ds(n // PAIRS, 1), :, :].rearrange("p a k d -> p (a k) d"), ALU.mult).then_inc(tab_made, 1)

            def pick_mask(n, par):
                if par == 1:
                    return
                need(pool, sm_made, 6 * (2 * n - 1))
                apart(pool)
                pool.tensor_copy(mask_now[:, :], mask[:, bass.ds(n % BP, 1), :].rearrange("p a k -> p (a k)")).then_inc(mask_picked, 1)

            def rope_sum(n, par, j):
                T = 2 * n + par
                pool.wait_ge(rope_terms, 4 * T + 2 * j + 2)
                part = slice(j * INNER, (j + 1) * INNER)
                pool.tensor_tensor(t1[:, par, part], t1[:, par, part], t2[:, part], ALU.add).then_inc(u_made, 1)

            def norms(n, par):
                T = 2 * n + par
                pool.wait_ge(ss_made, T + 1)
                apart(pool)
                pool.tensor_scalar(ssc[:, par, :], ss[:, par, :], 1e-24, None, ALU.max).then_inc(ss_clamped, 1)
                pool.wait_ge(ss_clamped, T + 1)
                need(pool, kn_made, T - 1)
                pool.tensor_tensor(rn[:, par, :], ssc[:, par, :], neg_half[:, :], ALU.pow).then_inc(rn_made, 1)

            def k_prev(n, par):
                T = 2 * n + par
                need(pool, kT_copied, 2 * T)
                need(pool, scores_done, 6 * (T - 1))
                apart(pool)
                if par == 0:
                    pool.wait_ge(mask_picked, n + 1)
                    apart(pool)
                    pool.tensor_scalar(kT[:, par, :, P:KW], kT[:, 1, :, P - WIN:P], mask_now[:, KW:KW + 1], None, ALU.mult).then_inc(kprev_copied, 1)
                else:
                    pool.tensor_copy(kT[:, par, :, P:KW], kT[:, 0, :, P - WIN:P]).then_inc(kprev_copied, 1)

            def add_b2(n, par):
                U = 2 * n + par
                pool.wait_ge(xm_made, U + 1)
                need(pool, xa_written, TILES + U - 1)
                apart(pool)
                pool.tensor_tensor(xmb[:, par, :], xm[:, par, :], b2_row[:, bass.ds(n // PAIRS, 1), :].rearrange("p a d -> p (a d)"),
                                   ALU.add).then_inc(xmb_made, 1)

            def ln_rstd(n, par):
                U = 2 * n + par
                pool.wait_ge(mv_made, U + 1)
                apart(pool)
                pool.tensor_scalar(ve[:, par:par + 1], mv[:, par, 1:2], 1e-5, None, ALU.add).then_inc(ve_made, 1)
                pool.wait_ge(ve_made, U + 1)
                need(pool, z_made, U - 1)
                pool.tensor_tensor(rstd[:, par:par + 1], ve[:, par:par + 1], neg_half[:, 0:1], ALU.pow).then_inc(rstd_made, 1)

            def step(n, p):
                on(norms, n, p, 2)
                on(add_b2, n, p, 4)
                on(pick_mask, n, p, 2)
                on(k_prev, n, p, 2)
                on(rope_sum, n, p, 1, 0)
                on(ln_rstd, n, p, 4)
                on(fetch, n, p, 0)
                on(rope_sum, n, p, 1, 1)

            in_steps(pool, step)

        @block.scalar
        def _(act):
            act.wait_ge(cleared, 1)
            act.wait_ge(consts_loaded, 16 * const_dma[0])

            def shift(n, par, T, ps, dst, carry, ready, saved):
                act.activation(dst[0:HALF, par, :], ps[0:HALF, 0:P], ACT.Copy).then_inc(ready, 1)
                act.activation(dst[HALF:P, par, 1:P], ps[HALF:P, 0:P - 1], ACT.Copy).then_inc(ready, 1)
                need(act, saved, T)
                if par == 0:
                    apart(act)
                    act.activation(dst[HALF:P, par, 0:1], carry[HALF:P, 1:2], ACT.Copy, scale=flag[HALF:P, bass.ds(n % BP, 1)]).then_inc(ready, 1)
                else:
                    act.activation(dst[HALF:P, par, 0:1], carry[HALF:P, 0:1], ACT.Copy).then_inc(ready, 1)
                need(act, ready, 3 * T)
                act.activation(carry[HALF:P, par:par + 1], ps[HALF:P, P - 1:P], ACT.Copy).then_inc(saved, 1)

            def attn_in(n, par):
                T = 2 * n + par
                act.wait_ge(x_turned, T + 1)
                need(act, v_done, 2 * (T - 1))
                shift(n, par, T, BANK["turn_x"], xsT, carry_a, xs_ready, carry_saved)

            def square(n, par, j):
                T = 2 * n + par
                if j == 0:
                    need(act, ss_made, T)
                act.wait_ge(qk_done, 4 * T + j + 1)
                act.activation(sq[:, j * 512:(j + 1) * 512], BANK[f"qk{j}"][:, :], ACT.Square).then_inc(sq_made, 1)

            def evac_v(n, par, j):
                T = 2 * n + par
                if j == 0:
                    need(act, av_done, 2 * T)
                act.wait_ge(v_done, 2 * T + j + 1)
                act.activation(V[:, par, j * 512:(j + 1) * 512], BANK[f"values{j}"][:, :], ACT.Copy).then_inc(v_copied, 1)

            def evac_q(n, par, j):
                T = 2 * n + par
                if j == 0:
                    need(act, scores_done, 6 * (T - 1))
                act.wait_ge(qk_turned, 4 * T + j + 1)
                act.activation(qT[:, par, 4 * j:4 * j + 4, :], BANK[f"turn_qk{j}"].rearrange("p (a b) -> p a b", b=P), ACT.Copy).then_inc(qT_copied, 1)

            def exps(n, par, q):
                T = 2 * n + par
                if q == 0:
                    act.wait_ge(nb_made, T + 1)
                    need(act, p_turned, 5 * (T - 1))
                    need(act, rden_made, T - 1)
                for h in range(4 * q, 4 * q + 4):
                    e = act.activation(PR[:, par, h, :], Sm[:, h, :], ACT.Exp, bias=nb[:, par, h:h + 1],
                                       scale=rq8[:, par, h:h + 1], accum_out=den[:, par, h:h + 1])
                e.then_inc(p_made, 1)

            def evac_p(n, par, q):
                T = 2 * n + par
                need(act, av_done, 2 * T)
                act.wait_ge(p_turned, 5 * T + q + 1)
                act.activation(PT[:, 4 * q:4 * q + 4, :], BANK[f"turn_p{q}"].rearrange("p (a b) -> p a b", b=P), ACT.Copy).then_inc(pt_act, 1)

            def evac_o(n, par, j):
                T = 2 * n + par
                need(act, y_done, T)
                act.wait_ge(o_turned, 2 * T + j + 1)
                act.activation(OT[:, 4 * j:4 * j + 4, :], BANK[f"turn_o{j}"].rearrange("p (a b) -> p a b", b=P), ACT.Copy).then_inc(o_copied, 1)

            def ffn_in(n, par):
                U = 2 * n + par
                act.wait_ge(xm_turned, U + 1)
                need(act, xs2_turned, U - 1)
                shift(n, par, U, psD[0], xmT, carry_m, xmT_ready, carry_m_saved)

            def evac_z(n, par):
                U = 2 * n + par
                act.wait_ge(z_turned, U + 1)
                need(act, ff_done, U - 1)
                apart(act)
                act.activation(zT[:, par, :], psD[0][:, 2 * P:3 * P], ACT.Identity, scale=ln_g[:, bass.ds(n // PAIRS, 1)],
                               bias=ln_b[:, bass.ds(n // PAIRS, 1)]).then_inc(zT_made, 1)

            def gelu(n, par):
                U = 2 * n + par
                need(act, h_made, 3 * (U - 1))
                act.wait_ge(ff_done, U + 1)
                apart(act)
                for ch, (lo, w) in enumerate(CH):
                    act.activation(gel[0:w, par, ch, :], psD[1][0:w, ch * P:(ch + 1) * P], ACT.Gelu,
                                   bias=b1_col[0:w, bass.ds(n // PAIRS, 1), 1, ch]).then_inc(gelu_made, 1)

            def step(n, p):
                on(evac_v, n, p, 2, 0)
                on(evac_o, n, p, 3, 0)
                on(attn_in, n, p, 0)
                on(evac_o, n, p, 3, 1)
                on(evac_v, n, p, 2, 1)
                on(square, n, p, 0, 0)
                on(evac_p, n, p, 2, 0)
                on(exps, n, p, 2, 1)
                on(square, n, p, 0, 1)
                on(evac_q, n, p, 1, 1)
                on(ffn_in, n, p, 3)
                on(exps, n, p, 2, 2)
                on(exps, n, p, 2, 3)
                on(evac_p, n, p, 2, 2)
                on(square, n, p, 0, 2)
                on(evac_z, n, p, 3)
                on(square, n, p, 0, 3)
                on(gelu, n, p, 3)
                on(exps, n, p, 1, 0)
                on(evac_q, n, p, 0, 0)

            in_steps(act, step)

        @block.vector
        def _(dve):
            with dve.Fori(0, TILES // 4) as n:
                ln.on_dve(dve, n, lambda e, n: None)
            dve.wait_ge(ln.z_made, TILES)
            dve.sem_inc(xa_written, TILES)
            dve.wait_ge(cleared, 1)
            dve.wait_ge(consts_loaded, 16 * const_dma[0])

            def rope(n, par, j):
                T = 2 * n + par
                if j == 0:
                    dve.wait_ge(tab_made, T + 1)
                    need(dve, u_made, 2 * T)
                    need(dve, qk_turned, 4 * (T - 1))
                k = 2 * (j // 2)
                HH = HD // 2
                dve.wait_ge(sq_made, 4 * T + j + 1)
                src = BANK[f"qk{j}"].rearrange("p (h d) -> p h d", d=HD)
                o1 = t1[:, par, j * 512:(j + 1) * 512].rearrange("p (h d) -> p h d", d=HD)
                o2 = t2[:, j * 512:(j + 1) * 512].rearrange("p (h d) -> p h d", d=HD)
                dve.tensor_tensor(o1, src, tab[:, par, k, :].unsqueeze(1).to_broadcast([P, 8, HD]), ALU.mult)
                dve.tensor_tensor(o2[:, :, 0:HH], src[:, :, HH:HD], tab[:, par, k + 1, 0:HH].unsqueeze(1).to_broadcast([P, 8, HH]), ALU.mult)
                dve.tensor_tensor(o2[:, :, HH:HD], src[:, :, 0:HH], tab[:, par, k + 1, HH:HD].unsqueeze(1).to_broadcast([P, 8, HH]),
                                  ALU.mult).then_inc(rope_terms, 1)

            def sumsq(n, par):
                T = 2 * n + par
                dve.wait_ge(sq_made, 4 * T + 4)
                need(dve, ss_clamped, T - 1)
                dve.tensor_reduce(ss[:, par, :], sq[:, :].rearrange("p (h d) -> p h d", d=HD), AX.X, ALU.add).then_inc(ss_made, 1)

            def k_norm(n, par):
                T = 2 * n + par
                dve.wait_ge(rn_made, T + 1)
                need(dve, nb_made, T - 1)
                need(dve, p_made, 4 * (T - 1))
                dve.tensor_scalar(rq8[:, par, :], rn[:, par, 0:H], 8.0, None, ALU.mult).then_inc(rq8_made, 1)
                dve.wait_ge(u_made, 2 * T + 2)
                dve.tensor_tensor(t1[:, par, INNER:2 * INNER].rearrange("p (h d) -> p h d", d=HD), t1[:, par, INNER:2 * INNER].rearrange("p (h d) -> p h d", d=HD),
                                  rn[:, par, H:2 * H].unsqueeze(2).to_broadcast([P, H, HD]), ALU.mult).then_inc(kn_made, 1)

            def evac_k(n, par, j):
                T = 2 * n + par
                if j == 0:
                    need(dve, kprev_copied, T)
                dve.wait_ge(qk_turned, 4 * T + j + 3)
                dve.tensor_copy(kT[:, par, 4 * j:4 * j + 4, 0:P], BANK[f"turn_qk{j + 2}"].rearrange("p (a b) -> p a b", b=P)).then_inc(kT_copied, 1)

            def masked(n, par, g):
                T = 2 * n + par
                if g == 0:
                    need(dve, p_made, 4 * T)
                    dve.wait_ge(mask_picked, n + 1)
                m = mask_now[:, 0:KW] if par == 0 else mask[:, 4, 0:KW]
                dve.wait_ge(scores_done, 6 * T + g + 1)
                apart(dve)
                for i, h in enumerate(S_GROUPS[g]):
                    e = dve.tensor_tensor_reduce(out=Sm[:, h, :], in0=BANK[f"scores{g}"][:, i * KW:(i + 1) * KW], in1=m, scale=1.0, scalar=-3e38,
                                                 op0=ALU.add, op1=ALU.max, accum_out=mx[:, par, h:h + 1])
                e.then_inc(sm_made, 1)

            def neg_max(n, par):
                T = 2 * n + par
                dve.wait_ge(sm_made, 6 * T + 6)
                dve.wait_ge(rq8_made, T + 1)
                dve.scalar_tensor_tensor(nb[:, par, :], mx[:, par, :], -1.0, rq8[:, par, :], ALU.mult, ALU.mult).then_inc(nb_made, 1)

            def evac_p(n, par, q):
                T = 2 * n + par
                need(dve, av_done, 2 * T)
                dve.wait_ge(p_turned, 5 * T + q + 1)
                ps = BANK[f"turn_p{q}"]
                if q < 4:
                    dve.tensor_copy(PT[:, 4 * q:4 * q + 4, :], ps.rearrange("p (a b) -> p a b", b=P)).then_inc(pt_dve, 1)
                else:
                    dve.tensor_copy(PTp[P - WIN:P, :, :], ps[P - WIN:P, :].rearrange("p (a b) -> p a b", b=WIN)).then_inc(pt_dve, 1)

            def inv_den(n, par):
                T = 2 * n + par
                dve.wait_ge(p_made, 4 * T + 4)
                dve.reciprocal(rden[:, par, :], den[:, par, :]).then_inc(rden_made, 1)

            def normalise(n, par, j):
                T = 2 * n + par
                dve.wait_ge(rden_made, T + 1)
                dve.wait_ge(av_done, 2 * T + j + 1)
                need(dve, o_turned, 2 * (T - 1) + j + 1)
                dve.tensor_tensor(On[:, j * 512:(j + 1) * 512].rearrange("p (h d) -> p h d", d=HD),
                                  BANK[f"attend{j}"].rearrange("p (h d) -> p h d", d=HD),
                                  rden[:, par, 8 * j:8 * j + 8].unsqueeze(2).to_broadcast([P, 8, HD]), ALU.mult).then_inc(o_normed, 1)

            def residual(n, par):
                T = 2 * n + par
                dve.wait_ge(y_done, T + 1)
                need(dve, xm_turned, T - 1)
                need(dve, xmb_made, T - 1)
                dve.tensor_tensor(xm[:, par, :], BANK["project"][:, 0:DIM], XA[:, bass.ds((n % PAIRS) * 2 + par, 1), :].rearrange("p a d -> p (a d)"),
                                  ALU.add).then_inc(xm_made, 1)

            def ln_stats(n, par):
                U = 2 * n + par
                dve.wait_ge(xs2_turned, U + 1)
                dve.bn_stats(st[:, par, :], psD[0][:, P:2 * P]).then_inc(stats_made, 1)
                dve.wait_ge(stats_made, U + 1)
                need(dve, ve_made, U - 1)
                apart(dve)
                dve.bn_aggr(mv[:, par, :], st[:, par, :]).then_inc(mv_made, 1)

            def ln_apply(n, par):
                U = 2 * n + par
                dve.wait_ge(rstd_made, U + 1)
                need(dve, z_turned, U - 1)
                dve.tensor_scalar(z[:, par, :], psD[0][:, P:2 * P], mv[:, par, 0:1], rstd[:, par:par + 1], ALU.subtract, ALU.mult).then_inc(z_made, 1)

            def gate(n, par):
                U = 2 * n + par
                need(dve, y2_done, U - 1)
                for ch, (lo, w) in enumerate(CH):
                    dve.wait_ge(gelu_made, 3 * U + ch + 1)
                    dve.scalar_tensor_tensor(hT[0:w, par, ch, :], psD[0][0:w, ch * P:(ch + 1) * P], b1_col[0:w, bass.ds(n // PAIRS, 1), 0, ch],
                                             gel[0:w, par, ch, :], ALU.add, ALU.mult).then_inc(h_made, 1)

            def ffn_out(n, par):
                U = 2 * n + par
                dve.wait_ge(y2_done, U + 1)
                dve.wait_ge(xmb_made, U + 1)
                dve.tensor_tensor(XA[:, bass.ds((n % PAIRS) * 2 + par, 1), :].rearrange("p a d -> p (a d)"), BANK["ffn_down"][:, 0:DIM], xmb[:, par, :],
                                  ALU.add).then_inc(xa_written, 1)

            def step(n, p):
                on(masked, n, p, 2, 1)
                on(rope, n, p, 1, 2)
                on(masked, n, p, 2, 2)
                on(masked, n, p, 2, 3)
                on(evac_p, n, p, 3, 3)
                on(evac_p, n, p, 3, 4)
                on(masked, n, p, 2, 4)
                on(rope, n, p, 1, 3)
                on(masked, n, p, 2, 5)
                on(inv_den, n, p, 3)
                on(neg_max, n, p, 2)
                on(normalise, n, p, 3, 0)
                on(sumsq, n, p, 1)
                on(normalise, n, p, 3, 1)
                on(gate, n, p, 4)
                on(rope, n, p, 0, 0)
                on(residual, n, p, 3)
                on(k_norm, n, p, 1)
                on(rope, n, p, 0, 1)
                on(evac_k, n, p, 1, 0)
                on(evac_k, n, p, 1, 1)
                on(ffn_out, n, p, 4)
                on(ln_stats, n, p, 3)
                on(evac_p, n, p, 2, 1)
                on(ln_apply, n, p, 3)
                on(masked, n, p, 1, 0)

            in_steps(dve, step)
            dve.wait_ge(xa_written, TILES + 2 * NB)
            for b in range(SEQS):
                part = slice(b * SEQ_TILES, (b + 1) * SEQ_TILES)
                dve.tensor_tensor(XA[:, part, :], XA[:, part, :], x[:, part, :], ALU.add).then_inc(summed, 1)

        @block.tensor
        def _(pe):
            pe.wait_ge(cleared, 1)
            pe.wait_ge(consts_loaded, 16 * const_dma[0])

            def turn_x(m, par, n, p):
                T = 2 * m + par
                pe.wait_ge(x_copied, T + 1)
                free_bank(pe, T_RING, "turn_x", n, p)
                pe.transpose(BANK["turn_x"][:, 0:P], xc[:, par, :], ident[:, :]).then_inc(x_turned, 1)

            def qk(m, par, n, p, j):
                T = 2 * m + par
                if j == 0:
                    pe.wait_ge(xs_ready, 3 * T + 3)
                    pe.wait_ge(wqk_loaded, 16 * (m // PAIRS + 1))
                free_bank(pe, Q_RING, f"qk{j}", n, p)
                pe.matmul(BANK[f"qk{j}"][:, :], xsT[:, par, :], wqk[:, j * 512:(j + 1) * 512], start=True, stop=True).then_inc(qk_done, 1)

            def values(m, par, n, p, j):
                if j == 0:
                    pe.wait_ge(wv_loaded, 16 * (m // PAIRS + 1))
                free_bank(pe, Q_RING, f"values{j}", n, p)
                pe.matmul(BANK[f"values{j}"][:, :], xsT[:, par, :], wv[:, j * 512:(j + 1) * 512], start=True, stop=True).then_inc(v_done, 1)

            def turn_qk(m, par, n, p, j):
                T = 2 * m + par
                if j == 0:
                    pe.wait_ge(u_made, 2 * T + 1)
                if j == 2:
                    pe.wait_ge(kn_made, T + 1)
                free_bank(pe, T_RING, f"turn_qk{j}", n, p)
                for i in range(4):
                    col = (j // 2) * INNER + (4 * (j % 2) + i) * P
                    e = pe.transpose(BANK[f"turn_qk{j}"][:, i * P:(i + 1) * P], t1[:, par, col:col + P], ident[:, :])
                e.then_inc(qk_turned, 1)

            def scores(m, par, n, p, g):
                T = 2 * m + par
                if g == 0:
                    pe.wait_ge(qT_copied, 2 * T + 2)
                    pe.wait_ge(kT_copied, 2 * T + 2)
                    pe.wait_ge(kprev_copied, T + 1)
                free_bank(pe, S_RING, f"scores{g}", n, p)
                for i, h in enumerate(S_GROUPS[g]):
                    r = slice(HD * (h % 2), HD * (h % 2) + HD)
                    e = pe.matmul(BANK[f"scores{g}"][:, i * KW:(i + 1) * KW], qT[r, par, h // 2, :], kT[r, par, h // 2, :], start=True, stop=True)
                e.then_inc(scores_done, 1)

            def turn_p(m, par, n, p, q):
                T = 2 * m + par
                ps = BANK[f"turn_p{q}"]
                if q < 4:
                    pe.wait_ge(p_made, 4 * T + q + 1)
                free_bank(pe, T_RING, f"turn_p{q}", n, p)
                if q < 4:
                    for i in range(4):
                        e = pe.transpose(ps[:, i * P:(i + 1) * P], PR[:, par, 4 * q + i, 0:P], ident[:, :])
                else:
                    apart(pe)
                    for h in range(H):
                        e = pe.transpose(ps[:, h * WIN:(h + 1) * WIN], PR[0:WIN, par, h, WIN:KW], ident[0:WIN, 0:WIN])
                e.then_inc(p_turned, 1)

            def attend(m, par, n, p, j):
                T = 2 * m + par
                if j == 0:
                    pe.wait_ge(v_copied, 2 * T + 2)
                    pe.wait_ge(pt_dve, 3 * T + 3)
                    pe.wait_ge(pt_act, 2 * T + 2)
                free_bank(pe, Q_RING, f"attend{j}", n, p)
                for i in range(8):
                    h = 8 * j + i
                    pe.matmul(BANK[f"attend{j}"][:, i * HD:(i + 1) * HD], PT[:, h, :], V[:, par, h * HD:(h + 1) * HD],
                              start=(i == 0), stop=True, skip_group_check=(i > 0))
                for i in range(8):
                    h = 8 * j + i
                    e = pe.matmul(BANK[f"attend{j}"][0:WIN, i * HD:(i + 1) * HD], PTp[P - WIN:P, h, :], V[P - WIN:P, 1 - par, h * HD:(h + 1) * HD],
                                  start=False, stop=True, skip_group_check=True)
                e.then_inc(av_done, 1)

            def turn_o(m, par, n, p, j):
                T = 2 * m + par
                pe.wait_ge(o_normed, 2 * T + j + 1)
                free_bank(pe, T_RING, f"turn_o{j}", n, p)
                for i in range(4):
                    col = (4 * j + i) * P
                    e = pe.transpose(BANK[f"turn_o{j}"][:, i * P:(i + 1) * P], On[:, col:col + P], ident[:, :])
                e.then_inc(o_turned, 1)

            def project(m, par, n, p):
                T = 2 * m + par
                pe.wait_ge(wo_loaded, 16 * (m // PAIRS + 1))
                free_bank(pe, Q_RING, "project", n, p)
                for k in range(INNER // P):
                    if k % 4 == 0:
                        pe.wait_ge(o_copied, 2 * T + k // 4 + 1)
                    e = pe.matmul(BANK["project"][:, 0:DIM], OT[:, k, :], wo[:, k, :], start=(k == 0), stop=(k == INNER // P - 1))
                e.then_inc(y_done, 1)

            def turn_xm(m, par, n, p):
                U = 2 * m + par
                pe.wait_ge(xm_made, U + 1)
                need(pe, h_made, 3 * U)
                pe.transpose(psD[0][:, 0:P], xm[:, par, :], ident[:, :]).then_inc(xm_turned, 1)

            def turn_back(m, par, n, p):
                U = 2 * m + par
                pe.wait_ge(xmT_ready, 3 * U + 3)
                pe.wait_ge(carry_m_saved, U + 1)
                pe.transpose(psD[0][:, P:2 * P], xmT[:, par, :], ident[:, :]).then_inc(xs2_turned, 1)

            def turn_z(m, par, n, p):
                U = 2 * m + par
                pe.wait_ge(z_made, U + 1)
                pe.transpose(psD[0][:, 2 * P:3 * P], z[:, par, :], ident[:, :]).then_inc(z_turned, 1)

            def ffn_up(m, par, n, p):
                U = 2 * m + par
                pe.wait_ge(zT_made, U + 1)
                pe.wait_ge(w1_loaded, 16 * (m // PAIRS + 1))
                need(pe, gelu_made, 3 * U)
                for half in (1, 0):
                    for ch, (lo, w) in enumerate(CH):
                        e = pe.matmul(psD[half][0:w, ch * P:(ch + 1) * P], w1[:, half * FF + lo:half * FF + lo + w], zT[:, par, :],
                                      start=True, stop=True)
                e.then_inc(ff_done, 1)

            def ffn_down(m, par, n, p):
                U = 2 * m + par
                pe.wait_ge(w2_loaded, 32 * (m // PAIRS + 1))
                pe.wait_ge(h_made, 3 * U + 3)
                free_bank(pe, Q_RING, "ffn_down", n, p)
                for ch, (lo, w) in enumerate(CH):
                    e = pe.matmul(BANK["ffn_down"][:, 0:DIM], hT[0:w, par, ch, :], w2[0:w, ch, :], start=(ch == 0), stop=(ch == 2))
                e.then_inc(y2_done, 1)

            def step(n, p):
                on(turn_qk, n, p, 1, n, p, 0)
                on(values, n, p, 2, n, p, 0)
                on(turn_o, n, p, 3, n, p, 0)
                on(turn_x, n, p, 0, n, p)
                on(values, n, p, 2, n, p, 1)
                on(turn_o, n, p, 3, n, p, 1)
                on(qk, n, p, 0, n, p, 0)
                on(turn_p, n, p, 2, n, p, 0)
                on(project, n, p, 3, n, p)
                on(qk, n, p, 0, n, p, 1)
                on(turn_qk, n, p, 1, n, p, 1)
                on(turn_xm, n, p, 3, n, p)
                on(ffn_down, n, p, 4, n, p)
                on(turn_qk, n, p, 1, n, p, 2)
                on(turn_qk, n, p, 1, n, p, 3)
                on(turn_back, n, p, 3, n, p)
                on(qk, n, p, 0, n, p, 2)
                on(turn_p, n, p, 2, n, p, 1)
                on(scores, n, p, 1, n, p, 0)
                on(scores, n, p, 1, n, p, 1)
                on(turn_p, n, p, 2, n, p, 2)
                on(qk, n, p, 0, n, p, 3)
                on(turn_p, n, p, 2, n, p, 3)
                on(turn_z, n, p, 3, n, p)
                on(scores, n, p, 1, n, p, 2)
                on(scores, n, p, 1, n, p, 3)
                on(turn_p, n, p, 2, n, p, 4)
                on(scores, n, p, 1, n, p, 4)
                on(ffn_up, n, p, 3, n, p)
                on(scores, n, p, 1, n, p, 5)
                on(attend, n, p, 2, n, p, 0)
                on(attend, n, p, 2, n, p, 1)

            in_steps(pe, step)


def retention_constants(T=1024, E=128, H=8, V=256, C=128):
    import numpy as np
    f = np.float32
    vec = ((np.arange(0, E, 2, dtype=f) + f(0.4 * E)) / f(1.4 * E)).astype(f)
    pos = np.arange(T, dtype=f)
    scale = (vec[None, :] ** (pos[:, None] / f(512.0))).astype(f)
    inv_freq = (f(1.0) / f(10000.0) ** (np.arange(E // 2, dtype=f) / f(E // 2))).astype(f)
    angle = (pos[:, None] * inv_freq[None, :]).astype(f)
    sin, cos = np.sin(angle).astype(f), np.cos(angle).astype(f)
    gamma = (f(1.0) - np.exp(np.linspace(np.log(1.0 / 32.0), np.log(1.0 / 512.0), H).astype(f))).astype(f)
    log_decay = np.log(gamma).astype(f).astype(np.float64)
    local = np.arange(T) % C
    row = np.sqrt(np.cumsum(np.exp(log_decay[None, :] * np.arange(T)[:, None]), 0))
    head = np.arange(E) // (E // H)
    fq = (np.exp(log_decay[None, :] * local[:, None]) / row * (E // H) ** -0.5)[:, head]
    fk = np.exp(-log_decay[None, :] * local[:, None])[:, head]
    two = lambda a: np.repeat(a.astype(np.float64), 2, axis=-1)
    sign = np.tile([-1.0, 1.0], E // 2)
    cq, sq_ = two(cos * scale) * fq, two(sin * scale) * sign * fq
    ck, sk = two(cos * (f(1.0) / scale)) * fk, two(sin * (f(1.0) / scale)) * sign * fk
    tile = lambda a: np.ascontiguousarray(a.reshape(T // C, C, 2 * E).transpose(1, 0, 2)).astype(f)
    p = np.arange(E)
    over = np.exp(log_decay * C)[head]
    return {"ret_cos": tile(np.concatenate([cq, ck], 1)), "ret_sin": tile(np.concatenate([sq_, sk], 1)),
            "ret_tri": (p[:, None] <= p[None, :]).astype(f), "ret_head_of": (head[:, None] == np.arange(H)[None, :]).astype(f),
            "ret_state_mask": ((head[:, None] == np.arange(V)[None, :] // (V // H)) * over[:, None]).astype(f),
            "ret_decay": over[:, None].astype(f)}


def linear_constants():
    import numpy as np
    f = np.float32
    p, ch = np.arange(128)[:, None, None], np.arange(4)[None, :, None]
    head = 4 * ch + p // 32
    return {"kv_mask": (head == np.arange(128)[None, None, :] // 8).astype(f), "ks_mask": (head == np.arange(16)[None, None, :]).astype(f)}


def local_constants(HD=64, n=1024, W=32, C=128):
    import numpy as np
    f = np.float32
    half = np.arange(0, HD, 2, dtype=f)
    inv_freq = (f(1.0) / f(10000.0) ** (half / f(HD))).astype(f)
    t = np.arange(n, dtype=f)
    freqs = (t[:, None] * inv_freq[None, :]).astype(f)
    freqs = np.concatenate([freqs, freqs], -1)
    base = ((half + f(0.4 * HD)) / f(1.4 * HD)).astype(f)
    power = ((t - n // 2) / f(W // 2)).astype(f)
    scale = (base[None, :] ** power[:, None]).astype(f)
    scale = np.concatenate([scale, scale], -1)
    sign = np.concatenate([-np.ones(HD // 2, f), np.ones(HD // 2, f)])
    inv = (f(1.0) / scale).astype(f)
    cos, sin = np.cos(freqs).astype(f), np.sin(freqs).astype(f)
    rope = np.stack([cos * scale, sin * scale * sign, cos * inv, sin * inv * sign], 1).astype(f)
    i, j = np.arange(C)[:, None], np.arange(C)[None, :]
    own = ((i // W == j // W) & (i >= j)) | ((i // W == j // W + 1) & (i <= j + W))
    prev = (i < W) & (i <= np.arange(W)[None, :])
    mask = np.full((C, 5, C + W + 1), -1e30, f)
    for k in range(5):
        mask[:, k, 0:C][own] = 0.0
        mask[:, k, C + W] = float(k > 0)
        if k:
            mask[:, k, C:C + W][prev] = 0.0
    flag = np.ones((C, 4), f)
    flag[:, 0] = 0.0
    return {"rope_const": rope.reshape(n // C, C, 4, HD).transpose(1, 0, 2, 3), "mask": mask, "flag": flag}


def program(nc, d, out):
    outer = ExitStack()
    with outer:
        def sem(name):
            return outer.enter_context(nc.semaphore(name))

        def keep(name, shape, dt=F32):
            return outer.enter_context(nc.sbuf_tensor(name, shape, dt))

        def part(prefix):
            return {k[len(prefix):]: v for k, v in d.items() if k.startswith(prefix)}

        bank = [outer.enter_context(nc.psum_tensor(f"bank{i}", [P, 512], F32))[:, :] for i in range(8)]
        ident = keep("identity", [P, P])
        ones_row = keep("ones_row", [1, P])
        x = keep("x", [P, TILES, DIM])
        loaded = sem("x_loaded")
        with nc.Block() as block:
            @block.sync
            def _(sp):
                sp.dma_start(ident[:, :], d["identity"]).then_inc(loaded, 16)
                sp.dma_start(x[:, :, :], d["hidden_states"].rearrange("b (t p) d -> p (b t) d", p=P)).then_inc(loaded, 16)
                sp.wait_ge(loaded, 32)

            @block.vector
            def _(dve):
                dve.memset(ones_row[:, :], 1.0)

        def phase(run):
            sems = []

            def signal(name):
                sems.append(nc.alloc_semaphore(name))
                return sems[-1]

            with ExitStack() as stack:
                run(lambda name, shape, dt=F32: stack.enter_context(nc.sbuf_tensor(name, shape, dt)), signal)
            nc.clear_and_free_semaphores(sems)
            nc.all_engine_barrier()

        phase(lambda sb, sem: retention_block(nc, sb, sem, bank, ident, ones_row, x, part("L0_attn_")))
        phase(lambda sb, sem: mixture(nc, sb, sem, bank, ident, ones_row, x, part("L0_ffn_")))
        phase(lambda sb, sem: linear_block(nc, sb, sem, bank, ident, ones_row, x, part("L1_attn_")))
        phase(lambda sb, sem: local_transformer(nc, sb, sem, bank, ident, x, out, part("L1_ffn_")))


_INS = ["L0_attn_w_qkv", "L0_attn_b_qkv", "L0_attn_w_g", "L0_attn_b_g", "L0_attn_w_p", "L0_attn_b_p",
        "L0_ffn_Wr", "L0_ffn_br", "L0_ffn_W1", "L0_ffn_b1", "L0_ffn_W2", "L0_ffn_b2",
        "L1_attn_proj", "L1_attn_w_qkv", "L1_attn_b_out", "L1_attn_gamma", "L1_attn_beta", "L1_attn_b1", "L1_attn_b2",
        "L1_ffn_Wqkv", "L1_ffn_q_scale", "L1_ffn_k_scale", "L1_ffn_Wo", "L1_ffn_ln_g", "L1_ffn_ln_b",
        "L1_ffn_W1", "L1_ffn_b1", "L1_ffn_W2", "L1_ffn_b2"]


def kernel(**inputs):
    import numpy as np
    import concourse.bacc as bacc
    from concourse.bass_utils import run_bass_kernel_spmd as run
    nc = bacc.Bacc("TRN2", target_bir_lowering=False, num_devices=1)
    arrays = {"hidden_states": inputs["L0_attn_hidden_states"], "identity": np.eye(P, dtype=np.float32)}
    for name in _INS:
        arrays[name] = inputs[name]
    w_qkv = inputs["L1_attn_w_qkv"]
    arrays.update(L1_attn_wvT=w_qkv[2 * DIM:].T, L1_attn_w_outT=inputs["L1_attn_w_out"].T,
                  L1_attn_w1T=inputs["L1_attn_w1"].T, L1_attn_w2T=inputs["L1_attn_w2"].T)
    arrays["L0_ffn_rank"] = np.broadcast_to(8.0 - np.arange(8, dtype=np.float32), (P, 4, 8))
    for prefix, consts in (("L0_attn_", retention_constants()), ("L1_attn_", linear_constants()), ("L1_ffn_", local_constants())):
        arrays.update({prefix + k: v for k, v in consts.items()})
    arrays = {"in_" + k: np.ascontiguousarray(v) for k, v in arrays.items()}
    d = {k[3:]: nc.dram_tensor(k, v.shape, F32, kind="ExternalInput").ap() for k, v in arrays.items()}
    out = nc.dram_tensor("out", (4, 1024, 128), F32, kind="ExternalOutput").ap()
    program(nc, d, out)
    return run(nc, [arrays], core_ids=[0]).results[0]["out"]
```

```python
import concourse.bass as bass
from concourse import mybir
from contextlib import ExitStack

F32 = mybir.dt.float32
ALU = mybir.AluOpType
ACT = mybir.ActivationFunctionType
AX = mybir.AxisListType
P = 128
DIM = 128
TILES = 32
SEQ_TILES = 8


def need(eng, sem, value):
    if not (isinstance(value, int) and value <= 0):
        eng.wait_ge(sem, value)


def apart(eng):
    eng.nop(nofuse=True)


class TileNorm:

    def __init__(self, sb, sem, tag, source, S, ident, banks, dest=None):
        self.source, self.S, self.ident, self.banks = source, S, ident, banks
        self.st = sb(tag + "_stats", [P, S, 6])
        self.mv = sb(tag + "_mean_var", [P, S, 2])
        self.ve = sb(tag + "_var_eps", [P, S])
        self.rstd = sb(tag + "_rstd", [P, S])
        self.z = None if dest else sb(tag + "_z", [P, S, DIM])
        self.dest = dest or (lambda n, s: self.z[:, s, :])
        self.zT = sb(tag + "_zT", [P, S * P]) if banks else None
        self.neg_half = sb(tag + "_neg_half", [P, S])
        self.cleared = sem(tag + "_cleared")
        self.stats_made, self.mean_var_made = sem(tag + "_stats_made"), sem(tag + "_mean_var_made")
        self.var_eps_made, self.rstd_made, self.z_made = sem(tag + "_var_eps_made"), sem(tag + "_rstd_made"), sem(tag + "_z_made")
        if banks:
            self.z_turned, self.zT_made = sem(tag + "_z_turned"), sem(tag + "_zT_made")

    def on_pool_start(self, pool):
        pool.memset(self.neg_half[:, :], -0.5).then_inc(self.cleared, 1)
        pool.wait_ge(self.cleared, 1)

    def on_dve(self, dve, n, free_z):
        S = self.S
        for s in range(S):
            dve.bn_stats(self.st[:, s, :], self.source(n, s)).then_inc(self.stats_made, 1)
        dve.wait_ge(self.stats_made, (n + 1) * S)
        apart(dve)
        for s in range(S):
            dve.bn_aggr(self.mv[:, s, :], self.st[:, s, :]).then_inc(self.mean_var_made, 1)
        dve.wait_ge(self.rstd_made, n + 1)
        free_z(dve, n)
        apart(dve)
        for s in range(S):
            dve.tensor_scalar(self.dest(n, s), self.source(n, s), self.mv[:, s, 0:1],
                              self.rstd[:, s:s + 1], ALU.subtract, ALU.mult).then_inc(self.z_made, 1)

    def on_pool(self, pool, n):
        pool.wait_ge(self.mean_var_made, (n + 1) * self.S)
        apart(pool)
        pool.tensor_scalar(self.ve[:, :], self.mv[:, :, 1], 1e-5, None, ALU.add).then_inc(self.var_eps_made, 1)
        pool.wait_ge(self.var_eps_made, n + 1)
        pool.tensor_tensor(self.rstd[:, :], self.ve[:, :], self.neg_half[:, :], ALU.pow).then_inc(self.rstd_made, 1)

    def on_pe(self, pe, n, free_ps):
        pe.wait_ge(self.z_made, (n + 1) * self.S)
        free_ps(pe, n)
        for s in range(self.S):
            e = pe.transpose(self.banks[s // 4][:, s % 4 * P:(s % 4 + 1) * P], self.z[:, s, :], self.ident[:, :])
            if s % 4 == 3:
                e.then_inc(self.z_turned, 1)

    def on_act(self, act, n, free_zT):
        free_zT(act, n)
        for i, b in enumerate(self.banks):
            act.wait_ge(self.z_turned, n * len(self.banks) + i + 1)
            act.activation(self.zT[:, i * 4 * P:(i + 1) * 4 * P], b[:, :], ACT.Copy).then_inc(self.zT_made, 1)


def tiles_of(x, S):
    return lambda n, s: x[:, bass.ds(n * S + s, 1), :].rearrange("p a d -> p (a d)")

def retention_block(nc, sb, sem, bank, ident, ones_row, x, c):
    H = 8
    V = c["w_g"].shape[1]
    QK = 2 * DIM
    DV = V // H
    SEQS = TILES // SEQ_TILES
    NT = SEQ_TILES
    wqkv = sb("ret_wqkv", [P, QK + V])
    wg = sb("ret_wg", [P, V])
    wp = sb("ret_wp", [P, V // P, DIM])
    b_qkv = sb("ret_b_qkv", [1, QK + V])
    b_g = sb("ret_b_g", [1, V])
    b_p = sb("ret_b_p", [1, DIM])
    cos_tab = sb("ret_cos", [P, NT, QK])
    sin_tab = sb("ret_sin", [P, NT, QK])
    tri = sb("ret_tri", [P, P])
    head_of = sb("ret_head_of", [P, H])
    state_mask = sb("ret_state_mask", [P, V])
    decay = sb("ret_decay", [P, 1])
    raw = sb("ret_qkv", [P, 2, QK + V])
    gs = sb("ret_gate", [P, 3, V])
    r1 = sb("ret_cos_part", [P, QK])
    r2 = sb("ret_sin_part", [P, QK])
    qk = sb("ret_qk", [P, 2, QK])
    qkT = sb("ret_qk_T", [P, 2, QK])
    qb = sb("ret_q_by_head", [P, 2, H, P])
    A = sb("ret_scores", [P, 2, H, P])
    state = sb("ret_state", [P, 2, V])
    grown = sb("ret_state_new", [P, V])
    tot = sb("ret_sum", [P, H])
    mu = sb("ret_mean", [P, H])
    xc = sb("ret_centred", [P, V])
    sq = sb("ret_squares", [P, V])
    var = sb("ret_var", [P, H])
    ve = sb("ret_var_eps", [P, H])
    rs = sb("ret_rstd", [P, H])
    neg_half = sb("ret_neg_half", [P, H])
    xn = sb("ret_normed", [P, V])
    gated = sb("ret_gated", [P, V])
    gT = sb("ret_gated_T", [P, V])
    ps_s, ps_q, ps_g, ps_t, ps_o, ps_m = bank[0:2], bank[2:4], bank[4], bank[5], bank[6], bank[7]
    ln = TileNorm(sb, sem, "ret_ln", tiles_of(x, NT), NT, ident, ps_s)
    names = ("loaded cleared qkv_done raw_made g_done gs_made parts_made qk_made qk_turned qkT_made qb_made s_done a_made o_done st_done "
             "grown_made state_made tot_made mu_made xc_made sq_made var_made ve_made rs_made xn_made gated_made gated_turned gT_made "
             "proj_done x_added").split()
    s_ = {k: sem("ret_" + k) for k in names}
    N_LOADS = 12
    wide = [P, H, DV]

    def by_head(a):
        return a.rearrange("p (h d) -> p h d", d=DV)

    def in_sequences(eng, body):
        body(0, True)
        with eng.Fori(1, SEQS - 1) as b:
            body(b, True)
        body(SEQS - 1, False)

    with nc.Block() as block:
        @block.sync
        def _(sp):
            n = [0]

            def load(dst, src):
                n[0] += 1
                sp.dma_start(dst, src).then_inc(s_["loaded"], 16)
            load(wqkv[:, :], c["w_qkv"])
            load(wg[:, :], c["w_g"])
            load(wp[:, :, :], c["w_p"].rearrange("(k p) d -> p k d", p=P))
            load(b_qkv[:, :], c["b_qkv"].unsqueeze(0))
            load(b_g[:, :], c["b_g"].unsqueeze(0))
            load(b_p[:, :], c["b_p"].unsqueeze(0))
            load(cos_tab[:, :, :], c["ret_cos"])
            load(sin_tab[:, :, :], c["ret_sin"])
            load(tri[:, :], c["ret_tri"])
            load(head_of[:, :], c["ret_head_of"])
            load(state_mask[:, :], c["ret_state_mask"])
            load(decay[:, :], c["ret_decay"])
            assert n[0] == N_LOADS

        @block.gpsimd
        def _(pool):
            pool.memset(neg_half[:, :], -0.5).then_inc(s_["cleared"], 1)
            ln.on_pool_start(pool)
            pool.wait_ge(s_["cleared"], 1)

            def group_rstd(b, t):
                T = NT * b + t
                pool.wait_ge(s_["var_made"], T + 1)
                apart(pool)
                pool.tensor_scalar(ve[:, :], var[:, :], 1.0 / DV, 1e-5, ALU.mult, ALU.add).then_inc(s_["ve_made"], 1)
                pool.wait_ge(s_["ve_made"], T + 1)
                need(pool, s_["xn_made"], T)
                pool.tensor_tensor(rs[:, :], ve[:, :], neg_half[:, :], ALU.pow).then_inc(s_["rs_made"], 1)

            def body(b, more):
                for t in range(NT - 1):
                    group_rstd(b, t)
                if more:
                    ln.on_pool(pool, b + 1)
                group_rstd(b, NT - 1)
            ln.on_pool(pool, 0)
            in_sequences(pool, body)

        @block.scalar
        def _(act):
            def evac_qkv(b, t):
                T = NT * b + t
                act.wait_ge(s_["qkv_done"], T + 1)
                need(act, s_["o_done"], T - 1)
                act.activation(raw[:, t % 2, :], ps_q[t % 2][:, :], ACT.Copy).then_inc(s_["raw_made"], 1)

            def gate(b, t):
                T = NT * b + t
                act.wait_ge(s_["g_done"], T + 1)
                need(act, s_["gated_made"], T - 2 if t >= 3 else NT * b)
                act.activation(gs[:, t % 3, :], ps_g[:, 0:V], ACT.Silu).then_inc(s_["gs_made"], 1)

            def square(b, t):
                T = NT * b + t
                act.wait_ge(s_["xc_made"], T + 1)
                need(act, s_["var_made"], T)
                act.activation(sq[:, :], xc[:, :], ACT.Square).then_inc(s_["sq_made"], 1)

            def evac_gated(b, t):
                T = NT * b + t
                act.wait_ge(s_["gated_turned"], T + 1)
                need(act, s_["proj_done"], T)
                act.activation(gT[:, :], ps_t[:, 0:V], ACT.Copy).then_inc(s_["gT_made"], 1)

            def norm(b):
                ln.on_act(act, b, lambda e, n: need(e, s_["g_done"], NT * n))

            def body(b, more):
                evac_qkv(b, 0)
                gate(b, 0)
                for t in range(NT):
                    T = NT * b + t
                    act.wait_ge(s_["qk_turned"], T + 1)
                    need(act, s_["o_done"], T - 1)
                    act.activation(qkT[:, t % 2, :], ps_t[:, 0:QK], ACT.Copy).then_inc(s_["qkT_made"], 1)
                    if t + 1 < NT:
                        evac_qkv(b, t + 1)
                    if t:
                        square(b, t - 1)
                    if t + 1 < NT:
                        gate(b, t + 1)
                    if t:
                        evac_gated(b, t - 1)
                if more:
                    norm(b + 1)
                square(b, NT - 1)
                evac_gated(b, NT - 1)
            norm(0)
            in_sequences(act, body)

        @block.vector
        def _(dve):
            dve.wait_ge(s_["loaded"], 16 * N_LOADS)

            def rope(b, t):
                T = NT * b + t
                dve.wait_ge(s_["raw_made"], T + 1)
                need(dve, s_["qk_made"], T)
                dve.tensor_tensor(r1[:, :], raw[:, t % 2, 0:QK], cos_tab[:, t, :], ALU.mult)
                for i in range(2):
                    m = dve.tensor_tensor(r2[:, i:QK:2], raw[:, t % 2, 1 - i:QK:2], sin_tab[:, t, i:QK:2], ALU.mult)
                m.then_inc(s_["parts_made"], 1)
                dve.wait_ge(s_["parts_made"], T + 1)
                need(dve, s_["st_done"], (NT - 1) * b + t - 1)
                need(dve, s_["qk_turned"], T - 1)
                dve.tensor_tensor(qk[:, t % 2, :], r1[:, :], r2[:, :], ALU.add).then_inc(s_["qk_made"], 1)

            def query_by_head(b, t):
                T = NT * b + t
                dve.wait_ge(s_["qkT_made"], T + 1)
                need(dve, s_["s_done"], 2 * (T - 1))
                dve.tensor_tensor(qb[:, t % 2, :, :], qkT[:, t % 2, 0:P].unsqueeze(1).to_broadcast([P, H, P]),
                                  head_of[:, :].unsqueeze(2).to_broadcast([P, H, P]), ALU.mult).then_inc(s_["qb_made"], 1)

            def scores(b, t):
                T = NT * b + t
                need(dve, s_["o_done"], T - 1)
                for i in range(2):
                    dve.wait_ge(s_["s_done"], 2 * T + i + 1)
                    dve.tensor_tensor(A[:, t % 2, 4 * i:4 * i + 4, :], ps_s[i].rearrange("p (h q) -> p h q", q=P),
                                      tri[:, :].unsqueeze(1).to_broadcast([P, 4, P]), ALU.mult).then_inc(s_["a_made"], 1)

            def next_state(b, t):
                K = (NT - 1) * b + t
                dve.wait_ge(s_["st_done"], K + 1)
                need(dve, s_["o_done"], NT * b + t)
                out = state[:, (t + 1) % 2, :] if t == 0 else grown[:, :]
                dve.tensor_tensor(out, ps_m[:, 0:V], state_mask[:, :], ALU.mult).then_inc(s_["grown_made"], 1)
                if t:
                    dve.wait_ge(s_["grown_made"], K + 1)
                    dve.wait_ge(s_["state_made"], K)
                    dve.scalar_tensor_tensor(state[:, (t + 1) % 2, :], state[:, t % 2, :], decay[:, 0:1], grown[:, :], ALU.mult, ALU.add
                                             ).then_inc(s_["state_made"], 1)
                else:
                    dve.wait_ge(s_["grown_made"], K + 1)
                    dve.sem_inc(s_["state_made"], 1)

            def centre(b, t):
                T = NT * b + t
                o = by_head(ps_o[:, 0:V])
                dve.wait_ge(s_["o_done"], T + 1)
                dve.tensor_reduce(tot[:, :], o, AX.X, ALU.add).then_inc(s_["tot_made"], 1)
                dve.wait_ge(s_["tot_made"], T + 1)
                dve.tensor_scalar(mu[:, :], tot[:, :], 1.0 / DV, None, ALU.mult).then_inc(s_["mu_made"], 1)
                dve.wait_ge(s_["mu_made"], T + 1)
                dve.tensor_tensor(by_head(xc[:, :]), o, mu[:, :].unsqueeze(2).to_broadcast(wide), ALU.subtract).then_inc(s_["xc_made"], 1)

            def variance(b, t):
                T = NT * b + t
                dve.wait_ge(s_["sq_made"], T + 1)
                dve.tensor_reduce(var[:, :], by_head(sq[:, :]), AX.X, ALU.add).then_inc(s_["var_made"], 1)

            def norm_and_gate(b, t):
                T = NT * b + t
                dve.wait_ge(s_["rs_made"], T + 1)
                dve.tensor_tensor(by_head(xn[:, :]), by_head(xc[:, :]), rs[:, :].unsqueeze(2).to_broadcast(wide), ALU.mult).then_inc(s_["xn_made"], 1)
                dve.wait_ge(s_["xn_made"], T + 1)
                dve.wait_ge(s_["gs_made"], T + 1)
                need(dve, s_["gated_turned"], T)
                dve.tensor_tensor(gated[:, :], xn[:, :], gs[:, t % 3, :], ALU.mult).then_inc(s_["gated_made"], 1)

            def residual(b, t):
                T = NT * b + t
                dve.wait_ge(s_["proj_done"], T + 1)
                apart(dve)
                xs = x[:, bass.ds(T, 1), :].rearrange("p a d -> p (a d)")
                dve.tensor_tensor(xs, ps_m[:, V:V + DIM], xs, ALU.add).then_inc(s_["x_added"], 1)

            def norm(b):
                ln.on_dve(dve, b, lambda e, n: need(e, ln.z_turned, 2 * n))

            def body(b, more):
                rope(b, 0)
                for t in range(NT):
                    query_by_head(b, t)
                    if t >= 2:
                        residual(b, t - 2)
                    if t:
                        centre(b, t - 1)
                    scores(b, t)
                    if t:
                        variance(b, t - 1)
                    if t + 1 < NT:
                        next_state(b, t)
                        rope(b, t + 1)
                    if t:
                        norm_and_gate(b, t - 1)
                if more:
                    norm(b + 1)
                residual(b, NT - 2)
                centre(b, NT - 1)
                variance(b, NT - 1)
                norm_and_gate(b, NT - 1)
                residual(b, NT - 1)
            norm(0)
            in_sequences(dve, body)

        @block.tensor
        def _(pe):
            pe.wait_ge(s_["loaded"], 16 * N_LOADS)

            def enter(b, t):
                T = NT * b + t
                pe.wait_ge(ln.zT_made, 2 * b + t // 4 + 1)
                zT = ln.zT[:, t * P:(t + 1) * P]
                need(pe, s_["raw_made"], T - 1)
                pe.matmul(ps_q[t % 2][:, :], zT, wqkv[:, :], start=True, stop=False)
                pe.matmul(ps_q[t % 2][:, :], ones_row[0:1, :], b_qkv[0:1, :], start=False, stop=True).then_inc(s_["qkv_done"], 1)
                need(pe, s_["gs_made"], T)
                pe.matmul(ps_g[:, 0:V], zT, wg[:, :], start=True, stop=False)
                pe.matmul(ps_g[:, 0:V], ones_row[0:1, :], b_g[0:1, :], start=False, stop=True).then_inc(s_["g_done"], 1)

            def turn_qk(b, t):
                T = NT * b + t
                pe.wait_ge(s_["qk_made"], T + 1)
                need(pe, s_["gT_made"], T - 1 if t else T)
                for i in range(2):
                    m = pe.transpose(ps_t[:, i * P:(i + 1) * P], qk[:, t % 2, i * P:(i + 1) * P], ident[:, :])
                m.then_inc(s_["qk_turned"], 1)

            def scores(b, t):
                T = NT * b + t
                pe.wait_ge(s_["qb_made"], T + 1)
                need(pe, s_["a_made"], 2 * T)
                if t == 0:
                    pe.wait_ge(ln.zT_made, 2 * b + 2)
                for i in range(2):
                    pe.matmul(ps_s[i][:, :], qkT[:, t % 2, P:2 * P], qb[:, t % 2, 4 * i:4 * i + 4, :].rearrange("p h q -> p (h q)"),
                              start=True, stop=True).then_inc(s_["s_done"], 1)

            def state_part(b, t):
                T = NT * b + t
                need(pe, s_["x_added"], T - 1 if t else T)
                need(pe, s_["grown_made"], (NT - 1) * b + t)
                pe.matmul(ps_m[:, 0:V], qk[:, t % 2, P:2 * P], raw[:, t % 2, QK:QK + V], start=True, stop=True).then_inc(s_["st_done"], 1)

            def output(b, t):
                T = NT * b + t
                need(pe, s_["xc_made"], T)
                if t:
                    pe.wait_ge(s_["state_made"], (NT - 1) * b + t)
                    pe.matmul(ps_o[:, 0:V], qkT[:, t % 2, 0:P], state[:, t % 2, :], start=True, stop=True)
                pe.wait_ge(s_["a_made"], 2 * T + 2)
                for h in range(H):
                    m = pe.matmul(ps_o[:, h * DV:(h + 1) * DV], A[:, t % 2, h, :], raw[:, t % 2, QK + h * DV:QK + (h + 1) * DV],
                                  start=(t == 0), stop=True, skip_group_check=True)
                m.then_inc(s_["o_done"], 1)

            def project(b, t):
                T = NT * b + t
                pe.wait_ge(s_["gated_made"], T + 1)
                pe.wait_ge(s_["qkT_made"], NT * b + min(t + 2, NT))
                for i in range(V // P):
                    m = pe.transpose(ps_t[:, i * P:(i + 1) * P], gated[:, i * P:(i + 1) * P], ident[:, :])
                m.then_inc(s_["gated_turned"], 1)
                pe.wait_ge(s_["gT_made"], T + 1)
                need(pe, s_["x_added"], T)
                pe.wait_ge(s_["grown_made"], (NT - 1) * b + min(t + 2, NT - 1))
                for i in range(V // P):
                    pe.matmul(ps_m[:, V:V + DIM], gT[:, i * P:(i + 1) * P], wp[:, i, :], start=(i == 0), stop=False)
                pe.matmul(ps_m[:, V:V + DIM], ones_row[0:1, :], b_p[0:1, :], start=False, stop=True).then_inc(s_["proj_done"], 1)

            def norm(b):
                ln.on_pe(pe, b, lambda e, n: need(e, s_["a_made"], 2 * NT * n))

            def body(b, more):
                enter(b, 0)
                for t in range(NT):
                    turn_qk(b, t)
                    if t + 1 < NT:
                        enter(b, t + 1)
                    scores(b, t)
                    if t + 1 < NT:
                        state_part(b, t)
                    output(b, t)
                    if t:
                        project(b, t - 1)
                if more:
                    norm(b + 1)
                project(b, NT - 1)
            norm(0)
            in_sequences(pe, body)

def mixture(nc, sb, sem, bank, ident, ones_row, x, c):
    EXPERTS, _, FF = c["W1"].shape
    FC = FF // P
    S = 4
    ROUNDS = TILES // S
    w1 = sb("moe_w1", [P, EXPERTS, FF])
    w2 = sb("moe_w2", [P, EXPERTS, FC, DIM])
    wr = sb("moe_wr", [P, EXPERTS])
    br = sb("moe_br", [1, EXPERTS])
    b1c = sb("moe_b1_col", [P, EXPERTS, FC])
    b2 = sb("moe_b2", [EXPERTS, DIM])
    rank = sb("moe_rank", [P, S, EXPERTS])
    hT = sb("moe_hidden_T", [P, 2, FC, S * P])
    acc = sb("moe_acc", [P, S, DIM])
    prob = sb("moe_probs", [P, S, EXPERTS])
    work = sb("moe_work", [P, S, EXPERTS])
    work2 = sb("moe_work2", [P, S, EXPERTS])
    hot1 = sb("moe_first", [P, S, EXPERTS])
    hot2 = sb("moe_second", [P, S, EXPERTS])
    col = sb("moe_col", [P, S])
    colb = sb("moe_colb", [P, S])
    gates = sb("moe_gates", [P, S, EXPERTS])
    gatesT = sb("moe_gates_T", [EXPERTS, S * P])
    psZ, psR = bank[0], bank[1]
    psY, psH = bank[2:4], bank[4:8]
    ln = TileNorm(sb, sem, "moe_ln", tiles_of(x, S), S, ident, [psZ])
    small_loaded, w_loaded = sem("moe_small_loaded"), [sem("moe_weights_loaded_0"), sem("moe_weights_loaded_1")]
    logits_done, exp_made, step_made, gates_made, gates_turned, gatesT_made, bias_done, acc_made = (sem("moe_" + s) for s in (
        "logits_done", "exp_made", "step_made", "gates_made", "gates_turned", "gatesT_made", "bias_done", "acc_made"))
    up_done, gelu_made, down_done, added = sem("moe_up_done"), sem("moe_gelu_made"), sem("moe_down_done"), sem("moe_added")
    N_SMALL = 5
    LOTS = [(0, 2), (2, EXPERTS)]
    STEPS = 21

    def in_rounds(eng, body):
        body(0, True)
        with eng.Fori(1, ROUNDS - 1) as n:
            body(n, True)
        body(ROUNDS - 1, False)

    with nc.Block() as block:
        @block.sync
        def _(sp):
            sp.dma_start(wr[:, :], c["Wr"]).then_inc(small_loaded, 16)
            sp.dma_start(br[:, :], c["br"].unsqueeze(0)).then_inc(small_loaded, 16)
            sp.dma_start(b2[:, :], c["b2"]).then_inc(small_loaded, 16)
            sp.dma_start(rank[:, :, :], c["rank"]).then_inc(small_loaded, 16)
            with nc.allow_non_contiguous_dma("small columns"):
                sp.dma_start(b1c[:, :, :], c["b1"].rearrange("e (c p) -> p e c", p=P)).then_inc(small_loaded, 16)
            for i, (lo, hi) in enumerate(LOTS):
                for dst, src in ((w1[:, lo:hi, :], c["W1"][lo:hi, :, :].rearrange("e p f -> p e f")),
                                 (w2[:, lo:hi, :, :], c["W2"][lo:hi, :, :].rearrange("e (c p) d -> p e c d", p=P))):
                    sp.dma_start(dst, src).then_inc(w_loaded[i], 16)

        @block.gpsimd
        def _(pool):
            ln.on_pool_start(pool)
            with pool.Fori(0, ROUNDS) as n:
                ln.on_pool(pool, n)

        @block.scalar
        def _(act):
            act.wait_ge(small_loaded, 16 * N_SMALL)

            def norm(n):
                ln.on_act(act, n, lambda e, n: need(e, up_done, n * EXPERTS * FC))

            def body(n, more):
                for e in range(EXPERTS):
                    i = n * EXPERTS + e
                    need(act, down_done, i - 1)
                    for ch in range(FC):
                        act.wait_ge(up_done, i * FC + ch + 1)
                        act.activation(hT[:, e % 2, ch, :], psH[ch][:, :], ACT.Gelu, bias=b1c[:, e, ch:ch + 1]).then_inc(gelu_made, 1)
                    if e == 0:
                        act.wait_ge(step_made, STEPS * n + 2)
                        act.activation(prob[:, :, :], work[:, :, :], ACT.Exp).then_inc(exp_made, 1)
                    if e == 1:
                        act.wait_ge(gates_turned, n + 1)
                        need(act, bias_done, n)
                        act.activation(gatesT[:, :], psZ[0:EXPERTS, :], ACT.Copy).then_inc(gatesT_made, 1)
                if more:
                    norm(n + 1)
            norm(0)
            in_rounds(act, body)

        @block.vector
        def _(dve):
            dve.wait_ge(small_loaded, 16 * N_SMALL)

            def route(n):
                k = [0]
                wide = [P, S, EXPERTS]

                def step(ins):
                    k[0] += 1
                    ins.then_inc(step_made, 1)
                    dve.wait_ge(step_made, STEPS * n + k[0])

                def spread(a):
                    return a[:, :].unsqueeze(2).to_broadcast(wide)

                def first_of_largest(hot, p):
                    step(dve.tensor_reduce(col[:, :], p[:, :, :], AX.X, ALU.max))
                    step(dve.tensor_tensor(work[:, :, :], p[:, :, :], spread(col), ALU.is_equal))
                    step(dve.tensor_tensor(work[:, :, :], work[:, :, :], rank[:, :, :], ALU.mult))
                    step(dve.tensor_reduce(colb[:, :], work[:, :, :], AX.X, ALU.max))
                    step(dve.tensor_tensor(hot[:, :, :], work[:, :, :], spread(colb), ALU.is_equal))

                logits = psR[:, 0:S * EXPERTS].rearrange("p (s e) -> p s e", e=EXPERTS)
                dve.wait_ge(logits_done, n + 1)
                step(dve.tensor_reduce(col[:, :], logits, AX.X, ALU.max))
                step(dve.tensor_tensor(work[:, :, :], logits, spread(col), ALU.subtract))
                dve.wait_ge(exp_made, n + 1)
                step(dve.tensor_reduce(col[:, :], prob[:, :, :], AX.X, ALU.add))
                step(dve.reciprocal(colb[:, :], col[:, :]))
                step(dve.tensor_tensor(prob[:, :, :], prob[:, :, :], spread(colb), ALU.mult))
                first_of_largest(hot1, prob)
                step(dve.scalar_tensor_tensor(work2[:, :, :], hot1[:, :, :], -2.0, prob[:, :, :], ALU.mult, ALU.add))
                first_of_largest(hot2, work2)
                step(dve.tensor_tensor(work[:, :, :], hot1[:, :, :], hot2[:, :, :], ALU.add))
                step(dve.tensor_tensor(work2[:, :, :], work[:, :, :], prob[:, :, :], ALU.mult))
                step(dve.tensor_reduce(col[:, :], work2[:, :, :], AX.X, ALU.add))
                step(dve.tensor_scalar(colb[:, :], col[:, :], 1e-9, None, ALU.add))
                step(dve.reciprocal(col[:, :], colb[:, :]))
                assert k[0] == STEPS
                need(dve, gates_turned, n)
                dve.tensor_tensor(gates[:, :, :], work2[:, :, :], spread(col), ALU.mult).then_inc(gates_made, 1)

            def norm(n):
                ln.on_dve(dve, n, lambda e, n: need(e, ln.z_turned, n))

            def body(n, more):
                dve.wait_ge(bias_done, n + 1)
                apart(dve)
                dve.tensor_tensor(acc[:, :, :].rearrange("p s d -> p (s d)"), psR[:, :],
                                  x[:, bass.ds(n * S, S), :].rearrange("p s d -> p (s d)"), ALU.add).then_inc(acc_made, 1)
                dve.wait_ge(acc_made, n + 1)
                for e in range(EXPERTS):
                    i = n * EXPERTS + e
                    dve.wait_ge(down_done, i + 1)
                    if e:
                        dve.wait_ge(added, S * i)
                    else:
                        dve.wait_ge(gates_made, n + 1)
                    apart(dve)
                    for s in range(S):
                        out = x[:, bass.ds(n * S + s, 1), :].rearrange("p a d -> p (a d)") if e == EXPERTS - 1 else acc[:, s, :]
                        dve.scalar_tensor_tensor(out, psY[e % 2][:, s * P:(s + 1) * P], gates[:, s, e:e + 1], acc[:, s, :],
                                                 ALU.mult, ALU.add).then_inc(added, 1)
                    if more and e == EXPERTS - 3:
                        norm(n + 1)
                if more:
                    route(n + 1)
            norm(0)
            route(0)
            in_rounds(dve, body)

        @block.tensor
        def _(pe):
            pe.wait_ge(small_loaded, 16 * N_SMALL)

            def up(n, e):
                i = n * EXPERTS + e
                if isinstance(n, int):
                    pe.wait_ge(w_loaded[0 if e < 2 else 1], 32)
                for ch in range(FC):
                    need(pe, gelu_made, (i - 1) * FC + ch + 1)
                    pe.matmul(psH[ch][:, :], w1[:, e, ch * P:(ch + 1) * P], ln.zT[:, :], start=True, stop=True).then_inc(up_done, 1)

            def down(n, e):
                i = n * EXPERTS + e
                need(pe, added, S * (i - 1))
                pe.wait_ge(gelu_made, (i + 1) * FC)
                for s in range(S):
                    for ch in range(FC):
                        m = pe.matmul(psY[e % 2][:, s * P:(s + 1) * P], hT[:, e % 2, ch, s * P:(s + 1) * P], w2[:, e, ch, :],
                                      start=(ch == 0), stop=(ch == FC - 1))
                m.then_inc(down_done, 1)

            def norm(n):
                ln.on_pe(pe, n, lambda e, n: need(e, gatesT_made, n))

            def logits(n):
                pe.wait_ge(ln.zT_made, n + 1)
                need(pe, acc_made, n)
                for s in range(S):
                    o = psR[:, s * EXPERTS:(s + 1) * EXPERTS]
                    pe.matmul(o, ln.zT[:, s * P:(s + 1) * P], wr[:, :], start=True, stop=False)
                    m = pe.matmul(o, ones_row[0:1, :], br[0:1, :], start=False, stop=True)
                m.then_inc(logits_done, 1)

            def body(n, more):
                up(n, 0)
                up(n, 1)
                down(n, 0)
                pe.wait_ge(gates_made, n + 1)
                for s in range(S):
                    m = pe.transpose(psZ[0:EXPERTS, s * P:(s + 1) * P], gates[:, s, :], ident[:, :])
                m.then_inc(gates_turned, 1)
                pe.wait_ge(gatesT_made, n + 1)
                apart(pe)
                for s in range(S):
                    m = pe.matmul(psR[:, s * P:(s + 1) * P], gatesT[:, s * P:(s + 1) * P], b2[:, :], start=True, stop=True)
                m.then_inc(bias_done, 1)
                for e in range(2, EXPERTS):
                    up(n, e)
                    down(n, e - 1)
                if more:
                    norm(n + 1)
                down(n, EXPERTS - 1)
                if more:
                    logits(n + 1)
            norm(0)
            logits(0)
            in_rounds(pe, body)

def linear_block(nc, sb, sem, bank, ident, ones_row, x, c):
    H, HD, NF = c["proj"].shape
    FF = c["w1T"].shape[1]
    FC = FF // P
    KC = H * NF // P
    SEQS = TILES // SEQ_TILES
    S = 4
    W = S * P
    wqk = sb("lin_wqk", [P, 2, DIM])
    wvT = sb("lin_wvT", [P, DIM])
    blocks = sb("lin_proj_blocks", [P, H * NF])
    G = sb("lin_feature_weights", [P, 2, H * NF])
    w_outT = sb("lin_w_outT", [P, DIM])
    w1T = sb("lin_w1T", [P, FF])
    w2T = sb("lin_w2T", [P, FC, DIM])
    b_out = sb("lin_b_out", [1, DIM])
    b2 = sb("lin_b2", [1, DIM])
    b1c = sb("lin_b1_col", [P, FC])
    gamma = sb("lin_gamma", [P, DIM])
    beta = sb("lin_beta", [P, DIM])
    kv_mask = sb("lin_kv_mask", [P, KC, DIM])
    ks_mask = sb("lin_ks_mask", [P, KC, H])
    low = sb("lin_low", [P, 2, W])
    kf = sb("lin_kf", [P, 2, H * NF])
    v1 = sb("lin_v_and_one", [P, SEQ_TILES, DIM + 1])
    kv = sb("lin_kv", [P, KC, DIM])
    ks = sb("lin_ksum", [P, KC, H])
    qf = sb("lin_qf_T", [P, KC, SEQ_TILES * P])
    den = sb("lin_den", [P, 2, S * H])
    rden = sb("lin_inv_den", [P, 2, S * H])
    at = sb("lin_attn", [P, 2, W])
    atT = sb("lin_attn_T", [P, 2, W])
    x1 = sb("lin_x1", [P, 2, S, DIM])
    gm = sb("lin_gained", [P, 2, S, DIM])
    x1n = sb("lin_x1_normed", [P, 2, S, DIM])
    x1T = sb("lin_x1_T", [P, 2, W])
    hT = sb("lin_hidden_T", [P, 2, FC, W])
    x2 = sb("lin_x2", [P, 2, S, DIM])
    gm2 = sb("lin_gained2", [P, 2, S, DIM])
    y = sb("lin_y", [P, 2, S, DIM])
    ps_z, ps_u, ps_kv, ps_v = bank[0:2], bank[2:4], bank[4:6], bank[6]
    ps_m, ps_den = (bank[7], ps_z[0]), (ps_v, ps_z[1])
    ln = TileNorm(sb, sem, "lin_ln", tiles_of(x, SEQ_TILES), SEQ_TILES, ident, ps_z)
    ln1 = [TileNorm(sb, sem, f"lin_ln1_{g}", lambda n, s, g=g: x1[:, g, s, :], S, ident, None) for g in range(2)]
    ln2 = [TileNorm(sb, sem, f"lin_ln2_{g}", lambda n, s, g=g: x2[:, g, s, :], S, ident, None) for g in range(2)]
    names = ("loaded weights_cleared blocks_loaded g_done g_made u_done low_made exp_made kf_made v_done v_made kv_done kv_made "
             "attn_done den_made rden_made at_made at_turned atT_made o_done x1_made gained1 x1n_made x1n_turned x1T_made "
             "up_done gelu_made down_done x2_made gained2 y_made x_added").split()
    s_ = {k: sem("lin_" + k) for k in names}
    N_LOADS = 12
    UT = 2 * SEQ_TILES

    with nc.Block() as block:
        @block.sync
        def _(sp):
            n = [0]

            def load(dst, src):
                n[0] += 1
                sp.dma_start(dst, src).then_inc(s_["loaded"], 16)
            load(wqk[:, :, :], c["w_qkv"][0:2 * DIM, :].rearrange("(a o) i -> o a i", a=2))
            load(wvT[:, :], c["wvT"])
            load(w_outT[:, :], c["w_outT"])
            load(w1T[:, :], c["w1T"])
            load(w2T[:, :, :], c["w2T"].rearrange("(c p) d -> p c d", p=P))
            load(b_out[:, :], c["b_out"].unsqueeze(0))
            load(b2[:, :], c["b2"].unsqueeze(0))
            with nc.allow_non_contiguous_dma("small columns"):
                load(b1c[:, :], c["b1"].rearrange("(c p) -> p c", p=P))
            load(gamma[:, :], c["gamma"].partition_broadcast(P))
            load(beta[:, :], c["beta"].partition_broadcast(P))
            load(kv_mask[:, :, :], c["kv_mask"])
            load(ks_mask[:, :, :], c["ks_mask"])
            assert n[0] == N_LOADS
            sp.wait_ge(s_["weights_cleared"], 2)
            for h in range(H):
                sp.dma_start(blocks[h * HD:(h + 1) * HD, h * NF:(h + 1) * NF], c["proj"][h, :, :]).then_inc(s_["blocks_loaded"], 16)

        @block.gpsimd
        def _(pool):
            pool.memset(blocks[:, :], 0.0).then_inc(s_["weights_cleared"], 1)
            pool.memset(v1[:, :, DIM:DIM + 1], 1.0).then_inc(s_["weights_cleared"], 1)
            for l in (ln, *ln1, *ln2):
                l.on_pool_start(pool)
            pool.wait_ge(s_["loaded"], 16 * N_LOADS)

            def gain(l, b, g, g_buf, out, gained, made, used):
                r = 2 * b + g
                pool.wait_ge(l.z_made, S * (b + 1))
                need(pool, made, r - 1)
                apart(pool)
                pool.tensor_tensor(g_buf[:, g, :, :], l.z[:, :, :], gamma[:, :].unsqueeze(1).to_broadcast([P, S, DIM]), ALU.mult).then_inc(gained, 1)
                pool.wait_ge(gained, r + 1)
                need(pool, used, r - 1)
                apart(pool)
                pool.tensor_tensor(out[:, g, :, :], g_buf[:, g, :, :], beta[:, :].unsqueeze(1).to_broadcast([P, S, DIM]), ALU.add).then_inc(made, 1)

            def body(b):
                ln.on_pool(pool, b)
                for g in range(2):
                    ln1[g].on_pool(pool, b)
                    gain(ln1[g], b, g, gm, x1n, s_["gained1"], s_["x1n_made"], s_["x2_made"])
                for g in range(2):
                    ln2[g].on_pool(pool, b)
                    gain(ln2[g], b, g, gm2, y, s_["gained2"], s_["y_made"], s_["x_added"])
            body(0)
            with pool.Fori(1, SEQS) as b:
                body(b)

        @block.scalar
        def _(act):
            act.wait_ge(s_["loaded"], 16 * N_LOADS)
            act.wait_ge(s_["g_done"], 2)
            for a in range(2):
                act.activation(G[:, a, :], ps_u[a][:, :], ACT.Copy).then_inc(s_["g_made"], 1)

            def exp_low(b, i):
                U = UT * b + i
                act.wait_ge(s_["low_made"], U + 1)
                act.activation(low[:, i % 2, :], low[:, i % 2, :], ACT.Exp).then_inc(s_["exp_made"], 1)

            def evac(b, g, dst, done, made, used):
                r = 2 * b + g
                act.wait_ge(done, r + 1)
                need(act, used, r - 1)
                act.activation(dst[:, g, :], ps_m[g][:, :], ACT.Copy).then_inc(made, 1)

            def body(b):
                ln.on_act(act, b, lambda e, n: need(e, s_["u_done"], UT * n))
                for half in range(2):
                    act.wait_ge(s_["v_done"], 2 * b + half + 1)
                    need(act, s_["kv_done"], b)
                    act.activation(v1[:, 4 * half:4 * half + 4, 0:DIM], ps_v.rearrange("p (s d) -> p s d", d=DIM), ACT.Copy).then_inc(s_["v_made"], 1)
                    for i in range(4 * half, 4 * half + 4):
                        exp_low(b, i)
                for i in range(SEQ_TILES, UT):
                    exp_low(b, i)
                for g in range(2):
                    evac(b, g, atT, s_["at_turned"], s_["atT_made"], s_["o_done"])
                for g in range(2):
                    evac(b, g, x1T, s_["x1n_turned"], s_["x1T_made"], s_["down_done"])
                for g in range(2):
                    r = 2 * b + g
                    for ch in range(FC):
                        act.wait_ge(s_["up_done"], FC * r + ch + 1)
                        need(act, s_["down_done"], r - 1)
                        act.activation(hT[:, g, ch, :], ps_u[ch % 2][:, :], ACT.Gelu, bias=b1c[:, ch:ch + 1]).then_inc(s_["gelu_made"], 1)
            body(0)
            with act.Fori(1, SEQS) as b:
                body(b)

        @block.vector
        def _(dve):
            dve.wait_ge(s_["loaded"], 16 * N_LOADS)

            def feature(b, i):
                U = UT * b + i
                dve.wait_ge(s_["u_done"], U + 1)
                need(dve, s_["kf_made"], U - 1)
                dve.tensor_scalar(low[:, i % 2, :], ps_u[i % 2][:, :], 0.0, None, ALU.min).then_inc(s_["low_made"], 1)

            def feature_end(b, i):
                U = UT * b + i
                out = kf[:, i % 2, :] if i < SEQ_TILES else qf[:, i % KC, (i - SEQ_TILES) // KC * W:((i - SEQ_TILES) // KC + 1) * W]
                dve.wait_ge(s_["exp_made"], U + 1)
                if i < SEQ_TILES:
                    need(dve, s_["kv_done"], SEQ_TILES * b + i - 1)
                else:
                    need(dve, s_["attn_done"], 2 * b)
                dve.scalar_tensor_tensor(out, ps_u[i % 2][:, :], 0.0, low[:, i % 2, :], ALU.max, ALU.add).then_inc(s_["kf_made"], 1)

            def attention(b, g):
                r = 2 * b + g
                dve.wait_ge(s_["attn_done"], r + 1)
                dve.tensor_scalar(den[:, g, :], ps_den[g][:, 0:S * H], 1e-8, None, ALU.add).then_inc(s_["den_made"], 1)
                dve.wait_ge(s_["den_made"], r + 1)
                dve.reciprocal(rden[:, g, :], den[:, g, :]).then_inc(s_["rden_made"], 1)
                dve.wait_ge(s_["rden_made"], r + 1)
                need(dve, s_["at_turned"], r - 1)
                dve.tensor_tensor(at[:, g, :].rearrange("p (h d) -> p h d", d=HD), ps_m[g].rearrange("p (h d) -> p h d", d=HD),
                                  rden[:, g, :].unsqueeze(2).to_broadcast([P, S * H, HD]), ALU.mult).then_inc(s_["at_made"], 1)

            def first_norm(b, g):
                r = 2 * b + g
                dve.wait_ge(s_["o_done"], r + 1)
                apart(dve)
                dve.tensor_tensor(x1[:, g, :, :].rearrange("p s d -> p (s d)"), ps_m[g][:, :],
                                  ln.z[:, 4 * g:4 * g + 4, :].rearrange("p s d -> p (s d)"), ALU.add).then_inc(s_["x1_made"], 1)
                dve.wait_ge(s_["x1_made"], r + 1)
                apart(dve)
                ln1[g].on_dve(dve, b, lambda e, n: need(e, s_["gained1"], 2 * n + g - 1))

            def second_norm(b, g):
                r = 2 * b + g
                dve.wait_ge(s_["down_done"], r + 1)
                dve.wait_ge(s_["x1n_made"], r + 1)
                dve.tensor_tensor(x2[:, g, :, :].rearrange("p s d -> p (s d)"), ps_m[g][:, :], x1n[:, g, :, :].rearrange("p s d -> p (s d)"),
                                  ALU.add).then_inc(s_["x2_made"], 1)
                dve.wait_ge(s_["x2_made"], r + 1)
                apart(dve)
                ln2[g].on_dve(dve, b, lambda e, n: need(e, s_["gained2"], 2 * n + g - 1))

            def block_out(b, g):
                r = 2 * b + g
                dve.wait_ge(s_["y_made"], r + 1)
                apart(dve)
                xs = x[:, bass.ds(r * S, S), :].rearrange("p s d -> p (s d)")
                dve.tensor_tensor(xs, xs, y[:, g, :, :].rearrange("p s d -> p (s d)"), ALU.add).then_inc(s_["x_added"], 1)

            def body(b):
                ln.on_dve(dve, b, lambda e, n: need(e, s_["x1_made"], 2 * n))
                feature(b, 0)
                for i in range(1, SEQ_TILES):
                    feature(b, i)
                    feature_end(b, i - 1)
                feature_end(b, SEQ_TILES - 1)
                dve.wait_ge(s_["kv_done"], SEQ_TILES * (b + 1))
                need(dve, s_["attn_done"], 2 * b)
                apart(dve)
                for ch in range(KC):
                    o = (ch % 2) * (DIM + 1)
                    dve.tensor_tensor(kv[:, ch, :], ps_kv[ch // 2][:, o:o + DIM], kv_mask[:, ch, :], ALU.mult)
                    dve.tensor_tensor(ks[:, ch, :], ps_kv[ch // 2][:, o + DIM:o + DIM + 1].to_broadcast([P, H]), ks_mask[:, ch, :],
                                      ALU.mult).then_inc(s_["kv_made"], 1)
                feature(b, SEQ_TILES)
                for i in range(SEQ_TILES + 1, UT):
                    feature(b, i)
                    feature_end(b, i - 1)
                feature_end(b, UT - 1)
                for g in range(2):
                    attention(b, g)
                for g in range(2):
                    first_norm(b, g)
                for g in range(2):
                    second_norm(b, g)
                for g in range(2):
                    block_out(b, g)
            body(0)
            with dve.Fori(1, SEQS) as b:
                body(b)

        @block.tensor
        def _(pe):
            pe.wait_ge(s_["loaded"], 16 * N_LOADS)
            pe.wait_ge(s_["blocks_loaded"], 16 * H)
            for a in range(2):
                pe.matmul(ps_u[a][:, :], wqk[:, a, :], blocks[:, :], start=True, stop=True).then_inc(s_["g_done"], 1)
            pe.wait_ge(s_["g_made"], 2)

            def free_u(b, i):
                if i < 2:
                    need(pe, s_["gelu_made"], 2 * FC * b)
                need(pe, s_["kf_made"], UT * b + i - 1)

            def attention(b, g):
                r = 2 * b + g
                pe.wait_ge(s_["kf_made"], UT * b + SEQ_TILES + KC * (g + 1))
                pe.wait_ge(s_["kv_made"], KC * (b + 1))
                need(pe, s_["x2_made"], r - 1)
                pe.wait_ge(s_["v_made"], 2 * b + 2)
                for t in range(S):
                    for ch in range(KC):
                        lhs = qf[:, ch, (4 * g + t) * P:(4 * g + t + 1) * P]
                        pe.matmul(ps_m[g][:, t * DIM:(t + 1) * DIM], lhs, kv[:, ch, :], start=(ch == 0), stop=(ch == KC - 1))
                    for ch in range(KC):
                        lhs = qf[:, ch, (4 * g + t) * P:(4 * g + t + 1) * P]
                        m = pe.matmul(ps_den[g][:, t * H:(t + 1) * H], lhs, ks[:, ch, :], start=(ch == 0), stop=(ch == KC - 1))
                m.then_inc(s_["attn_done"], 1)

            def turn_attention(b, g):
                pe.wait_ge(s_["at_made"], 2 * b + g + 1)
                for t in range(S):
                    m = pe.transpose(ps_m[g][:, t * P:(t + 1) * P], at[:, g, t * P:(t + 1) * P], ident[:, :])
                m.then_inc(s_["at_turned"], 1)

            def project(b, g):
                pe.wait_ge(s_["atT_made"], 2 * b + g + 1)
                for t in range(S):
                    o = ps_m[g][:, t * DIM:(t + 1) * DIM]
                    pe.matmul(o, atT[:, g, t * P:(t + 1) * P], w_outT[:, :], start=True, stop=False)
                    m = pe.matmul(o, ones_row[0:1, :], b_out[0:1, :], start=False, stop=True)
                m.then_inc(s_["o_done"], 1)

            def turn_x1(b, g):
                pe.wait_ge(s_["x1_made"], 2 * b + g + 1)
                pe.wait_ge(s_["x1n_made"], 2 * b + g + 1)
                for t in range(S):
                    m = pe.transpose(ps_m[g][:, t * P:(t + 1) * P], x1n[:, g, t, :], ident[:, :])
                m.then_inc(s_["x1n_turned"], 1)

            def ffn_up(b, g):
                r = 2 * b + g
                pe.wait_ge(s_["x1T_made"], r + 1)
                for ch in range(FC):
                    if ch < 2:
                        pe.wait_ge(s_["kf_made"], UT * (b + 1))
                    need(pe, s_["gelu_made"], FC * r + ch - 1)
                    pe.matmul(ps_u[ch % 2][:, :], w1T[:, ch * P:(ch + 1) * P], x1T[:, g, :], start=True, stop=True).then_inc(s_["up_done"], 1)

            def ffn_down(b, g):
                r = 2 * b + g
                pe.wait_ge(s_["gelu_made"], FC * (r + 1))
                for t in range(S):
                    o = ps_m[g][:, t * DIM:(t + 1) * DIM]
                    for ch in range(FC):
                        pe.matmul(o, hT[:, g, ch, t * P:(t + 1) * P], w2T[:, ch, :], start=(ch == 0), stop=False)
                    m = pe.matmul(o, ones_row[0:1, :], b2[0:1, :], start=False, stop=True)
                m.then_inc(s_["down_done"], 1)

            def body(b):
                ln.on_pe(pe, b, lambda e, n: (need(e, ln.zT_made, 2 * n), need(e, s_["x2_made"], 2 * n)))
                pe.wait_ge(ln.zT_made, 2 * b + 2)

                def values(half):
                    need(pe, s_["v_made"] if half else s_["rden_made"], 2 * b + half)
                    for t in range(4 * half, 4 * half + 4):
                        m = pe.matmul(ps_v[:, t % 4 * DIM:(t % 4 + 1) * DIM], ln.zT[:, t * P:(t + 1) * P], wvT[:, :], start=True, stop=True)
                    m.then_inc(s_["v_done"], 1)

                def keys(t):
                    free_u(b, t)
                    pe.matmul(ps_u[t % 2][:, :], ln.zT[:, t * P:(t + 1) * P], G[:, 1, :], start=True, stop=True).then_inc(s_["u_done"], 1)

                def add_kv(t):
                    pe.wait_ge(s_["v_made"], 2 * b + t // 4 + 1)
                    pe.wait_ge(s_["kf_made"], UT * b + t + 1)
                    if t == 0:
                        need(pe, s_["kv_made"], KC * b)
                    for ch in range(KC):
                        o = (ch % 2) * (DIM + 1)
                        m = pe.matmul(ps_kv[ch // 2][:, o:o + DIM + 1], kf[:, t % 2, ch * P:(ch + 1) * P], v1[:, t, :],
                                      start=(t == 0 and ch % 2 == 0), stop=(t == SEQ_TILES - 1 and ch % 2 == 1), skip_group_check=True)
                    m.then_inc(s_["kv_done"], 1)
                values(0)
                keys(0)
                keys(1)
                for t in range(2, SEQ_TILES):
                    if t == 4:
                        values(1)
                    keys(t)
                    add_kv(t - 2)
                add_kv(SEQ_TILES - 2)
                add_kv(SEQ_TILES - 1)
                for i in range(SEQ_TILES, UT):
                    free_u(b, i)
                    ch, half = i % KC, (i - SEQ_TILES) // KC
                    pe.matmul(ps_u[i % 2][:, :], G[:, 0, ch * P:(ch + 1) * P], ln.zT[:, half * W:(half + 1) * W], start=True, stop=True).then_inc(s_["u_done"], 1)
                for stage in (attention, turn_attention, project, turn_x1, ffn_up, ffn_down):
                    for g in range(2):
                        stage(b, g)
            body(0)
            with pe.Fori(1, SEQS) as b:
                body(b)


def local_transformer(nc, sb, sem, bank, ident, x, out, c):
    LAYERS, DIM, FF2 = c["W1"].shape
    FF = FF2 // 2
    INNER = c["Wo"].shape[1]
    HD = c["q_scale"].shape[1]
    H = INNER // HD
    PAIRS = TILES // 2
    SEQS = TILES // SEQ_TILES
    BP = 4
    WIN = 32
    KW = P + WIN
    HALF = DIM // 2
    CH = [(0, 128), (128, 128), (256, FF - 256)]
    NB = LAYERS * PAIRS

    XA = sb("layer_x", [P, TILES, DIM])
    wqk = sb("wqk", [P, 2 * INNER])
    wv = sb("wv", [P, INNER])
    wo = sb("wo", [P, INNER // P, DIM])
    w1 = sb("w1", [P, FF2])
    w2 = sb("w2", [P, 3, DIM])
    rope_c = sb("rope_const", [P, 8, 4, HD])
    qk_scales = sb("qk_scales", [P, LAYERS, 4, HD])
    ln_g = sb("ln_g_col", [P, LAYERS])
    ln_b = sb("ln_b_col", [P, LAYERS])
    b1_col = sb("b1_col", [P, LAYERS, 2, 3])
    b2_row = sb("b2_row", [P, LAYERS, DIM])
    mask = sb("mask", [P, 5, KW + 1])
    mask_now = sb("mask_now", [P, KW + 1])
    flag = sb("flag", [P, 4])
    neg_half = sb("neg_half", [P, 32])

    xc = sb("x_now", [P, 2, DIM])
    tab = sb("rope_tab", [P, 2, 4, HD])
    xsT = sb("x_shift_T", [P, 2, P])
    carry_a = sb("carry_attn", [P, 2])
    sq = sb("squares", [P, 4 * 512])
    t1 = sb("qk_roped", [P, 2, 2 * INNER])
    t2 = sb("rope_sin_part", [P, 2 * INNER])
    V = sb("v", [P, 2, INNER])
    ss = sb("sumsq", [P, 2, 2 * H])
    ssc = sb("sumsq_clamped", [P, 2, 2 * H])
    rn = sb("inv_norm", [P, 2, 2 * H])
    rq8 = sb("q_logit_scale", [P, 2, H])
    qT = sb("qT", [P, 2, H // 2, P])
    kT = sb("kT", [P, 2, H // 2, KW])
    Sm = sb("masked_scores", [P, H, KW])
    mx = sb("row_max", [P, 2, H])
    nb = sb("neg_max", [P, 2, H])
    PR = sb("probs", [P, 2, H, KW])
    den = sb("denoms", [P, 2, H])
    rden = sb("inv_denoms", [P, 2, H])
    PT = sb("probs_T", [P, H, P])
    GH = P // WIN
    PRw = sb("probs_prev", [WIN, 2, H, WIN])
    PTp = sb("probs_T_prev", [P, H // GH, WIN])
    Vw = sb("v_window", [P, 2, H // GH, GH, HD])
    On = sb("attn_out", [P, INNER])
    OT = sb("attn_out_T", [P, INNER // P, P])
    xm = sb("x_mid", [P, 2, DIM])
    xmb = sb("x_mid_plus_b2", [P, 2, DIM])
    xmT = sb("x_mid_shift_T", [P, 2, P])
    carry_m = sb("carry_ffn", [P, 2])
    st = sb("ln_stats", [P, 2, 6])
    mv = sb("ln_mean_var", [P, 2, 2])
    ve = sb("ln_var_eps", [P, 2])
    rstd = sb("ln_rstd", [P, 2])
    z = sb("ln_out", [P, 2, DIM])
    zT = sb("ln_out_T", [P, 2, P])
    gel = sb("gelu_gate", [P, 2, 3, P])
    hT = sb("hidden_T", [P, 2, 3, P])

    psQ, psT, psS, psD = bank[0:2], bank[2:4], bank[4:6], bank[6:8]

    consts_loaded = sem("consts_loaded")
    wqk_loaded, wv_loaded, wo_loaded, w1_loaded, w2_loaded = sem("wqk_loaded"), sem("wv_loaded"), sem("wo_loaded"), sem("w1_loaded"), sem("w2_loaded")
    cleared = sem("cleared")
    mask_picked = sem("mask_picked")
    xa_written = sem("xa_written")
    x_copied, tab_made, x_turned, xs_ready, carry_saved = sem("x_copied"), sem("tab_made"), sem("x_turned"), sem("xs_ready"), sem("carry_saved")
    qk_done, v_done, sq_made, v_copied = sem("qk_done"), sem("v_done"), sem("sq_made"), sem("v_copied")
    rope_terms, u_made, ss_made, ss_clamped, rn_made, kn_made = (sem(n) for n in ("rope_terms", "u_made", "ss_made", "ss_clamped", "rn_made", "kn_made"))
    qk_turned, qT_copied, kT_copied, kprev_copied = sem("qk_turned"), sem("qT_copied"), sem("kT_copied"), sem("kprev_copied")
    scores_done, sm_made, rq8_made, nb_made, p_made, rden_made = (sem(n) for n in ("scores_done", "sm_made", "rq8_made", "nb_made", "p_made", "rden_made"))
    vw_made, pw_made, p_turned, pt_act, pt_dve, av_done, o_normed, o_turned, o_copied, y_done, xm_made = (sem(n) for n in (
        "vw_made", "pw_made", "p_turned", "pt_act", "pt_dve", "av_done", "o_normed", "o_turned", "o_copied", "y_done", "xm_made"))
    xm_turned, xmT_ready, carry_m_saved, xmb_made, xs2_turned = (sem(n) for n in ("xm_turned", "xmT_ready", "carry_m_saved", "xmb_made", "xs2_turned"))
    stats_made, mv_made, ve_made, rstd_made, z_made, z_turned, zT_made = (sem(n) for n in ("stats_made", "mv_made", "ve_made", "rstd_made", "z_made", "z_turned", "zT_made"))
    ff_done, gelu_made, h_made, y2_done = sem("ff_done"), sem("gelu_made"), sem("h_made"), sem("y2_done")
    stored = sem("stored")

    summed = sem("summed")
    ln = TileNorm(sb, sem, "loc_ln", tiles_of(x, SEQ_TILES), SEQ_TILES, ident, None, dest=tiles_of(XA, SEQ_TILES))
    const_dma = [0]

    T_RING = [
        ("turn_qk3", 2, [(kT_copied, 2, 2)]),
        ("turn_p2", 3, [(pt_act, 2, 2)]),
        ("turn_x", 0, [(xs_ready, 3, 3), (carry_saved, 1, 1)]),
        ("turn_qk0", 1, [(qT_copied, 2, 1)]),
        ("turn_p3", 3, [(pt_dve, 3, 2)]),
        ("turn_p4", 3, [(pt_dve, 3, 3)]),
        ("turn_qk1", 1, [(qT_copied, 2, 2)]),
        ("turn_p0", 2, [(pt_act, 2, 1)]),
        ("turn_o0", 3, [(o_copied, 2, 1)]),
        ("turn_o1", 3, [(o_copied, 2, 2)]),
        ("turn_p1", 2, [(pt_dve, 3, 1)]),
        ("turn_qk2", 1, [(kT_copied, 2, 1)])]
    Q_RING = [
        ("qk2", 1, [(sq_made, 4, 3), (rope_terms, 4, 3)]),
        ("qk3", 1, [(sq_made, 4, 4), (rope_terms, 4, 4)]),
        ("values1", 2, [(v_copied, 2, 2)]),
        ("attend0", 3, [(o_normed, 2, 1)]),
        ("attend1", 3, [(o_normed, 2, 2)]),
        ("qk0", 0, [(sq_made, 4, 1), (rope_terms, 4, 1)]),
        ("qk1", 0, [(sq_made, 4, 2), (rope_terms, 4, 2)]),
        ("values0", 1, [(v_copied, 2, 1)]),
        ("project", 3, [(xm_made, 1, 1)]),
        ("ffn_down", 4, [(xa_written, 1, TILES + 1)])]
    S_RING = [
        ("scores0", 2, [(sm_made, 6, 1)]),
        ("scores1", 2, [(sm_made, 6, 2)]),
        ("scores2", 2, [(sm_made, 6, 3)]),
        ("scores3", 2, [(sm_made, 6, 4)]),
        ("scores4", 2, [(sm_made, 6, 5)]),
        ("scores5", 2, [(sm_made, 6, 6)])]
    RINGS = ((T_RING, psT), (Q_RING, psQ), (S_RING, psS))
    BANK = {use: banks[i % 2] for ring, banks in RINGS for i, (use, _, _) in enumerate(ring)}
    S_GROUPS = [(0, 2, 4), (1, 3, 5), (6, 8, 10), (7, 9, 11), (12, 14), (13, 15)]
    NT = LAYERS * TILES


    def behind(n, p, lag):
        return n + (p - lag) // 2, (p - lag) % 2

    def is_tile(m, par):
        return not isinstance(m, int) or 0 <= 2 * m + par < NT

    def free_bank(pe, ring, use, n, p):
        i = [name for name, _, _ in ring].index(use)
        for j in range(i - 2, i - 2 - 4 * len(ring), -2):
            _, lag, emptied = ring[j % len(ring)]
            m, par = behind(n, p, lag - j // len(ring))
            if is_tile(m, par):
                for s, k, signal in emptied:
                    pe.wait_ge(s, k * (2 * m + par) + signal)
                return

    def in_steps(eng, step):
        for n in range(4):
            step(n, 0)
            step(n, 1)
        with eng.Fori(4, NB - 1) as n:
            step(n, 0)
            step(n, 1)
        for n in range(NB - 1, NB + 3):
            step(n, 0)
            step(n, 1)

    def on(stage, n, p, lag, *more):
        m, par = behind(n, p, lag)
        if is_tile(m, par):
            stage(m, par, *more)

    with nc.Block() as block:
        @block.sync
        def _(sp):
            def load(dst, src):
                const_dma[0] += 1
                sp.dma_start(dst, src).then_inc(consts_loaded, 16)
            load(rope_c[:, :, :, :], c["rope_const"])
            for k, (name, lo) in enumerate((("q_scale", 0), ("q_scale", 1), ("k_scale", 0), ("k_scale", 1))):
                src = c[name].partition_broadcast(P)
                if lo == 0:
                    load(qk_scales[:, :, k, :], src)
                else:
                    load(qk_scales[:, :, k, 0:HD // 2], src[:, :, HD // 2:HD])
                    load(qk_scales[:, :, k, HD // 2:HD], src[:, :, 0:HD // 2])
            with nc.allow_non_contiguous_dma("small columns"):
                load(ln_g[:, :], c["ln_g"].rearrange("l d -> d l"))
                load(ln_b[:, :], c["ln_b"].rearrange("l d -> d l"))
                for half in range(2):
                    for ch, (lo, w) in enumerate(CH):
                        load(b1_col[0:w, :, half, ch], c["b1"][:, half * FF + lo:half * FF + lo + w].rearrange("l d -> d l"))
            load(b2_row[:, :, :], c["b2"].partition_broadcast(P))
            load(mask[:, :, :], c["mask"])
            load(flag[:, :], c["flag"])

            def load_wqk(l):
                sp.dma_start(wqk[:, :], c["Wqkv"][bass.ds(l, 1), :, 0:2 * INNER].rearrange("a k n -> k (a n)")).then_inc(wqk_loaded, 16)

            def load_wv(l):
                sp.dma_start(wv[:, :], c["Wqkv"][bass.ds(l, 1), :, 2 * INNER:3 * INNER].rearrange("a k n -> k (a n)")).then_inc(wv_loaded, 16)

            def load_wo(l):
                sp.dma_start(wo[:, :, :], c["Wo"][bass.ds(l, 1), :, :].rearrange("a (k p) n -> p (a k) n", p=P)).then_inc(wo_loaded, 16)

            def load_w1(l):
                sp.dma_start(w1[:, :], c["W1"][bass.ds(l, 1), :, :].rearrange("a k n -> k (a n)")).then_inc(w1_loaded, 16)

            def load_w2(l):
                sp.dma_start(w2[:, 0:2, :], c["W2"][bass.ds(l, 1), 0:256, :].rearrange("a (k p) n -> p (a k) n", p=P)).then_inc(w2_loaded, 16)
                sp.dma_start(w2[0:FF - 256, 2, :], c["W2"][bass.ds(l, 1), 256:FF, :].rearrange("a k n -> k (a n)")).then_inc(w2_loaded, 16)

            for load_it in (load_wqk, load_wv, load_wo, load_w1, load_w2):
                load_it(0)
            with sp.Fori(1, LAYERS) as l:
                for used, k, load_it in ((qk_done, 4, load_wqk), (v_done, 2, load_wv), (y_done, 1, load_wo), (ff_done, 1, load_w1), (y2_done, 1, load_w2)):
                    sp.wait_ge(used, k * TILES * l)
                    load_it(l)
            outs = out.rearrange("b (t p) d -> p b t d", p=P)
            for b in range(SEQS):
                sp.wait_ge(summed, b + 1)
                sp.dma_start(outs[:, b, :, :], XA[:, b * SEQ_TILES:(b + 1) * SEQ_TILES, :]).then_inc(stored, 16)
            sp.wait_ge(stored, 16 * SEQS)

        @block.gpsimd
        def _(pool):
            ln.on_pool_start(pool)
            with pool.Fori(0, SEQS) as n:
                ln.on_pool(pool, n)
            pool.memset(Vw[:, :, :, :, :], 0.0)
            pool.memset(kT[:, 1, :, P - WIN:P], 0.0)
            pool.memset(carry_a[:, :], 0.0)
            pool.memset(carry_m[:, :], 0.0)
            pool.memset(neg_half[:, :], -0.5).then_inc(cleared, 1)
            pool.wait_ge(cleared, 1)
            pool.wait_ge(consts_loaded, 16 * const_dma[0])

            def fetch(n, par):
                T = 2 * n + par
                t = (n % PAIRS) * 2 + par
                need(pool, xa_written, T + 1)
                need(pool, x_turned, T - 1)
                apart(pool)
                pool.tensor_copy(xc[:, par, :], XA[:, bass.ds(t, 1), :]).then_inc(x_copied, 1)
                need(pool, rope_terms, 4 * (T - 1))
                apart(pool)
                pool.tensor_tensor(tab[:, par, :, :], rope_c[:, bass.ds((n % BP) * 2 + par, 1), :, :].rearrange("p a k d -> p (a k) d"),
                                   qk_scales[:, bass.ds(n // PAIRS, 1), :, :].rearrange("p a k d -> p (a k) d"), ALU.mult).then_inc(tab_made, 1)

            def pick_mask(n, par):
                if par == 1:
                    return
                need(pool, sm_made, 6 * (2 * n - 1))
                apart(pool)
                pool.tensor_copy(mask_now[:, :], mask[:, bass.ds(n % BP, 1), :].rearrange("p a k -> p (a k)")).then_inc(mask_picked, 1)

            def rope_sum(n, par, j):
                T = 2 * n + par
                pool.wait_ge(rope_terms, 4 * T + 2 * j + 2)
                part = slice(j * INNER, (j + 1) * INNER)
                pool.tensor_tensor(t1[:, par, part], t1[:, par, part], t2[:, part], ALU.add).then_inc(u_made, 1)

            def norms(n, par):
                T = 2 * n + par
                pool.wait_ge(ss_made, T + 1)
                apart(pool)
                pool.tensor_scalar(ssc[:, par, :], ss[:, par, :], 1e-24, None, ALU.max).then_inc(ss_clamped, 1)
                pool.wait_ge(ss_clamped, T + 1)
                need(pool, kn_made, T - 1)
                pool.tensor_tensor(rn[:, par, :], ssc[:, par, :], neg_half[:, :], ALU.pow).then_inc(rn_made, 1)

            def k_prev(n, par):
                T = 2 * n + par
                need(pool, kT_copied, 2 * T)
                need(pool, scores_done, 6 * (T - 1))
                apart(pool)
                if par == 0:
                    pool.wait_ge(mask_picked, n + 1)
                    apart(pool)
                    pool.tensor_scalar(kT[:, par, :, P:KW], kT[:, 1, :, P - WIN:P], mask_now[:, KW:KW + 1], None, ALU.mult).then_inc(kprev_copied, 1)
                else:
                    pool.tensor_copy(kT[:, par, :, P:KW], kT[:, 0, :, P - WIN:P]).then_inc(kprev_copied, 1)

            def add_b2(n, par):
                U = 2 * n + par
                pool.wait_ge(xm_made, U + 1)
                need(pool, xa_written, TILES + U - 1)
                apart(pool)
                pool.tensor_tensor(xmb[:, par, :], xm[:, par, :], b2_row[:, bass.ds(n // PAIRS, 1), :].rearrange("p a d -> p (a d)"),
                                   ALU.add).then_inc(xmb_made, 1)

            def ln_rstd(n, par):
                U = 2 * n + par
                pool.wait_ge(mv_made, U + 1)
                apart(pool)
                pool.tensor_scalar(ve[:, par:par + 1], mv[:, par, 1:2], 1e-5, None, ALU.add).then_inc(ve_made, 1)
                pool.wait_ge(ve_made, U + 1)
                need(pool, z_made, U - 1)
                pool.tensor_tensor(rstd[:, par:par + 1], ve[:, par:par + 1], neg_half[:, 0:1], ALU.pow).then_inc(rstd_made, 1)

            def step(n, p):
                on(add_b2, n, p, 5)
                on(rope_sum, n, p, 2, 0)
                on(rope_sum, n, p, 2, 1)
                on(norms, n, p, 2)
                on(pick_mask, n, p, 2)
                on(fetch, n, p, 0)
                on(k_prev, n, p, 2)
                on(ln_rstd, n, p, 4)

            in_steps(pool, step)

        @block.scalar
        def _(act):
            act.wait_ge(cleared, 1)
            act.wait_ge(consts_loaded, 16 * const_dma[0])

            def shift(n, par, T, ps, dst, carry, ready, saved):
                act.activation(dst[0:HALF, par, :], ps[0:HALF, 0:P], ACT.Copy).then_inc(ready, 1)
                act.activation(dst[HALF:P, par, 1:P], ps[HALF:P, 0:P - 1], ACT.Copy).then_inc(ready, 1)
                need(act, saved, T)
                if par == 0:
                    apart(act)
                    act.activation(dst[HALF:P, par, 0:1], carry[HALF:P, 1:2], ACT.Copy, scale=flag[HALF:P, bass.ds(n % BP, 1)]).then_inc(ready, 1)
                else:
                    act.activation(dst[HALF:P, par, 0:1], carry[HALF:P, 0:1], ACT.Copy).then_inc(ready, 1)
                need(act, ready, 3 * T)
                act.activation(carry[HALF:P, par:par + 1], ps[HALF:P, P - 1:P], ACT.Copy).then_inc(saved, 1)

            def attn_in(n, par):
                T = 2 * n + par
                act.wait_ge(x_turned, T + 1)
                need(act, v_done, 2 * (T - 1))
                shift(n, par, T, BANK["turn_x"], xsT, carry_a, xs_ready, carry_saved)

            def square(n, par, j):
                T = 2 * n + par
                if j == 0:
                    need(act, ss_made, T)
                act.wait_ge(qk_done, 4 * T + j + 1)
                act.activation(sq[:, j * 512:(j + 1) * 512], BANK[f"qk{j}"][:, :], ACT.Square).then_inc(sq_made, 1)

            def evac_v(n, par, j):
                T = 2 * n + par
                if j == 0:
                    need(act, av_done, 2 * (T - 1))
                    need(act, vw_made, GH * (T - 1))
                act.wait_ge(v_done, 2 * T + j + 1)
                act.activation(V[:, par, j * 512:(j + 1) * 512], BANK[f"values{j}"][:, :], ACT.Copy).then_inc(v_copied, 1)

            def v_window(n, par):
                T = 2 * n + par
                need(act, av_done, 2 * T)
                act.wait_ge(v_copied, 2 * T + 2)
                apart(act)
                for i in range(GH):
                    act.activation(Vw[i * WIN:(i + 1) * WIN, par, :, i, :], V[P - WIN:P, par, :].rearrange("p (g i d) -> p g i d", i=GH, d=HD)[:, :, i, :],
                                   ACT.Copy).then_inc(vw_made, 1)

            def evac_q(n, par, j):
                T = 2 * n + par
                if j == 0:
                    need(act, scores_done, 6 * (T - 1))
                act.wait_ge(qk_turned, 4 * T + j + 1)
                act.activation(qT[:, par, 4 * j:4 * j + 4, :], BANK[f"turn_qk{j}"].rearrange("p (a b) -> p a b", b=P), ACT.Copy).then_inc(qT_copied, 1)

            def exps(n, par, q):
                T = 2 * n + par
                if q == 0:
                    act.wait_ge(nb_made, T + 1)
                    need(act, p_turned, 5 * (T - 1))
                    need(act, pw_made, T - 1)
                    need(act, rden_made, T - 1)
                for h in range(4 * q, 4 * q + 4):
                    e = act.activation(PR[:, par, h, :], Sm[:, h, :], ACT.Exp, bias=nb[:, par, h:h + 1],
                                       scale=rq8[:, par, h:h + 1], accum_out=den[:, par, h:h + 1])
                e.then_inc(p_made, 1)

            def evac_p(n, par, q):
                T = 2 * n + par
                need(act, av_done, 2 * T)
                act.wait_ge(p_turned, 5 * T + q + 1)
                act.activation(PT[:, 4 * q:4 * q + 4, :], BANK[f"turn_p{q}"].rearrange("p (a b) -> p a b", b=P), ACT.Copy).then_inc(pt_act, 1)

            def evac_o(n, par, j):
                T = 2 * n + par
                need(act, y_done, T)
                act.wait_ge(o_turned, 2 * T + j + 1)
                act.activation(OT[:, 4 * j:4 * j + 4, :], BANK[f"turn_o{j}"].rearrange("p (a b) -> p a b", b=P), ACT.Copy).then_inc(o_copied, 1)

            def ffn_in(n, par):
                U = 2 * n + par
                act.wait_ge(xm_turned, U + 1)
                need(act, xs2_turned, U - 1)
                shift(n, par, U, psD[0], xmT, carry_m, xmT_ready, carry_m_saved)

            def evac_z(n, par):
                U = 2 * n + par
                act.wait_ge(z_turned, U + 1)
                need(act, ff_done, U - 1)
                apart(act)
                act.activation(zT[:, par, :], psD[0][:, 2 * P:3 * P], ACT.Identity, scale=ln_g[:, bass.ds(n // PAIRS, 1)],
                               bias=ln_b[:, bass.ds(n // PAIRS, 1)]).then_inc(zT_made, 1)

            def gelu(n, par):
                U = 2 * n + par
                need(act, h_made, 3 * (U - 1))
                act.wait_ge(ff_done, U + 1)
                apart(act)
                for ch, (lo, w) in enumerate(CH):
                    act.activation(gel[0:w, par, ch, :], psD[1][0:w, ch * P:(ch + 1) * P], ACT.Gelu,
                                   bias=b1_col[0:w, bass.ds(n // PAIRS, 1), 1, ch]).then_inc(gelu_made, 1)

            def step(n, p):
                on(evac_v, n, p, 2, 0)
                on(exps, n, p, 3, 2)
                on(ffn_in, n, p, 4)
                on(exps, n, p, 3, 3)
                on(square, n, p, 1, 2)
                on(square, n, p, 1, 3)
                on(evac_p, n, p, 3, 2)
                on(evac_z, n, p, 4)
                on(evac_v, n, p, 2, 1)
                on(attn_in, n, p, 0)
                on(evac_q, n, p, 1, 0)
                on(gelu, n, p, 4)
                on(exps, n, p, 2, 0)
                on(exps, n, p, 2, 1)
                on(evac_q, n, p, 1, 1)
                on(square, n, p, 0, 0)
                on(evac_p, n, p, 2, 0)
                on(square, n, p, 0, 1)
                on(evac_o, n, p, 3, 0)
                on(evac_o, n, p, 3, 1)
                on(v_window, n, p, 2)

            in_steps(act, step)

        @block.vector
        def _(dve):
            with dve.Fori(0, SEQS) as n:
                ln.on_dve(dve, n, lambda e, n: None)
            dve.wait_ge(ln.z_made, TILES)
            dve.sem_inc(xa_written, TILES)
            dve.wait_ge(cleared, 1)
            dve.wait_ge(consts_loaded, 16 * const_dma[0])

            def rope(n, par, j):
                T = 2 * n + par
                if j == 0:
                    dve.wait_ge(tab_made, T + 1)
                    need(dve, u_made, 2 * T)
                    need(dve, qk_turned, 4 * (T - 1))
                k = 2 * (j // 2)
                HH = HD // 2
                dve.wait_ge(sq_made, 4 * T + j + 1)
                src = BANK[f"qk{j}"].rearrange("p (h d) -> p h d", d=HD)
                o1 = t1[:, par, j * 512:(j + 1) * 512].rearrange("p (h d) -> p h d", d=HD)
                o2 = t2[:, j * 512:(j + 1) * 512].rearrange("p (h d) -> p h d", d=HD)
                dve.tensor_tensor(o1, src, tab[:, par, k, :].unsqueeze(1).to_broadcast([P, 8, HD]), ALU.mult)
                dve.tensor_tensor(o2[:, :, 0:HH], src[:, :, HH:HD], tab[:, par, k + 1, 0:HH].unsqueeze(1).to_broadcast([P, 8, HH]), ALU.mult)
                dve.tensor_tensor(o2[:, :, HH:HD], src[:, :, 0:HH], tab[:, par, k + 1, HH:HD].unsqueeze(1).to_broadcast([P, 8, HH]),
                                  ALU.mult).then_inc(rope_terms, 1)

            def sumsq(n, par):
                T = 2 * n + par
                dve.wait_ge(sq_made, 4 * T + 4)
                need(dve, ss_clamped, T - 1)
                dve.tensor_reduce(ss[:, par, :], sq[:, :].rearrange("p (h d) -> p h d", d=HD), AX.X, ALU.add).then_inc(ss_made, 1)

            def k_norm(n, par):
                T = 2 * n + par
                dve.wait_ge(rn_made, T + 1)
                need(dve, nb_made, T - 1)
                need(dve, p_made, 4 * (T - 1))
                dve.tensor_scalar(rq8[:, par, :], rn[:, par, 0:H], 8.0, None, ALU.mult).then_inc(rq8_made, 1)
                dve.wait_ge(u_made, 2 * T + 2)
                dve.tensor_tensor(t1[:, par, INNER:2 * INNER].rearrange("p (h d) -> p h d", d=HD), t1[:, par, INNER:2 * INNER].rearrange("p (h d) -> p h d", d=HD),
                                  rn[:, par, H:2 * H].unsqueeze(2).to_broadcast([P, H, HD]), ALU.mult).then_inc(kn_made, 1)

            def evac_k(n, par, j):
                T = 2 * n + par
                if j == 0:
                    need(dve, kprev_copied, T)
                dve.wait_ge(qk_turned, 4 * T + j + 3)
                dve.tensor_copy(kT[:, par, 4 * j:4 * j + 4, 0:P], BANK[f"turn_qk{j + 2}"].rearrange("p (a b) -> p a b", b=P)).then_inc(kT_copied, 1)

            def masked(n, par, g):
                T = 2 * n + par
                if g == 0:
                    need(dve, p_made, 4 * T)
                    dve.wait_ge(mask_picked, n + 1)
                m = mask_now[:, 0:KW] if par == 0 else mask[:, 4, 0:KW]
                dve.wait_ge(scores_done, 6 * T + g + 1)
                apart(dve)
                for i, h in enumerate(S_GROUPS[g]):
                    e = dve.tensor_tensor_reduce(out=Sm[:, h, :], in0=BANK[f"scores{g}"][:, i * KW:(i + 1) * KW], in1=m, scale=1.0, scalar=-3e38,
                                                 op0=ALU.add, op1=ALU.max, accum_out=mx[:, par, h:h + 1])
                e.then_inc(sm_made, 1)

            def neg_max(n, par):
                T = 2 * n + par
                dve.wait_ge(sm_made, 6 * T + 6)
                dve.wait_ge(rq8_made, T + 1)
                dve.scalar_tensor_tensor(nb[:, par, :], mx[:, par, :], -1.0, rq8[:, par, :], ALU.mult, ALU.mult).then_inc(nb_made, 1)

            def evac_p(n, par, q):
                T = 2 * n + par
                need(dve, av_done, 2 * T)
                dve.wait_ge(p_turned, 5 * T + q + 1)
                ps = BANK[f"turn_p{q}"]
                if q < 4:
                    dve.tensor_copy(PT[:, 4 * q:4 * q + 4, :], ps.rearrange("p (a b) -> p a b", b=P)).then_inc(pt_dve, 1)
                else:
                    dve.tensor_copy(PTp[:, :, :], ps[:, 0:P].rearrange("p (a b) -> p a b", b=WIN)).then_inc(pt_dve, 1)

            def p_window(n, par):
                T = 2 * n + par
                dve.wait_ge(p_made, 4 * T + 4)
                need(dve, p_turned, 5 * (T - 1))
                apart(dve)
                dve.tensor_copy(PRw[:, par, :, :], PR[0:WIN, par, :, P:KW]).then_inc(pw_made, 1)

            def inv_den(n, par):
                T = 2 * n + par
                dve.wait_ge(p_made, 4 * T + 4)
                dve.reciprocal(rden[:, par, :], den[:, par, :]).then_inc(rden_made, 1)

            def normalise(n, par, j):
                T = 2 * n + par
                dve.wait_ge(rden_made, T + 1)
                dve.wait_ge(av_done, 2 * T + j + 1)
                need(dve, o_turned, 2 * (T - 1) + j + 1)
                dve.tensor_tensor(On[:, j * 512:(j + 1) * 512].rearrange("p (h d) -> p h d", d=HD),
                                  BANK[f"attend{j}"].rearrange("p (h d) -> p h d", d=HD),
                                  rden[:, par, 8 * j:8 * j + 8].unsqueeze(2).to_broadcast([P, 8, HD]), ALU.mult).then_inc(o_normed, 1)

            def residual(n, par):
                T = 2 * n + par
                dve.wait_ge(y_done, T + 1)
                need(dve, xm_turned, T - 1)
                need(dve, xmb_made, T - 1)
                dve.tensor_tensor(xm[:, par, :], BANK["project"][:, 0:DIM], XA[:, bass.ds((n % PAIRS) * 2 + par, 1), :].rearrange("p a d -> p (a d)"),
                                  ALU.add).then_inc(xm_made, 1)

            def ln_stats(n, par):
                U = 2 * n + par
                dve.wait_ge(xs2_turned, U + 1)
                dve.bn_stats(st[:, par, :], psD[0][:, P:2 * P]).then_inc(stats_made, 1)
                dve.wait_ge(stats_made, U + 1)
                need(dve, ve_made, U - 1)
                apart(dve)
                dve.bn_aggr(mv[:, par, :], st[:, par, :]).then_inc(mv_made, 1)

            def ln_apply(n, par):
                U = 2 * n + par
                dve.wait_ge(rstd_made, U + 1)
                need(dve, z_turned, U - 1)
                dve.tensor_scalar(z[:, par, :], psD[0][:, P:2 * P], mv[:, par, 0:1], rstd[:, par:par + 1], ALU.subtract, ALU.mult).then_inc(z_made, 1)

            def gate(n, par):
                U = 2 * n + par
                need(dve, y2_done, U - 1)
                for ch, (lo, w) in enumerate(CH):
                    dve.wait_ge(gelu_made, 3 * U + ch + 1)
                    dve.scalar_tensor_tensor(hT[0:w, par, ch, :], psD[0][0:w, ch * P:(ch + 1) * P], b1_col[0:w, bass.ds(n // PAIRS, 1), 0, ch],
                                             gel[0:w, par, ch, :], ALU.add, ALU.mult).then_inc(h_made, 1)

            def ffn_out(n, par):
                U = 2 * n + par
                dve.wait_ge(y2_done, U + 1)
                dve.wait_ge(xmb_made, U + 1)
                dve.tensor_tensor(XA[:, bass.ds((n % PAIRS) * 2 + par, 1), :].rearrange("p a d -> p (a d)"), BANK["ffn_down"][:, 0:DIM], xmb[:, par, :],
                                  ALU.add).then_inc(xa_written, 1)

            def step(n, p):
                on(inv_den, n, p, 3)
                on(rope, n, p, 1, 3)
                on(masked, n, p, 2, 3)
                on(p_window, n, p, 3)
                on(evac_p, n, p, 3, 3)
                on(evac_p, n, p, 3, 4)
                on(masked, n, p, 2, 4)
                on(masked, n, p, 2, 5)
                on(neg_max, n, p, 2)
                on(sumsq, n, p, 1)
                on(normalise, n, p, 3, 0)
                on(normalise, n, p, 3, 1)
                on(rope, n, p, 0, 0)
                on(rope, n, p, 0, 1)
                on(k_norm, n, p, 1)
                on(gate, n, p, 4)
                on(evac_p, n, p, 2, 1)
                on(residual, n, p, 3)
                on(evac_k, n, p, 1, 0)
                on(ffn_out, n, p, 4)
                on(evac_k, n, p, 1, 1)
                on(ln_stats, n, p, 3)
                on(ln_apply, n, p, 3)
                on(masked, n, p, 1, 0)
                on(rope, n, p, 0, 2)
                on(masked, n, p, 1, 1)
                on(masked, n, p, 1, 2)

            in_steps(dve, step)
            dve.wait_ge(xa_written, TILES + 2 * NB)
            for b in range(SEQS):
                part = slice(b * SEQ_TILES, (b + 1) * SEQ_TILES)
                dve.tensor_tensor(XA[:, part, :], XA[:, part, :], x[:, part, :], ALU.add).then_inc(summed, 1)

        @block.tensor
        def _(pe):
            pe.wait_ge(cleared, 1)
            pe.wait_ge(consts_loaded, 16 * const_dma[0])

            def turn_x(m, par, n, p):
                T = 2 * m + par
                pe.wait_ge(x_copied, T + 1)
                free_bank(pe, T_RING, "turn_x", n, p)
                pe.transpose(BANK["turn_x"][:, 0:P], xc[:, par, :], ident[:, :]).then_inc(x_turned, 1)

            def qk(m, par, n, p, j):
                T = 2 * m + par
                if j == 0:
                    pe.wait_ge(xs_ready, 3 * T + 3)
                    pe.wait_ge(wqk_loaded, 16 * (m // PAIRS + 1))
                free_bank(pe, Q_RING, f"qk{j}", n, p)
                pe.matmul(BANK[f"qk{j}"][:, :], xsT[:, par, :], wqk[:, j * 512:(j + 1) * 512], start=True, stop=True).then_inc(qk_done, 1)

            def values(m, par, n, p, j):
                if j == 0:
                    pe.wait_ge(wv_loaded, 16 * (m // PAIRS + 1))
                free_bank(pe, Q_RING, f"values{j}", n, p)
                pe.matmul(BANK[f"values{j}"][:, :], xsT[:, par, :], wv[:, j * 512:(j + 1) * 512], start=True, stop=True).then_inc(v_done, 1)

            def turn_qk(m, par, n, p, j):
                T = 2 * m + par
                if j == 0:
                    pe.wait_ge(u_made, 2 * T + 1)
                if j == 2:
                    pe.wait_ge(kn_made, T + 1)
                free_bank(pe, T_RING, f"turn_qk{j}", n, p)
                for i in range(4):
                    col = (j // 2) * INNER + (4 * (j % 2) + i) * P
                    e = pe.transpose(BANK[f"turn_qk{j}"][:, i * P:(i + 1) * P], t1[:, par, col:col + P], ident[:, :])
                e.then_inc(qk_turned, 1)

            def scores(m, par, n, p, g):
                T = 2 * m + par
                if g == 0:
                    pe.wait_ge(qT_copied, 2 * T + 2)
                    pe.wait_ge(kT_copied, 2 * T + 2)
                    pe.wait_ge(kprev_copied, T + 1)
                free_bank(pe, S_RING, f"scores{g}", n, p)
                for i, h in enumerate(S_GROUPS[g]):
                    r = slice(HD * (h % 2), HD * (h % 2) + HD)
                    e = pe.matmul(BANK[f"scores{g}"][:, i * KW:(i + 1) * KW], qT[r, par, h // 2, :], kT[r, par, h // 2, :], start=True, stop=True)
                e.then_inc(scores_done, 1)

            def turn_p(m, par, n, p, q):
                T = 2 * m + par
                ps = BANK[f"turn_p{q}"]
                if q < 4:
                    pe.wait_ge(p_made, 4 * T + q + 1)
                free_bank(pe, T_RING, f"turn_p{q}", n, p)
                if q < 4:
                    for i in range(4):
                        e = pe.transpose(ps[:, i * P:(i + 1) * P], PR[:, par, 4 * q + i, 0:P], ident[:, :])
                else:
                    pe.wait_ge(pw_made, T + 1)
                    apart(pe)
                    for g in range(H // GH):
                        e = pe.transpose(ps[:, g * WIN:(g + 1) * WIN], PRw[0:WIN, par, g * GH:(g + 1) * GH, :].rearrange("p i k -> p (i k)"), ident[0:WIN, 0:WIN])
                e.then_inc(p_turned, 1)

            def attend(m, par, n, p, j):
                T = 2 * m + par
                if j == 0:
                    pe.wait_ge(v_copied, 2 * T + 2)
                    pe.wait_ge(pt_dve, 3 * T + 3)
                    pe.wait_ge(pt_act, 2 * T + 2)
                    need(pe, vw_made, GH * T)
                free_bank(pe, Q_RING, f"attend{j}", n, p)
                for i in range(8):
                    h = 8 * j + i
                    pe.matmul(BANK[f"attend{j}"][:, i * HD:(i + 1) * HD], PT[:, h, :], V[:, par, h * HD:(h + 1) * HD],
                              start=(i == 0), stop=True, skip_group_check=(i > 0))
                for g in range(2):
                    part = slice(g * GH * HD, (g + 1) * GH * HD)
                    e = pe.matmul(BANK[f"attend{j}"][0:WIN, part], PTp[:, 2 * j + g, :], Vw[:, 1 - par, 2 * j + g, :, :].rearrange("p i d -> p (i d)"),
                                  start=False, stop=True, skip_group_check=True)
                e.then_inc(av_done, 1)

            def turn_o(m, par, n, p, j):
                T = 2 * m + par
                pe.wait_ge(o_normed, 2 * T + j + 1)
                free_bank(pe, T_RING, f"turn_o{j}", n, p)
                for i in range(4):
                    col = (4 * j + i) * P
                    e = pe.transpose(BANK[f"turn_o{j}"][:, i * P:(i + 1) * P], On[:, col:col + P], ident[:, :])
                e.then_inc(o_turned, 1)

            def project(m, par, n, p):
                T = 2 * m + par
                pe.wait_ge(wo_loaded, 16 * (m // PAIRS + 1))
                free_bank(pe, Q_RING, "project", n, p)
                for k in range(INNER // P):
                    if k % 4 == 0:
                        pe.wait_ge(o_copied, 2 * T + k // 4 + 1)
                    e = pe.matmul(BANK["project"][:, 0:DIM], OT[:, k, :], wo[:, k, :], start=(k == 0), stop=(k == INNER // P - 1))
                e.then_inc(y_done, 1)

            def turn_xm(m, par, n, p):
                U = 2 * m + par
                pe.wait_ge(xm_made, U + 1)
                need(pe, h_made, 3 * U)
                pe.transpose(psD[0][:, 0:P], xm[:, par, :], ident[:, :]).then_inc(xm_turned, 1)

            def turn_back(m, par, n, p):
                U = 2 * m + par
                pe.wait_ge(xmT_ready, 3 * U + 3)
                pe.wait_ge(carry_m_saved, U + 1)
                pe.transpose(psD[0][:, P:2 * P], xmT[:, par, :], ident[:, :]).then_inc(xs2_turned, 1)

            def turn_z(m, par, n, p):
                U = 2 * m + par
                pe.wait_ge(z_made, U + 1)
                pe.transpose(psD[0][:, 2 * P:3 * P], z[:, par, :], ident[:, :]).then_inc(z_turned, 1)

            def ffn_up(m, par, n, p):
                U = 2 * m + par
                pe.wait_ge(zT_made, U + 1)
                pe.wait_ge(w1_loaded, 16 * (m // PAIRS + 1))
                need(pe, gelu_made, 3 * U)
                for half in (1, 0):
                    for ch, (lo, w) in enumerate(CH):
                        e = pe.matmul(psD[half][0:w, ch * P:(ch + 1) * P], w1[:, half * FF + lo:half * FF + lo + w], zT[:, par, :],
                                      start=True, stop=True)
                e.then_inc(ff_done, 1)

            def ffn_down(m, par, n, p):
                U = 2 * m + par
                pe.wait_ge(w2_loaded, 32 * (m // PAIRS + 1))
                pe.wait_ge(h_made, 3 * U + 3)
                free_bank(pe, Q_RING, "ffn_down", n, p)
                for ch, (lo, w) in enumerate(CH):
                    e = pe.matmul(BANK["ffn_down"][:, 0:DIM], hT[0:w, par, ch, :], w2[0:w, ch, :], start=(ch == 0), stop=(ch == 2))
                e.then_inc(y2_done, 1)

            def step(n, p):
                on(turn_xm, n, p, 4, n, p)
                on(turn_qk, n, p, 2, n, p, 3)
                on(qk, n, p, 1, n, p, 2)
                on(turn_back, n, p, 4, n, p)
                on(scores, n, p, 2, n, p, 0)
                on(qk, n, p, 1, n, p, 3)
                on(turn_p, n, p, 3, n, p, 2)
                on(scores, n, p, 2, n, p, 1)
                on(turn_z, n, p, 4, n, p)
                on(scores, n, p, 2, n, p, 2)
                on(turn_x, n, p, 0, n, p)
                on(values, n, p, 2, n, p, 1)
                on(turn_qk, n, p, 1, n, p, 0)
                on(scores, n, p, 2, n, p, 3)
                on(ffn_up, n, p, 4, n, p)
                on(turn_p, n, p, 3, n, p, 3)
                on(scores, n, p, 2, n, p, 4)
                on(turn_p, n, p, 3, n, p, 4)
                on(scores, n, p, 2, n, p, 5)
                on(attend, n, p, 3, n, p, 0)
                on(attend, n, p, 3, n, p, 1)
                on(turn_qk, n, p, 1, n, p, 1)
                on(qk, n, p, 0, n, p, 0)
                on(turn_p, n, p, 2, n, p, 0)
                on(qk, n, p, 0, n, p, 1)
                on(turn_o, n, p, 3, n, p, 0)
                on(turn_o, n, p, 3, n, p, 1)
                on(values, n, p, 1, n, p, 0)
                on(turn_p, n, p, 2, n, p, 1)
                on(project, n, p, 3, n, p)
                on(turn_qk, n, p, 1, n, p, 2)
                on(ffn_down, n, p, 4, n, p)

            in_steps(pe, step)


def retention_constants(T=1024, E=128, H=8, V=256, C=128):
    import numpy as np
    f = np.float32
    vec = ((np.arange(0, E, 2, dtype=f) + f(0.4 * E)) / f(1.4 * E)).astype(f)
    pos = np.arange(T, dtype=f)
    scale = (vec[None, :] ** (pos[:, None] / f(512.0))).astype(f)
    inv_freq = (f(1.0) / f(10000.0) ** (np.arange(E // 2, dtype=f) / f(E // 2))).astype(f)
    angle = (pos[:, None] * inv_freq[None, :]).astype(f)
    sin, cos = np.sin(angle).astype(f), np.cos(angle).astype(f)
    gamma = (f(1.0) - np.exp(np.linspace(np.log(1.0 / 32.0), np.log(1.0 / 512.0), H).astype(f))).astype(f)
    log_decay = np.log(gamma).astype(f).astype(np.float64)
    local = np.arange(T) % C
    row = np.sqrt(np.cumsum(np.exp(log_decay[None, :] * np.arange(T)[:, None]), 0))
    head = np.arange(E) // (E // H)
    fq = (np.exp(log_decay[None, :] * local[:, None]) / row * (E // H) ** -0.5)[:, head]
    fk = np.exp(-log_decay[None, :] * local[:, None])[:, head]
    two = lambda a: np.repeat(a.astype(np.float64), 2, axis=-1)
    sign = np.tile([-1.0, 1.0], E // 2)
    cq, sq_ = two(cos * scale) * fq, two(sin * scale) * sign * fq
    ck, sk = two(cos * (f(1.0) / scale)) * fk, two(sin * (f(1.0) / scale)) * sign * fk
    tile = lambda a: np.ascontiguousarray(a.reshape(T // C, C, 2 * E).transpose(1, 0, 2)).astype(f)
    p = np.arange(E)
    over = np.exp(log_decay * C)[head]
    return {"ret_cos": tile(np.concatenate([cq, ck], 1)), "ret_sin": tile(np.concatenate([sq_, sk], 1)),
            "ret_tri": (p[:, None] <= p[None, :]).astype(f), "ret_head_of": (head[:, None] == np.arange(H)[None, :]).astype(f),
            "ret_state_mask": ((head[:, None] == np.arange(V)[None, :] // (V // H)) * over[:, None]).astype(f),
            "ret_decay": over[:, None].astype(f)}


def linear_constants():
    import numpy as np
    f = np.float32
    p, ch = np.arange(128)[:, None, None], np.arange(4)[None, :, None]
    head = 4 * ch + p // 32
    return {"kv_mask": (head == np.arange(128)[None, None, :] // 8).astype(f), "ks_mask": (head == np.arange(16)[None, None, :]).astype(f)}


def local_constants(HD=64, n=1024, W=32, C=128):
    import numpy as np
    f = np.float32
    half = np.arange(0, HD, 2, dtype=f)
    inv_freq = (f(1.0) / f(10000.0) ** (half / f(HD))).astype(f)
    t = np.arange(n, dtype=f)
    freqs = (t[:, None] * inv_freq[None, :]).astype(f)
    freqs = np.concatenate([freqs, freqs], -1)
    base = ((half + f(0.4 * HD)) / f(1.4 * HD)).astype(f)
    power = ((t - n // 2) / f(W // 2)).astype(f)
    scale = (base[None, :] ** power[:, None]).astype(f)
    scale = np.concatenate([scale, scale], -1)
    sign = np.concatenate([-np.ones(HD // 2, f), np.ones(HD // 2, f)])
    inv = (f(1.0) / scale).astype(f)
    cos, sin = np.cos(freqs).astype(f), np.sin(freqs).astype(f)
    rope = np.stack([cos * scale, sin * scale * sign, cos * inv, sin * inv * sign], 1).astype(f)
    i, j = np.arange(C)[:, None], np.arange(C)[None, :]
    own = ((i // W == j // W) & (i >= j)) | ((i // W == j // W + 1) & (i <= j + W))
    prev = (i < W) & (i <= np.arange(W)[None, :])
    mask = np.full((C, 5, C + W + 1), -1e30, f)
    for k in range(5):
        mask[:, k, 0:C][own] = 0.0
        mask[:, k, C + W] = float(k > 0)
        if k:
            mask[:, k, C:C + W][prev] = 0.0
    flag = np.ones((C, 4), f)
    flag[:, 0] = 0.0
    return {"rope_const": rope.reshape(n // C, C, 4, HD).transpose(1, 0, 2, 3), "mask": mask, "flag": flag}


def program(nc, d, out):
    outer = ExitStack()
    with outer:
        def sem(name):
            return outer.enter_context(nc.semaphore(name))

        def keep(name, shape, dt=F32):
            return outer.enter_context(nc.sbuf_tensor(name, shape, dt))

        def part(prefix):
            return {k[len(prefix):]: v for k, v in d.items() if k.startswith(prefix)}

        bank = [outer.enter_context(nc.psum_tensor(f"bank{i}", [P, 512], F32))[:, :] for i in range(8)]
        ident = keep("identity", [P, P])
        ones_row = keep("ones_row", [1, P])
        x = keep("x", [P, TILES, DIM])
        loaded = sem("x_loaded")
        with nc.Block() as block:
            @block.sync
            def _(sp):
                sp.dma_start(ident[:, :], d["identity"]).then_inc(loaded, 16)
                sp.dma_start(x[:, :, :], d["hidden_states"].rearrange("b (t p) d -> p (b t) d", p=P)).then_inc(loaded, 16)
                sp.wait_ge(loaded, 32)

            @block.vector
            def _(dve):
                dve.memset(ones_row[:, :], 1.0)

        def phase(run):
            sems = []

            def signal(name):
                sems.append(nc.alloc_semaphore(name))
                return sems[-1]

            with ExitStack() as stack:
                run(lambda name, shape, dt=F32: stack.enter_context(nc.sbuf_tensor(name, shape, dt)), signal)
            nc.clear_and_free_semaphores(sems)
            nc.all_engine_barrier()

        phase(lambda sb, sem: retention_block(nc, sb, sem, bank, ident, ones_row, x, part("L0_attn_")))
        phase(lambda sb, sem: mixture(nc, sb, sem, bank, ident, ones_row, x, part("L0_ffn_")))
        phase(lambda sb, sem: linear_block(nc, sb, sem, bank, ident, ones_row, x, part("L1_attn_")))
        phase(lambda sb, sem: local_transformer(nc, sb, sem, bank, ident, x, out, part("L1_ffn_")))


_INS = ["L0_attn_w_qkv", "L0_attn_b_qkv", "L0_attn_w_g", "L0_attn_b_g", "L0_attn_w_p", "L0_attn_b_p",
        "L0_ffn_Wr", "L0_ffn_br", "L0_ffn_W1", "L0_ffn_b1", "L0_ffn_W2", "L0_ffn_b2",
        "L1_attn_proj", "L1_attn_w_qkv", "L1_attn_b_out", "L1_attn_gamma", "L1_attn_beta", "L1_attn_b1", "L1_attn_b2",
        "L1_ffn_Wqkv", "L1_ffn_q_scale", "L1_ffn_k_scale", "L1_ffn_Wo", "L1_ffn_ln_g", "L1_ffn_ln_b",
        "L1_ffn_W1", "L1_ffn_b1", "L1_ffn_W2", "L1_ffn_b2"]


def kernel(**inputs):
    import numpy as np
    import concourse.bacc as bacc
    from concourse.bass_utils import run_bass_kernel_spmd as run
    nc = bacc.Bacc("TRN2", target_bir_lowering=False, num_devices=1)
    arrays = {"hidden_states": inputs["L0_attn_hidden_states"], "identity": np.eye(P, dtype=np.float32)}
    for name in _INS:
        arrays[name] = inputs[name]
    w_qkv = inputs["L1_attn_w_qkv"]
    arrays.update(L1_attn_wvT=w_qkv[2 * DIM:].T, L1_attn_w_outT=inputs["L1_attn_w_out"].T,
                  L1_attn_w1T=inputs["L1_attn_w1"].T, L1_attn_w2T=inputs["L1_attn_w2"].T)
    arrays["L0_ffn_rank"] = np.broadcast_to(8.0 - np.arange(8, dtype=np.float32), (P, 4, 8))
    for prefix, consts in (("L0_attn_", retention_constants()), ("L1_attn_", linear_constants()), ("L1_ffn_", local_constants())):
        arrays.update({prefix + k: v for k, v in consts.items()})
    arrays = {"in_" + k: np.ascontiguousarray(v) for k, v in arrays.items()}
    d = {k[3:]: nc.dram_tensor(k, v.shape, F32, kind="ExternalInput").ap() for k, v in arrays.items()}
    out = nc.dram_tensor("out", (4, 1024, 128), F32, kind="ExternalOutput").ap()
    program(nc, d, out)
    return run(nc, [arrays], core_ids=[0]).results[0]["out"]
```
